# Optimizing a Trainium2 kernel written in Bass

```python
import numpy as np
import jax
import jax.numpy as jnp

def _softmax(x, axis=-1):
    return jax.nn.softmax(x, axis=axis)

def _gelu(x):
    return jax.nn.gelu(x, approximate=True)

def _silu(x):
    return jax.nn.silu(x)

def _sigmoid(x):
    return jax.nn.sigmoid(x)

def _layernorm(x, axis=-1, eps=1e-05):
    m = jnp.mean(x, axis=axis, keepdims=True)
    v = jnp.var(x, axis=axis, keepdims=True)
    return (x - m) / jnp.sqrt(v + eps)

def _scatter_add(tgt, idx, src, axis=0):
    return tgt.at[idx].add(src)

def _segment_sum(src, seg, n):
    return jax.ops.segment_sum(src, seg, n)
kernel_name = 'mk_decoder_preln_d1_seqx_r4_3a53ca'

def setup_inputs(seed: int=0):
    np.random.seed(seed)
    _w = jnp.asarray

    def _rec_inputs():
        import jax
        import jax.numpy as jnp
        _rk = jax.random.key(seed)
        x = -0.0002928 + 1 * jax.random.normal(jax.random.fold_in(_rk, 1), (2, 1024, 256), jnp.float32)
        _lenS = 1024 - jax.random.randint(jax.random.fold_in(_rk, 7), (2,), 0, max(1, 1024 // 4) + 1, jnp.int32)
        _lenS2 = 154 - jax.random.randint(jax.random.fold_in(_rk, 8), (2,), 0, max(1, 154 // 4) + 1, jnp.int32)
        _ctx_1024P = jax.random.normal(jax.random.fold_in(_rk, 11), (2, 16, 256), jnp.float32)
        _ctx_1024c = jax.random.dirichlet(jax.random.fold_in(_rk, 511), 0.3 * jnp.ones((16,), jnp.float32), (2, 154))
        _ctx_1024t = jnp.einsum('bsk,bkd->bsd', _ctx_1024c, _ctx_1024P)
        _ctx_1024t = _ctx_1024t * jax.lax.rsqrt(jnp.mean(jnp.square(_ctx_1024t)) + 1e-12) * 0.953939
        ctx_1024 = -1.39393e-06 + 0.999914 * (_ctx_1024t + 0.3 * jax.random.normal(jax.random.fold_in(_rk, 611), (2, 154, 256), jnp.float32))
        _validS = jnp.arange(1024)[None, :] < _lenS[:, None]
        _validS2 = jnp.arange(154)[None, :] < _lenS2[:, None]
        _causal = jnp.tril(jnp.ones((1024, 1024), dtype=bool))
        mask_BxS2_ik1 = jnp.where(jnp.broadcast_to(_validS2[:, :], (2, 154)), 1, 0).astype(jnp.int32)
        mask_1xSxS2_ik1 = jnp.where(jnp.broadcast_to(_validS2[0:1, None, :], (1, 1024, 154)), 1, 0).astype(jnp.int32)
        return (x, ctx_1024, mask_BxS2_ik1, mask_1xSxS2_ik1)
    x, ctx_1024, mask_BxS2_ik1, mask_1xSxS2_ik1 = _rec_inputs()

    def _L0_attn_setup():
        import jax, jax.numpy as jnp
        import numpy as np
        from jax import lax
        D_MODEL = 256
        D_INNER = 512
        D_STATE = 64
        D_CONV = 4
        HEADDIM = 64
        NHEADS = D_INNER // HEADDIM
        CONV_DIM = D_INNER + 2 * D_STATE
        D_IN_PROJ = 2 * D_INNER + 2 * D_STATE + NHEADS
        D_FF = 4 * D_MODEL
        EPS = 1e-05

        def _layernorm(x, w, b):
            mu = jnp.mean(x, -1, keepdims=True)
            var = jnp.mean((x - mu) ** 2, -1, keepdims=True)
            return (x - mu) * lax.rsqrt(var + EPS) * w + b

        def _silu(x):
            return x * jax.nn.sigmoid(x)

        def _mamba2(x, in_proj_w, conv_w, conv_b, dt_bias, A_log, D_param, norm_w, out_proj_w):
            B, L, _ = x.shape
            zxbcdt = jnp.einsum('bld,ed->ble', x, in_proj_w)
            z = zxbcdt[..., :D_INNER]
            xBC = zxbcdt[..., D_INNER:D_INNER + CONV_DIM]
            dt_raw = zxbcdt[..., D_INNER + CONV_DIM:]
            dt = jax.nn.softplus(dt_raw + dt_bias)
            xp = jnp.pad(xBC, ((0, 0), (D_CONV - 1, 0), (0, 0)))
            xBC = sum((conv_w[:, k] * xp[:, k:k + L, :] for k in range(D_CONV))) + conv_b
            xBC = _silu(xBC)
            xs = xBC[..., :D_INNER].reshape(B, L, NHEADS, HEADDIM)
            Bm = xBC[..., D_INNER:D_INNER + D_STATE]
            Cm = xBC[..., D_INNER + D_STATE:]
            A = -jnp.exp(A_log)
            dA = jnp.exp(dt * A)
            dtx = dt[..., None] * xs

            def step(h, inp):
                dA_t, dtx_t, B_t, C_t = inp
                h = dA_t[:, :, None, None] * h + dtx_t[..., None] * B_t[:, None, None, :]
                y_t = jnp.einsum('bhpn,bn->bhp', h, C_t)
                return (h, y_t)
            h0 = jnp.zeros((B, NHEADS, HEADDIM, D_STATE), x.dtype)
            _, ys = lax.scan(step, h0, (jnp.swapaxes(dA, 0, 1), jnp.swapaxes(dtx, 0, 1), jnp.swapaxes(Bm, 0, 1), jnp.swapaxes(Cm, 0, 1)))
            y = jnp.swapaxes(ys, 0, 1) + D_param[None, None, :, None] * xs
            y = y.reshape(B, L, D_INNER)
            y = y * _silu(z)
            y = y * lax.rsqrt(jnp.mean(y * y, -1, keepdims=True) + EPS) * norm_w
            return jnp.einsum('ble,de->bld', y, out_proj_w)

        def _mlp(x, fc_w, fc_b, proj_w, proj_b):
            h = jax.nn.gelu(jnp.einsum('bld,fd->blf', x, fc_w) + fc_b, approximate=False)
            return jnp.einsum('blf,df->bld', h, proj_w) + proj_b
        key = jax.random.key(seed)
        ks = jax.random.split(key, 16)
        B, L = (4, 1024)
        s = 0.02
        inp = {'x': jax.random.normal(ks[0], (B, L, D_MODEL), jnp.float32), 'ln1_w': jnp.ones((D_MODEL,), jnp.float32), 'ln1_b': jnp.zeros((D_MODEL,), jnp.float32), 'ln2_w': jnp.ones((D_MODEL,), jnp.float32), 'ln2_b': jnp.zeros((D_MODEL,), jnp.float32), 'in_proj_w': jax.random.normal(ks[1], (D_IN_PROJ, D_MODEL), jnp.float32) * s, 'conv_w': jax.random.normal(ks[2], (CONV_DIM, D_CONV), jnp.float32) * 0.1, 'conv_b': jnp.zeros((CONV_DIM,), jnp.float32), 'dt_bias': jax.random.normal(ks[3], (NHEADS,), jnp.float32) * 0.1, 'A_log': jnp.log(jax.random.uniform(ks[4], (NHEADS,), jnp.float32, 1.0, 16.0)), 'D_param': jnp.ones((NHEADS,), jnp.float32), 'norm_w': jnp.ones((D_INNER,), jnp.float32), 'out_proj_w': jax.random.normal(ks[5], (D_MODEL, D_INNER), jnp.float32) * s, 'fc_w': jax.random.normal(ks[6], (D_FF, D_MODEL), jnp.float32) * s, 'fc_b': jnp.zeros((D_FF,), jnp.float32), 'proj_w': jax.random.normal(ks[7], (D_MODEL, D_FF), jnp.float32) * s, 'proj_b': jnp.zeros((D_MODEL,), jnp.float32)}
        return inp
    _L0_attn_all = _L0_attn_setup()
    _L0_attn_in = {k: v for k, v in _L0_attn_all.items() if k in ('ln1_w', 'ln1_b', 'ln2_w', 'ln2_b', 'in_proj_w', 'conv_w', 'conv_b', 'dt_bias', 'A_log', 'D_param', 'norm_w', 'out_proj_w', 'fc_w', 'fc_b', 'proj_w', 'proj_b')}
    del _L0_attn_all

    def _L0_xattn_setup():
        import jax, jax.numpy as jnp
        import numpy as np
        D_MODEL = 256
        NUM_HEADS = 16
        D_K = D_MODEL // NUM_HEADS
        B, T = (2, 512)
        key = jax.random.key(seed)
        ks = jax.random.split(key, 12)
        s = 1.0 / np.sqrt(D_MODEL)
        inp = {'query': jax.random.normal(ks[0], (B, T, D_MODEL), jnp.float32), 'key': jax.random.normal(ks[1], (B, T, D_MODEL), jnp.float32), 'value': jax.random.normal(ks[2], (B, T, D_MODEL), jnp.float32), 'Wq': jax.random.normal(ks[3], (D_MODEL, D_MODEL), jnp.float32) * s, 'bq': jnp.zeros((D_MODEL,), jnp.float32), 'Wk': jax.random.normal(ks[4], (D_MODEL, D_MODEL), jnp.float32) * s, 'bk': jnp.zeros((D_MODEL,), jnp.float32), 'Wv': jax.random.normal(ks[5], (D_MODEL, D_MODEL), jnp.float32) * s, 'bv': jnp.zeros((D_MODEL,), jnp.float32), 'Wo': jax.random.normal(ks[6], (D_MODEL, D_MODEL), jnp.float32) * s, 'bo': jnp.zeros((D_MODEL,), jnp.float32), 'key_padding_mask': jax.random.randint(ks[7], (B, T), 0, 2, jnp.int32), 'attention_mask': jnp.triu(jnp.ones((1, T, T), jnp.int32), k=1)}
        return inp
    _L0_xattn_all = _L0_xattn_setup()
    _L0_xattn_in = {k: v for k, v in _L0_xattn_all.items() if k in ('Wq', 'bq', 'Wk', 'bk', 'Wv', 'bv', 'Wo', 'bo')}
    del _L0_xattn_all

    def _L0_ffn_setup():
        import jax, jax.numpy as jnp
        import numpy as np
        D = 256
        H = 1024
        E = 12
        K = 3
        B, S = (1, 512)
        key = jax.random.key(seed)
        ks = jax.random.split(key, 6)
        scale = 0.02
        x = jax.random.normal(ks[0], (B, S, D), dtype=jnp.float32)
        Wg = jax.random.normal(ks[1], (D, E), dtype=jnp.float32) * scale
        Wup = jax.random.normal(ks[2], (E, D, H), dtype=jnp.float32) * scale
        bup = jax.random.normal(ks[3], (E, H), dtype=jnp.float32) * scale
        Wdown = jax.random.normal(ks[4], (E, H, D), dtype=jnp.float32) * scale
        bdown = jax.random.normal(ks[5], (E, D), dtype=jnp.float32) * scale
        return {'x': x, 'Wg': Wg, 'Wup': Wup, 'bup': bup, 'Wdown': Wdown, 'bdown': bdown}
    _L0_ffn_all = _L0_ffn_setup()
    _L0_ffn_in = {k: v for k, v in _L0_ffn_all.items() if k in ('Wg', 'Wup', 'bup', 'Wdown', 'bdown')}
    del _L0_ffn_all
    return {'x': x, 'ctx_1024': ctx_1024, 'mask_BxS2_ik1': mask_BxS2_ik1, 'mask_1xSxS2_ik1': mask_1xSxS2_ik1, 'L0_attn_ln1_w': _L0_attn_in['ln1_w'], 'L0_attn_ln1_b': _L0_attn_in['ln1_b'], 'L0_attn_ln2_w': _L0_attn_in['ln2_w'], 'L0_attn_ln2_b': _L0_attn_in['ln2_b'], 'L0_attn_in_proj_w': _L0_attn_in['in_proj_w'], 'L0_attn_conv_w': _L0_attn_in['conv_w'], 'L0_attn_conv_b': _L0_attn_in['conv_b'], 'L0_attn_dt_bias': _L0_attn_in['dt_bias'], 'L0_attn_A_log': _L0_attn_in['A_log'], 'L0_attn_D_param': _L0_attn_in['D_param'], 'L0_attn_norm_w': _L0_attn_in['norm_w'], 'L0_attn_out_proj_w': _L0_attn_in['out_proj_w'], 'L0_attn_fc_w': _L0_attn_in['fc_w'], 'L0_attn_fc_b': _L0_attn_in['fc_b'], 'L0_attn_proj_w': _L0_attn_in['proj_w'], 'L0_attn_proj_b': _L0_attn_in['proj_b'], 'L0_xattn_Wq': _L0_xattn_in['Wq'], 'L0_xattn_bq': _L0_xattn_in['bq'], 'L0_xattn_Wk': _L0_xattn_in['Wk'], 'L0_xattn_bk': _L0_xattn_in['bk'], 'L0_xattn_Wv': _L0_xattn_in['Wv'], 'L0_xattn_bv': _L0_xattn_in['bv'], 'L0_xattn_Wo': _L0_xattn_in['Wo'], 'L0_xattn_bo': _L0_xattn_in['bo'], 'L0_ffn_Wg': _L0_ffn_in['Wg'], 'L0_ffn_Wup': _L0_ffn_in['Wup'], 'L0_ffn_bup': _L0_ffn_in['bup'], 'L0_ffn_Wdown': _L0_ffn_in['Wdown'], 'L0_ffn_bdown': _L0_ffn_in['bdown']}

def reference(x, ctx_1024, mask_BxS2_ik1, mask_1xSxS2_ik1, L0_attn_ln1_w, L0_attn_ln1_b, L0_attn_ln2_w, L0_attn_ln2_b, L0_attn_in_proj_w, L0_attn_conv_w, L0_attn_conv_b, L0_attn_dt_bias, L0_attn_A_log, L0_attn_D_param, L0_attn_norm_w, L0_attn_out_proj_w, L0_attn_fc_w, L0_attn_fc_b, L0_attn_proj_w, L0_attn_proj_b, L0_xattn_Wq, L0_xattn_bq, L0_xattn_Wk, L0_xattn_bk, L0_xattn_Wv, L0_xattn_bv, L0_xattn_Wo, L0_xattn_bo, L0_ffn_Wg, L0_ffn_Wup, L0_ffn_bup, L0_ffn_Wdown, L0_ffn_bdown):
    import jax
    import jax.numpy as jnp

    def _L0_attn_ref(x, ln1_w, ln1_b, ln2_w, ln2_b, in_proj_w, conv_w, conv_b, dt_bias, A_log, D_param, norm_w, out_proj_w, fc_w, fc_b, proj_w, proj_b):
        import jax, jax.numpy as jnp
        import numpy as np
        from jax import lax
        D_MODEL = 256
        D_INNER = 512
        D_STATE = 64
        D_CONV = 4
        HEADDIM = 64
        NHEADS = D_INNER // HEADDIM
        CONV_DIM = D_INNER + 2 * D_STATE
        D_IN_PROJ = 2 * D_INNER + 2 * D_STATE + NHEADS
        D_FF = 4 * D_MODEL
        EPS = 1e-05

        def _layernorm(x, w, b):
            mu = jnp.mean(x, -1, keepdims=True)
            var = jnp.mean((x - mu) ** 2, -1, keepdims=True)
            return (x - mu) * lax.rsqrt(var + EPS) * w + b

        def _silu(x):
            return x * jax.nn.sigmoid(x)

        def _mamba2(x, in_proj_w, conv_w, conv_b, dt_bias, A_log, D_param, norm_w, out_proj_w):
            B, L, _ = x.shape
            zxbcdt = jnp.einsum('bld,ed->ble', x, in_proj_w)
            z = zxbcdt[..., :D_INNER]
            xBC = zxbcdt[..., D_INNER:D_INNER + CONV_DIM]
            dt_raw = zxbcdt[..., D_INNER + CONV_DIM:]
            dt = jax.nn.softplus(dt_raw + dt_bias)
            xp = jnp.pad(xBC, ((0, 0), (D_CONV - 1, 0), (0, 0)))
            xBC = sum((conv_w[:, k] * xp[:, k:k + L, :] for k in range(D_CONV))) + conv_b
            xBC = _silu(xBC)
            xs = xBC[..., :D_INNER].reshape(B, L, NHEADS, HEADDIM)
            Bm = xBC[..., D_INNER:D_INNER + D_STATE]
            Cm = xBC[..., D_INNER + D_STATE:]
            A = -jnp.exp(A_log)
            dA = jnp.exp(dt * A)
            dtx = dt[..., None] * xs

            def step(h, inp):
                dA_t, dtx_t, B_t, C_t = inp
                h = dA_t[:, :, None, None] * h + dtx_t[..., None] * B_t[:, None, None, :]
                y_t = jnp.einsum('bhpn,bn->bhp', h, C_t)
                return (h, y_t)
            h0 = jnp.zeros((B, NHEADS, HEADDIM, D_STATE), x.dtype)
            _, ys = lax.scan(step, h0, (jnp.swapaxes(dA, 0, 1), jnp.swapaxes(dtx, 0, 1), jnp.swapaxes(Bm, 0, 1), jnp.swapaxes(Cm, 0, 1)))
            y = jnp.swapaxes(ys, 0, 1) + D_param[None, None, :, None] * xs
            y = y.reshape(B, L, D_INNER)
            y = y * _silu(z)
            y = y * lax.rsqrt(jnp.mean(y * y, -1, keepdims=True) + EPS) * norm_w
            return jnp.einsum('ble,de->bld', y, out_proj_w)

        def _mlp(x, fc_w, fc_b, proj_w, proj_b):
            h = jax.nn.gelu(jnp.einsum('bld,fd->blf', x, fc_w) + fc_b, approximate=False)
            return jnp.einsum('blf,df->bld', h, proj_w) + proj_b
        x = x + _mamba2(_layernorm(x, ln1_w, ln1_b), in_proj_w, conv_w, conv_b, dt_bias, A_log, D_param, norm_w, out_proj_w)
        x = x + _mlp(_layernorm(x, ln2_w, ln2_b), fc_w, fc_b, proj_w, proj_b)
        return x

    def _L0_xattn_ref(query, key, value, Wq, bq, Wk, bk, Wv, bv, Wo, bo, key_padding_mask, attention_mask):
        import jax, jax.numpy as jnp
        import numpy as np
        D_MODEL = 256
        NUM_HEADS = 16
        D_K = D_MODEL // NUM_HEADS
        B, T = (2, 512)
        Bz, Tq, D = query.shape

        def proj(x, W, b):
            y = x @ W.T + b
            return y.reshape(Bz, -1, NUM_HEADS, D_K).transpose(0, 2, 1, 3)
        q = proj(query, Wq, bq)
        k = proj(key, Wk, bk)
        v = proj(value, Wv, bv)
        scores = jnp.einsum('bhqd,bhkd->bhqk', q, k) / np.float32(np.sqrt(D_K))
        min_val = jnp.finfo(scores.dtype).min
        scores = jnp.where(key_padding_mask[:, None, None, :] == 1, min_val, scores)
        scores = jnp.where(attention_mask[:, None, :, :] == 1, min_val, scores)
        attn = jax.nn.softmax(scores, axis=-1)
        ctx = jnp.einsum('bhqk,bhkd->bqhd', attn, v)
        ctx = ctx.reshape(Bz, Tq, NUM_HEADS * D_K)
        return ctx @ Wo.T + bo

    def _L0_ffn_ref(x, Wg, Wup, bup, Wdown, bdown):
        import jax, jax.numpy as jnp
        import numpy as np
        D = 256
        H = 1024
        E = 12
        K = 3
        B, S = (1, 512)
        gate_logits = jnp.einsum('bsd,de->bse', x, Wg)
        topw, sel = jax.lax.top_k(gate_logits, K)
        topw = jax.nn.softmax(topw.astype(jnp.float32), axis=-1).astype(x.dtype)
        cw = jnp.einsum('bsk,bske->bse', topw, jax.nn.one_hot(sel, E, dtype=x.dtype))
        h = jax.nn.gelu(jnp.einsum('bsd,edh->ebsh', x, Wup) + bup[:, None, None, :], approximate=False)
        y = jnp.einsum('ebsh,ehd->ebsd', h, Wdown) + bdown[:, None, None, :]
        return jnp.einsum('bse,ebsd->bsd', cw, y)
    x = x + _L0_attn_ref(_layernorm(x, axis=-1), L0_attn_ln1_w, L0_attn_ln1_b, L0_attn_ln2_w, L0_attn_ln2_b, L0_attn_in_proj_w, L0_attn_conv_w, L0_attn_conv_b, L0_attn_dt_bias, L0_attn_A_log, L0_attn_D_param, L0_attn_norm_w, L0_attn_out_proj_w, L0_attn_fc_w, L0_attn_fc_b, L0_attn_proj_w, L0_attn_proj_b)
    x = x + _L0_xattn_ref(_layernorm(x, axis=-1), ctx_1024, ctx_1024, L0_xattn_Wq, L0_xattn_bq, L0_xattn_Wk, L0_xattn_bk, L0_xattn_Wv, L0_xattn_bv, L0_xattn_Wo, L0_xattn_bo, mask_BxS2_ik1, mask_1xSxS2_ik1)
    x = x + _L0_ffn_ref(_layernorm(x, axis=-1), L0_ffn_Wg, L0_ffn_Wup, L0_ffn_bup, L0_ffn_Wdown, L0_ffn_bdown)
    return x

_drawn_inputs = setup_inputs


def setup_inputs(seed=0):
    import zlib

    import numpy as np

    out = dict(_drawn_inputs(seed))
    spreads = {'L0_attn_ln1_w': (1.0, 0.2),
     'L0_attn_ln1_b': (0.0, 0.339),
     'L0_attn_ln2_w': (1.0, 0.6),
     'L0_attn_ln2_b': (0.0, 0.8),
     'L0_attn_conv_b': (0.0, 0.1),
     'L0_attn_D_param': (1.0, 0.2),
     'L0_attn_norm_w': (1.0, 0.2),
     'L0_attn_fc_b': (0.0, 0.441),
     'L0_attn_proj_b': (0.0, 0.1),
     'L0_xattn_bq': (0.0, 0.429),
     'L0_xattn_bk': (0.0, 2.0),
     'L0_xattn_bv': (0.0, 0.1),
     'L0_xattn_bo': (0.0, 0.1)}
    factors = {'L0_attn_dt_bias': 64.0, 'L0_attn_A_log': 64.0, 'L0_ffn_bup': 29.32, 'L0_ffn_bdown': 8.0}
    for name, (base, spread) in spreads.items():
        noise = np.random.default_rng([zlib.crc32(name.encode()), seed]).standard_normal(out[name].shape)
        drawn = base * np.exp(spread * noise) if base else spread * noise
        out[name] = jnp.asarray(drawn.astype(out[name].dtype))
    for name, factor in factors.items():
        out[name] = (out[name] * factor).astype(out[name].dtype)
    return out
```

```python
TW = 128


def build(nc, t):
    import concourse.bass as bass
    from concourse import mybir
    from concourse.alu_op_type import AluOpType as ALU
    from contextlib import ExitStack, contextmanager

    F32, U32, I32 = mybir.dt.float32, mybir.dt.uint32, mybir.dt.int32
    ACT = mybir.ActivationFunctionType
    AX = mybir.AxisListType.X
    ds = bass.ds

    P = 128
    B, L, D = t["x"].shape
    NT = B * L // P
    TG = 4
    NG = NT // TG
    GPB = NG // B
    GW = TG * P
    KB = D // P
    DI = t["out_proj"].shape[0]
    IB = DI // P
    NH = 8
    HD = DI // NH
    NS = 64
    TAPS = 4
    XB = IB + 2
    F = t["fc"].shape[1]
    FB = F // P
    AH, DK = 16, 16
    S2 = t["ctxT"].shape[2]
    KT = S2 // 2
    E, _, H = t["Wup"].shape
    HB = H // P
    NTOK = B * L
    SUB = TW // P
    ROWS = NTOK + TW
    MT = 80
    RW = D + 1 + E
    EPS = 1e-5
    NEG = -3.4028234663852886e38

    with ExitStack() as ctx:
        def sb(name, shape, dt=F32):
            return ctx.enter_context(nc.sbuf_tensor(name, shape, dt))

        def sem(name):
            return ctx.enter_context(nc.semaphore(name))

        ps = ctx.enter_context(nc.psum_tensor("ps", [P, 8, 512], F32))

        X = sb("X", [P, NT, D])
        HR = sb("HR", [P, NT, D])
        consts = sb("consts", [P, 4, P])
        ident, upto, after, ones = (consts[:, i, :] for i in range(4))
        headmask = sb("headmask", [P, 8])
        iota12 = sb("iota12", [P, E])
        tokid = sb("tokid", [P, NT + 1])
        colv = sb("colv", [P, t["cols"].shape[1]])
        rowv = sb("rowv", [P, t["rows"].shape[0]])
        r1 = sb("r1", [P, 4096])
        r2 = sb("r2", [P, 4096])
        EP = t["in_proj"].shape[1]
        win = r1[:, 0:KB * EP].rearrange("p (k e) -> p k e", k=KB)
        wout = r1[:, KB * EP:KB * EP + IB * D].rearrange("p (k d) -> p k d", k=IB)
        wfc = r2[:, 0:2048].rearrange("p (k f) -> p k f", k=KB)
        wproj = r2[:, 2048:4096].rearrange("p (k d) -> p k d", k=FB)
        wup = [r[:, 0:2048].rearrange("p (k f) -> p k f", k=KB) for r in (r1, r2)]
        wdn = [r[:, 2048:4096].rearrange("p (k d) -> p k d", k=HB) for r in (r1, r2)]
        bup = [sb(f"bup{s}", [P, HB]) for s in range(2)]
        wq, wk, wv, wo = (sb(n, [P, KB, D]) for n in ("wq", "wk", "wv", "wo"))
        ctxT = sb("ctxT", [P, KB, B * S2])
        kbd = sb("kbd", [P, KB, B, 8 * S2])
        vone = sb("vone", [P, 2, B, AH, DK + 1])
        qmask_i = sb("qmask_i", [P, L // P, S2], I32)
        qmask = qmask_i[:, :, :].bitcast(F32)
        kmask_i = sb("kmask_i", [P, B, S2], I32)
        kmask = kmask_i[:, :, :].bitcast(F32)
        wg = sb("wg", [P, KB, E])
        bdn = sb("bdn", [E, D])

        CO = {"ln1w": 0, "ln1b": 2, "ln2w": 4, "ln2b": 6, "fcb": 8, "bq": 16, "bk": 18, "normw": 20,
              "convw": 24, "convb": 24 + XB * TAPS}
        RO = {"dtb": 0, "alog": 8, "dpar": 16, "projb": 16 + DI, "bo": 16 + DI + D, "bv": 16 + DI + 2 * D, "tri": 16 + DI + 3 * D,
              "tstart": 16 + DI + 3 * D + E * E}
        slots = nc.dram_tensor("slots", [E * ROWS, RW], F32, kind="Internal").ap()

        def col(name, i):
            return colv[:, CO[name] + i:CO[name] + i + 1]

        st = sb("st", [P, NT, 6])
        mean = sb("mean", [P, NT])
        var = sb("var", [P, NT])
        std = sb("std", [P, NT])
        rstd = sb("rstd", [P, NT])
        la = sb("la", [P, NT])
        lb = sb("lb", [P, NT])
        lc = sb("lc", [P, NT])
        nrm = sb("nrm", [P, TG, D])
        nT = sb("nT", [P, KB, GW])

        reg = sb("reg", [P, XB * (GW + 3) + XB * GW + TG * DI])
        o1 = XB * (GW + 3)
        o2 = o1 + XB * GW
        pre = reg[:, 0:o1].rearrange("p (k n) -> p k n", k=XB)
        xbc = reg[:, o1:o2].rearrange("p (k n) -> p k n", k=XB)
        zs = reg[:, o2:o2 + TG * DI].rearrange("p (k n) -> p k n", k=TG)
        gT = reg[:, 0:FB * GW].rearrange("p (k n) -> p k n", k=FB)

        SCR = 11136
        scr = sb("scr", [P, SCR])
        at = [0]

        def cut(n):
            at[0] += n
            assert at[0] <= SCR, at
            return scr[:, at[0] - n:at[0]]

        xs = [cut(DI) for _ in range(2)]
        xdt = [cut(DI) for _ in range(2)]
        xw = [cut(DI) for _ in range(2)]
        xsD = [cut(DI) for _ in range(2)]
        bst = [cut(NS) for _ in range(2)]
        gm = [cut(P) for _ in range(2)]
        wgt = [cut(NH * P).rearrange("p (h n) -> p h n", h=NH) for _ in range(2)]
        aU = cut(NH * P).rearrange("p (h n) -> p h n", h=NH)
        state = cut(DI)
        sdec = cut(DI)
        y1 = cut(DI)
        ygat = cut(TG * DI).rearrange("p (k n) -> p k n", k=TG)
        at[0] = 0
        qT = cut(KB * GW).rearrange("p (k n) -> p k n", k=KB)
        sc = [cut(4 * S2).rearrange("p (h n) -> p h n", h=4) for _ in range(2)]
        pr = [cut(4 * S2).rearrange("p (h n) -> p h n", h=4) for _ in range(2)]
        pT = [cut(8 * P).rearrange("p (h n) -> p h n", h=8) for _ in range(2)]
        cx = cut(D)
        cxT = cut(KB * P).rearrange("p (k n) -> p k n", k=KB)
        yT = sb("yT", [P, IB, P])
        sq = sb("sq", [P, DI])
        mk = sb("mk", [P, S2])
        kTs = sb("kTs", [P, B * S2])
        small = {n: sb("s_" + n, [P, TG, NH]) for n in
                 ("raw", "abs", "e", "w", "lw", "wm", "eq", "den", "q", "dt", "a")}
        aneg = sb("aneg", [P, NH])
        cexp = sb("cexp", [P, 3, TG, NH])
        ss = sb("ss", [P, TG])
        sv = sb("sv", [P, TG])
        sstd = sb("sstd", [P, TG])
        srs = sb("srs", [P, TG])
        smx = [sb(f"smx{i}", [P, 4]) for i in range(2)]
        rsum = sb("rsum", [P, AH])
        at[0] = 0
        rowx = cut(TG * RW).rearrange("p (j n) -> p j n", j=TG)
        padrow = cut(RW)
        lg = cut(TG * E).rearrange("p (j n) -> p j n", j=TG)
        top = cut(TG * 8).rearrange("p (j n) -> p j n", j=TG)
        tix = cut(TG * 8).rearrange("p (j n) -> p j n", j=TG).bitcast(U32)
        tixf = cut(TG * 8).rearrange("p (j n) -> p j n", j=TG)
        tsh = cut(TG * 3).rearrange("p (j n) -> p j n", j=TG)
        tex = cut(TG * 3).rearrange("p (j n) -> p j n", j=TG)
        tsum = cut(TG)
        trs = cut(TG)
        tw = cut(TG * 3).rearrange("p (j n) -> p j n", j=TG)
        oh = cut(TG * 3 * E).rearrange("p (j k n) -> p j k n", j=TG, k=3)
        pick = cut(TG * 3 * E).rearrange("p (j k n) -> p j k n", j=TG, k=3)
        sel = cut(TG * E).rearrange("p (j n) -> p j n", j=TG)
        pos = cut(TG * E).rearrange("p (j n) -> p j n", j=TG)
        posf = cut(TG * 3).rearrange("p (j n) -> p j n", j=TG)
        posk = cut(TG * 3).bitcast(U32)
        run = cut(E)
        cnt = cut(E)
        cwork = cut(E * max(E, NTOK // TW))
        tabf = cut(3 * E + 1)
        tab = cut(3 * E + 1).bitcast(I32)
        tilef = cut(MT)
        tiletab = cut(MT).bitcast(I32)
        tstep = cut(E)
        tcmp = cut(MT * E).rearrange("p (k e) -> p k e", k=MT)
        tk = cut(MT)
        xt = cut(SUB * RW).rearrange("p (j n) -> p j n", j=SUB)
        xT = cut(KB * TW).rearrange("p (k n) -> p k n", k=KB)
        meta = cut(SUB * (1 + E)).rearrange("p (j n) -> p j n", j=SUB)
        ysc = cut(SUB * D).rearrange("p (j n) -> p j n", j=SUB)
        ytok = cut(SUB).bitcast(U32)
        eT = gT[:, :, 0:TW]
        cwT = reg[0:E, 0:TG * P].rearrange("p (j n) -> p j n", j=TG)

        x_in, prm_in, mlp_in, att_in = (sem(n) for n in ("x_in", "prm_in", "mlp_in", "att_in"))
        exp_in = [sem(f"exp_in{s}") for s in range(2)]
        acc_in, rows_out, pad_out, xt_in, acc_out = (sem(n) for n in ("acc_in", "rows_out", "pad_out", "xt_in", "acc_out"))
        dve_step = sem("dve_step")
        dve_pad, pool_pad, act_pad, pe_pad, sp_pad = (sem(n) for n in ("dve_pad", "pool_pad", "act_pad", "pe_pad", "sp_pad"))
        dve_names = ("ln_var n_ready nT_ready dt_abs dt_w a_ready conv_done xdt_ready gm_ready w_ready y1_ready "
                     "state_ready yg_ready rms_var h_done wout_ready "
                     "b_var b_n b_nT b_res "
                     "kv_ready c_var c_n c_nT c_q c_sc cx_ready c_out c_max "
                     "d_var d_n d_nT d_lg d_shift sel_ready pos_ready cw_ready cwT_ready d_bias tab_ready xT_ready meta_ready y_ready aneg_in").split()
        pe_names = ("nT_ps dt_ps x_ps z_ps c_ps xT_ps bg_ps seg_ps off_ps st_ps y_ps yT_ps op_ps "
                    "b_nT_ps b_up_ps b_dn_ps k_ps v_ps c_nT_ps q_ps sc_ps pT_ps val_ps ctx_ps cxT_ps co_ps "
                    "d_nT_ps lg_ps pos_ps cwT_ps db_ps t_ps u_ps dn_ps").split()
        act_names = ("ln_std dt_e dt_lw x_ev x_act z_act c_exp xs_ready e_ready ss_ready rms_std yT_ready "
                     "b_std b_gel c_std p_ready pT_ready cxT_ready d_std d_exp d_gel aneg_exp").split()
        pool_names = "aU_ready xsD_ready xw_ready sdec_ready y1d_ready b_x c_sub rows_gone y_gone".split()
        S = {n: sem(n) for n in dve_names + pe_names + act_names + pool_names}

        def bank(i, n=512):
            return ps[:, i, 0:n]

        def heads(ap):
            return ap.rearrange("p (h n) -> p h n", h=NH)

        def over(ap, n):
            return ap.unsqueeze(2).to_broadcast([ap.shape[0], ap.shape[1], n])

        @contextmanager
        def batch_groups(eng):
            with eng.Fori(0, B) as b:
                with eng.Fori(0, GPB) as gi:
                    yield b, gi, eng.snap(b * GPB + gi)

        def load_expert(eng, e, s):
            for dst, src in ((wup[s], t["Wup"].rearrange("e (k p) f -> e p k f", p=P)),
                             (wdn[s], t["Wdown"].rearrange("e (k p) d -> e p k d", p=P)),
                             (bup[s][:, :], t["bup"])):
                eng.dma_start(dst, src[ds(e, 1)].squeeze(0)).then_inc(exp_in[s], 16)

        block = ctx.enter_context(nc.Block())

        @block.sync
        def _(sp):
            xv = t["x"].rearrange("b (t p) d -> p (b t) d", p=P)
            sp.dma_start(X[:, :, :], xv).then_inc(x_in, 16)
            prm = [(consts[:, :, :], t["consts"].rearrange("c p n -> p c n")),
                   (headmask[:, :], t["headmask"]), (iota12[:, :], t["iota12"]), (tokid[:, :], t["tokid"]),
                   (colv[:, :], t["cols"]), (rowv[:, :], t["rows"].partition_broadcast(P)),
                   (win, t["in_proj"].rearrange("(k p) e -> p k e", p=P)),
                   (wout, t["out_proj"].rearrange("(k p) d -> p k d", p=P))]
            for dst, src in prm:
                sp.dma_start(dst, src).then_inc(prm_in, 16)
            assert len(prm) == 8
            sp.dma_start(wfc, t["fc"].rearrange("(k p) f -> p k f", p=P)).then_inc(mlp_in, 16)
            sp.dma_start(wproj, t["proj"].rearrange("(k p) d -> p k d", p=P)).then_inc(mlp_in, 16)
            att = [(w[:, :, :], t[n].rearrange("(k p) d -> p k d", p=P)) for w, n in
                   ((wq, "Wq"), (wk, "Wk"), (wv, "Wv"), (wo, "Wo"), (wg, "Wg"))]
            att += [(ctxT[:, :, :], t["ctxT"].rearrange("(k p) b s -> p k (b s)", p=P)),
                    (qmask_i[:, :, :], t["qmask"].rearrange("o (t p) s -> p (o t) s", p=P)),
                    (kmask_i[:, :, :], t["kmask"].partition_broadcast(P)),
                    (bdn[:, :], t["bdown"])]
            for dst, src in att:
                sp.dma_start(dst, src).then_inc(att_in, 16)
            assert len(att) == 9
            sp.wait_ge(S["h_done"], NT + 1)
            sp.wait_ge(S["b_dn_ps"], NT + 1)
            load_expert(sp, 0, 0)
            acc = t["out"].rearrange("(t p) d -> p t d", p=P)
            with sp.Fori(0, NG) as g:
                sp.wait_ge(S["d_bias"], TG * g + TG + 1)
                sp.dma_start(acc[:, ds(TG * g, TG), :], X[:, ds(TG * g, TG), :]).then_inc(acc_in, 16)
            sp.wait_ge(S["tab_ready"], 1 + 1)
            sp.dma_start(t["out"][NTOK:NTOK + P, :], padrow[:, 0:D]).then_inc(acc_in, 16)
            with sp.Fori(0, E) as e:
                used = sp.value_load(tab[0:1, ds(2 * E + 1 + e, 1)], min_val=0, max_val=NTOK)
                for r in range(SUB):
                    sp.dma_start(slots[ds(e * ROWS + used + r * P, P), :], padrow).then_inc(pad_out, 16)
            sp.wait_ge(rows_out, NT * 3 * 16)
            sp.wait_ge(pad_out, E * SUB * 16)

            def read_tile(k):
                at_row = sp.value_load(tiletab[0:1, ds(k, 1)], min_val=0, max_val=E * ROWS - TW)
                sp.wait_ge(S["t_ps"], k + 1)
                sp.wait_ge(S["meta_ready"], k + 1)
                sp.sem_inc(sp_pad, 1)
                sp.dma_start(xt, slots[ds(at_row, TW), :].rearrange("(r p) n -> p r n", p=P)).then_inc(xt_in, 16)

            def feed(e, s, another):
                first = sp.value_load(tab[0:1, ds(E + e, 1)], min_val=0, max_val=60)
                tiles = sp.value_load(tab[0:1, ds(e, 1)], min_val=1, max_val=NTOK // TW)
                read_tile(first + 1)
                if another:
                    sp.wait_ge(S["dn_ps"], first * SUB + 1)
                    sp.sem_inc(sp_pad, 1)
                    load_expert(sp, e + 1, 1 - s)
                with sp.Fori(1, tiles) as j:
                    read_tile(sp.snap(first + j) + 1)

            read_tile(0)
            with sp.Fori(0, E // 2 - 1) as ep:
                for s in range(2):
                    feed(sp.snap(2 * ep + s), s, True)
            for s in range(2):
                feed(E - 2 + s, s, s == 0)

        @block.vector
        def _(dve):
            n = [0]

            def c(ins):
                n[0] += 1
                ins.then_inc(dve_step, 1)

            def f():
                dve.wait_ge(dve_step, n[0])

            def restart():
                if n[0]:
                    f()
                dve.sem_clear(dve_step)
                n[0] = 0

            TT, TS, STT = dve.tensor_tensor, dve.tensor_scalar, dve.scalar_tensor_tensor

            def moments(a, m):
                s = slice(a, a + m)
                c(TT(la[:, s], st[:, s, 1], st[:, s, 4], ALU.add))
                c(TT(lb[:, s], st[:, s, 1], st[:, s, 4], ALU.subtract))
                c(TT(lc[:, s], st[:, s, 2], st[:, s, 5], ALU.add))
                f()
                c(TS(mean[:, s], la[:, s], 0.5, None, ALU.mult))
                c(STT(var[:, s], lb[:, s], 0.25, lb[:, s], ALU.mult, ALU.mult))
                c(TS(lc[:, s], lc[:, s], 1.0 / D, EPS, ALU.mult, ALU.add))
                f()
                return TT(var[:, s], lc[:, s], var[:, s], ALU.add)

            for name in dve_names:
                dve.sem_inc(S[name], 1)
            dve.wait_ge(x_in, 16)
            restart()
            with dve.Fori(0, NT) as i:
                dve.bn_stats(st[:, ds(i, 1), :].squeeze(1), X[:, ds(i, 1), :].squeeze(1)).then_inc(dve_step, 1)
            n[0] = NT
            f()
            moments(0, NT).then_inc(S["ln_var"], 1)
            dve.wait_ge(S["ln_std"], 1 + 1)
            c(dve.reciprocal(rstd[:, :], std[:, :]))
            restart()
            with dve.Fori(0, NT) as i:
                dve.sem_clear(dve_step)
                TS(HR[:, ds(i, 1), :].squeeze(1), X[:, ds(i, 1), :].squeeze(1), mean[:, ds(i, 1)], rstd[:, ds(i, 1)],
                   ALU.subtract, ALU.mult).then_inc(dve_step, 1)
                dve.wait_ge(dve_step, 1)
                dve.bn_stats(st[:, ds(i, 1), :].squeeze(1), HR[:, ds(i, 1), :].squeeze(1)).then_inc(dve_step, 1)
                dve.wait_ge(dve_step, 2)
            n[0] = 2
            restart()
            moments(0, NT).then_inc(S["ln_var"], 1)
            dve.wait_ge(prm_in, 8 * 16)
            TS(aneg[:, :], rowv[:, RO["alog"]:RO["alog"] + NH], 80.0, None, ALU.min).then_inc(S["aneg_in"], 1)
            dve.wait_ge(S["aneg_exp"], 1 + 1)
            c(TS(aneg[:, :], aneg[:, :], -1.0, None, ALU.mult))
            for k in range(IB):
                ins = TS(wout[:, k, :], wout[:, k, :], col("normw", k), None, ALU.mult)
                c(ins) if k < IB - 1 else ins.then_inc(S["wout_ready"], 1)
            dve.wait_ge(S["ln_std"], 2 + 1)
            c(dve.reciprocal(rstd[:, :], std[:, :]))
            restart()

            sm = {k: v[:, :, :] for k, v in small.items()}
            with dve.Fori(0, B) as b:
                dve.memset(state[0:NS, :], 0.0).then_inc(S["state_ready"], 1)
                dve.memset(pre[:, :, 0:TAPS - 1], 0.0).then_inc(dve_step, 1)
                dve.wait_ge(dve_step, 1)
                dve.sem_clear(dve_step)
                with dve.Fori(0, GPB) as gi:
                    g = dve.snap(b * GPB + gi)
                    dve.wait_ge(S["nT_ps"], KB * g + 1)
                    for j in range(TG):
                        i = TG * g + j
                        ins = TS(nrm[:, j, :], HR[:, ds(i, 1), :].squeeze(1), mean[:, ds(i, 1)], rstd[:, ds(i, 1)],
                                 ALU.subtract, ALU.mult)
                        c(ins) if j < TG - 1 else ins.then_inc(S["n_ready"], 1)
                    for k in range(KB):
                        dve.wait_ge(S["nT_ps"], KB * g + k + 1 + 1)
                        TS(nT[:, k, :], bank(k), col("ln1w", k), col("ln1b", k), ALU.mult, ALU.add).then_inc(S["nT_ready"], 1)
                    dve.wait_ge(S["dt_ps"], g + 1 + 1)
                    c(TT(sm["raw"], bank(7, TG * NH).rearrange("p (j h) -> p j h", j=TG),
                         rowv[:, RO["dtb"]:RO["dtb"] + NH].unsqueeze(1).to_broadcast([P, TG, NH]), ALU.add))
                    f()
                    STT(sm["abs"], sm["raw"], -1.0, sm["raw"], ALU.mult, ALU.max).then_inc(S["dt_abs"], 1)
                    dve.wait_ge(S["dt_e"], g + 1 + 1)
                    TS(sm["w"], sm["e"], 1.0, None, ALU.add).then_inc(S["dt_w"], 1)
                    dve.wait_ge(S["dt_w"], g + 1 + 1)
                    c(TS(sm["wm"], sm["w"], -1.0, None, ALU.add))
                    f()
                    c(TS(sm["eq"], sm["wm"], 0.0, None, ALU.is_equal))
                    f()
                    c(TT(sm["den"], sm["wm"], sm["eq"], ALU.add))
                    f()
                    c(dve.reciprocal(sm["q"], sm["den"]))
                    f()
                    c(TT(sm["q"], sm["q"], sm["e"], ALU.mult))
                    c(TT(sm["eq"], sm["eq"], sm["e"], ALU.mult))
                    f()
                    dve.wait_ge(S["dt_lw"], g + 1 + 1)
                    c(TT(sm["q"], sm["q"], sm["lw"], ALU.mult))
                    f()
                    c(TT(sm["q"], sm["q"], sm["eq"], ALU.add))
                    f()
                    c(STT(sm["dt"], sm["raw"], 0.0, sm["q"], ALU.max, ALU.add))
                    f()
                    c(TT(sm["a"], sm["dt"], aneg[:, :].unsqueeze(1).to_broadcast([P, TG, NH]), ALU.mult))
                    f()
                    TS(sm["a"], sm["a"], -104.0, None, ALU.max).then_inc(S["a_ready"], 1)
                    for k in range(XB):
                        pp = P if k < IB else NS
                        dve.wait_ge(S["x_ev"], XB * g + k + 1 + 1)
                        for w in range(TAPS):
                            wc = colv[0:pp, CO["convw"] + k * TAPS + w:CO["convw"] + k * TAPS + w + 1]
                            src = pre[0:pp, k, w:w + GW]
                            if w == 0:
                                c(TS(xbc[0:pp, k, :], src, wc, None, ALU.mult))
                            else:
                                f()
                                ins = STT(xbc[0:pp, k, :], src, wc, xbc[0:pp, k, :], ALU.mult, ALU.add)
                                c(ins) if w < TAPS - 1 else ins.then_inc(S["conv_done"], 1)
                    dve.wait_ge(S["conv_done"], XB * g + XB + 1)
                    c(dve.tensor_copy(pre[:, 0:IB, 0:TAPS - 1], pre[:, 0:IB, GW:GW + TAPS - 1]))
                    c(dve.tensor_copy(pre[0:NS, IB:XB, 0:TAPS - 1], pre[0:NS, IB:XB, GW:GW + TAPS - 1]))

                    def before(j):
                        s = j % 2
                        i = TG * g + j
                        dve.wait_ge(S["xs_ready"], i + 1 + 1)
                        TT(heads(xdt[s]), heads(xs[s]), over(small["dt"][:, j, :], HD), ALU.mult).then_inc(S["xdt_ready"], 1)
                        dve.wait_ge(S["bg_ps"], i + 1 + 1)
                        c(dve.tensor_copy(bst[s], ps[:, 5, 0:NS]))
                        TT(gm[s], ps[:, 5, P:2 * P], upto, ALU.mult).then_inc(S["gm_ready"], 1)

                    def main(j):
                        s = j % 2
                        i = TG * g + j
                        dve.wait_ge(S["gm_ready"], i + 1 + 1)
                        dve.wait_ge(S["e_ready"], i + 1 + 1)
                        TT(wgt[s], wgt[s], gm[s].unsqueeze(1).to_broadcast([P, NH, P]), ALU.mult).then_inc(S["w_ready"], 1)
                        dve.wait_ge(S["off_ps"], i + 1 + 1)
                        dve.wait_ge(S["yg_ready"], i + 1)
                        TT(heads(y1), heads(bank(7)), over(cexp[:, 0, j, :], HD), ALU.mult).then_inc(S["y1_ready"], 1)
                        dve.wait_ge(S["sdec_ready"], i + 1 + 1)
                        dve.wait_ge(S["st_ps"], i + 1 + 1)
                        TT(state[0:NS, :], sdec[0:NS, :], ps[0:NS, 0, :], ALU.add).then_inc(S["state_ready"], 1)
                        dve.wait_ge(S["y_ps"], i + 1 + 1)
                        dve.wait_ge(S["y1d_ready"], i + 1 + 1)
                        c(TT(y1, bank(6), y1, ALU.add))
                        f()
                        TT(ygat[:, j, :], y1, zs[:, j, :], ALU.mult).then_inc(S["yg_ready"], 1)

                    dve.wait_ge(S["c_exp"], g + 1 + 1)
                    dve.wait_ge(S["z_act"], TG * g + TG + 1)
                    before(0)
                    for j in range(TG):
                        if j + 1 < TG:
                            before(j + 1)
                        main(j)
                    dve.wait_ge(S["ss_ready"], TG * g + TG + 1)
                    TS(sv[:, :], ss[:, :], 1.0 / DI, EPS, ALU.mult, ALU.add).then_inc(S["rms_var"], 1)
                    dve.wait_ge(S["rms_std"], g + 1 + 1)
                    c(dve.reciprocal(srs[:, :], sstd[:, :]))
                    f()
                    for j in range(TG):
                        i = TG * g + j
                        dve.wait_ge(S["op_ps"], i + 1 + 1)
                        hr = HR[:, ds(i, 1), :].squeeze(1)
                        STT(hr, ps[:, 6 * (j % 2), 0:D], srs[:, j:j + 1], hr, ALU.mult, ALU.add).then_inc(S["h_done"], 1)
                    restart()

            dve.wait_ge(S["h_done"], NT + 1)
            with dve.Fori(0, NG) as g:
                for j in range(TG):
                    i = TG * g + j
                    c(dve.bn_stats(st[:, j, :], HR[:, ds(i, 1), :].squeeze(1)))
                f()
                moments(0, TG).then_inc(S["b_var"], 1)
                dve.wait_ge(S["b_std"], g + 1 + 1)
                c(dve.reciprocal(rstd[:, 0:TG], std[:, 0:TG]))
                f()
                dve.wait_ge(S["b_nT_ps"], KB * g + 1)
                for j in range(TG):
                    i = TG * g + j
                    ins = TS(nrm[:, j, :], HR[:, ds(i, 1), :].squeeze(1), mean[:, j:j + 1], rstd[:, j:j + 1],
                             ALU.subtract, ALU.mult)
                    c(ins) if j < TG - 1 else ins.then_inc(S["b_n"], 1)
                for k in range(KB):
                    dve.wait_ge(S["b_nT_ps"], KB * g + k + 1 + 1)
                    TS(nT[:, k, :], bank(k), col("ln2w", k), col("ln2b", k), ALU.mult, ALU.add).then_inc(S["b_nT"], 1)
                for j in range(TG):
                    i = TG * g + j
                    hr = HR[:, ds(i, 1), :].squeeze(1)
                    dve.wait_ge(S["b_dn_ps"], i + 1 + 1)
                    c(TT(hr, hr, ps[:, 6 + j % 2, 0:D], ALU.add))
                    f()
                    TT(hr, hr, rowv[:, RO["projb"]:RO["projb"] + D], ALU.add).then_inc(S["b_res"], 1)
                restart()

            dve.wait_ge(att_in, 9 * 16)
            for k in range(KB):
                dve.wait_ge(S["k_ps"], k + 1 + 1)
                c(TS(kTs[:, :], ps[:, k, 0:B * S2], col("bk", k), None, ALU.add))
                f()
                for b in range(B):
                    c(TT(kbd[:, k, b, :].rearrange("p (h s) -> p h s", h=8),
                         kTs[:, b * S2:(b + 1) * S2].unsqueeze(1).to_broadcast([P, 8, S2]),
                         over(headmask[:, :], S2), ALU.mult))
                f()
            c(dve.memset(vone[:, :, :, :, DK:DK + 1], 1.0))
            for kt in range(2):
                for b in range(B):
                    u = kt * B + b
                    dve.wait_ge(S["v_ps"], u + 1 + 1)
                    c(TT(vone[0:KT, kt, b, :, 0:DK], ps[0:KT, 2 + u, 0:D].rearrange("p (h n) -> p h n", h=AH),
                         rowv[0:KT, RO["bv"]:RO["bv"] + D].rearrange("p (h n) -> p h n", h=AH), ALU.add))
            c(TS(qmask, qmask_i[:, :, :], 1, NEG, ALU.is_equal, ALU.mult))
            TS(kmask, kmask_i[:, :, :], 1, NEG, ALU.is_equal, ALU.mult).then_inc(S["kv_ready"], 1)
            restart()

            with dve.Fori(0, NG) as g:
                dve.wait_ge(S["b_x"], TG * g + TG + 1)
                dve.sem_inc(dve_pad, 1)
                for j in range(TG):
                    c(dve.bn_stats(st[:, ds(TG * g + j, 1), :].squeeze(1), X[:, ds(TG * g + j, 1), :].squeeze(1)))
                restart()
            moments(0, NT).then_inc(S["c_var"], 1)
            dve.wait_ge(S["c_std"], 1 + 1)
            c(dve.reciprocal(rstd[:, :], std[:, :]))
            f()

            def att_norm(g, j):
                i = TG * g + j
                dve.wait_ge(S["c_nT_ps"], KB * g + 1)
                ins = TS(nrm[:, j, :], X[:, ds(i, 1), :].squeeze(1), mean[:, ds(i, 1)], rstd[:, ds(i, 1)],
                         ALU.subtract, ALU.mult)
                c(ins) if j < TG - 1 else ins.then_inc(S["c_n"], 1)

            def att_turned(g, k):
                dve.wait_ge(S["c_nT_ps"], KB * g + k + 1 + 1)
                dve.tensor_copy(nT[:, k, :], bank(0)).then_inc(S["c_nT"], 1)

            def att_query(g):
                for k in range(KB):
                    dve.wait_ge(S["q_ps"], KB * g + k + 1 + 1)
                    TS(qT[:, k, :], bank(2 + k), col("bq", k), 1.0 / DK ** 0.5, ALU.add, ALU.mult).then_inc(S["c_q"], 1)

            def att_scores(g, u):
                s = u % 2
                if u % 4 == 0:
                    c(TT(mk[:, :], qmask[:, ds((g % GPB) * TG + u // 4, 1), :].squeeze(1),
                         kmask[:, ds(g // GPB, 1), :].squeeze(1), ALU.min))
                    f()
                dve.wait_ge(S["sc_ps"], 16 * g + u + 1 + 1)
                if not (first_group(g) and u < 2):
                    dve.wait_ge(S["p_ready"], 16 * g + u - 1 + 1)
                TT(sc[s].rearrange("p (c h) n -> p c h n", c=2),
                   ps[:, 2 + 2 * s:4 + 2 * s, 0:2 * S2].rearrange("p c (h n) -> p c h n", h=2),
                   mk[:, :].unsqueeze(1).unsqueeze(1).to_broadcast([P, 2, 2, S2]), ALU.add).then_inc(S["c_sc"], 1)
                dve.wait_ge(S["c_sc"], 16 * g + u + 1 + 1)
                dve.sem_inc(dve_pad, 1)
                dve.tensor_reduce(smx[s][:, :], sc[s], AX, ALU.max).then_inc(S["c_max"], 1)

            def first_group(g):
                return isinstance(g, int) and g == 0

            def att_normalise(g, j):
                dve.wait_ge(S["ctx_ps"], TG * g + j + 1 + 1)
                dve.sem_inc(dve_pad, 1)
                acc = ps[:, 1, 0:AH * (DK + 1)].rearrange("p (h n) -> p h n", h=AH)
                c(dve.reciprocal(rsum[:, :], acc[:, :, DK]))
                f()
                TT(cx.rearrange("p (h n) -> p h n", h=AH), acc[:, :, 0:DK], over(rsum[:, :], DK), ALU.mult).then_inc(S["cx_ready"], 1)

            def att_output(g, j):
                i = TG * g + j
                xr = X[:, ds(i, 1), :].squeeze(1)
                dve.wait_ge(S["co_ps"], i + 1 + 1)
                c(TT(xr, xr, ps[:, 0, D:2 * D], ALU.add))
                f()
                TT(xr, xr, rowv[:, RO["bo"]:RO["bo"] + D], ALU.add).then_inc(S["c_out"], 1)

            def att_group(g, following):
                for u in range(16):
                    if u % 4 == 1 and u > 4:
                        att_normalise(g, u // 4 - 1)
                    if following is not None:
                        if u < 2:
                            att_norm(following, 2 * u)
                            att_norm(following, 2 * u + 1)
                        if u == 4:
                            att_turned(following, 0)
                        if u == 9:
                            att_turned(following, 1)
                        if u == 14:
                            att_query(following)
                    if u % 4 == 3 and u > 4:
                        att_output(g, u // 4 - 1)
                    if u < 14:
                        att_scores(g, u + 2)
                if following is not None:
                    att_scores(following, 0)
                att_normalise(g, TG - 1)
                if following is not None:
                    att_scores(following, 1)
                att_output(g, TG - 1)
                dve.wait_ge(S["c_out"], TG * g + TG + 1)
                dve.sem_inc(dve_pad, 1)
                restart()

            for j in range(TG):
                att_norm(0, j)
            for k in range(KB):
                att_turned(0, k)
            att_query(0)
            for u in range(2):
                att_scores(0, u)
            restart()
            with dve.Fori(0, NG - 1) as g:
                att_group(g, dve.snap(g + 1))
            att_group(NG - 1, None)

            c(dve.memset(padrow, 0.0))
            f()
            c(dve.tensor_copy(padrow[:, D:D + 1], tokid[:, NT:NT + 1]))
            c(dve.tensor_copy(run, rowv[:, RO["tstart"]:RO["tstart"] + E]))
            restart()
            with dve.Fori(0, NG) as g:
                for j in range(TG):
                    i = TG * g + j
                    c(dve.bn_stats(st[:, j, :], X[:, ds(i, 1), :].squeeze(1)))
                f()
                moments(0, TG).then_inc(S["d_var"], 1)
                dve.wait_ge(S["d_std"], g + 1 + 1)
                c(dve.reciprocal(rstd[:, 0:TG], std[:, 0:TG]))
                f()
                dve.wait_ge(S["rows_gone"], g + 1)
                dve.sem_inc(dve_pad, 1)
                c(dve.tensor_copy(rowx[:, :, D], tokid[:, ds(TG * g, TG)]))
                for j in range(TG):
                    i = TG * g + j
                    ins = TS(rowx[:, j, 0:D], X[:, ds(i, 1), :].squeeze(1), mean[:, j:j + 1], rstd[:, j:j + 1],
                             ALU.subtract, ALU.mult)
                    c(ins) if j < TG - 1 else ins.then_inc(S["d_n"], 1)
                for k in range(KB):
                    dve.wait_ge(S["d_nT_ps"], KB * g + k + 1 + 1)
                    dve.tensor_copy(nT[:, k, :], bank(k)).then_inc(S["d_nT"], 1)
                dve.wait_ge(S["lg_ps"], g + 1 + 1)
                dve.tensor_copy(lg, ps[:, 2, 0:TG * E].rearrange("p (j e) -> p j e", j=TG)).then_inc(S["d_lg"], 1)
                dve.wait_ge(S["d_lg"], g + 1 + 1)
                dve.sem_inc(dve_pad, 1)
                for j in range(TG):
                    c(dve.max(top[:, j, :], lg[:, j, :]))
                f()
                for j in range(TG):
                    c(dve.max_index(tix[:, j, :], top[:, j, :], lg[:, j, :]))
                TT(tsh, top[:, :, 0:3], top[:, :, 0:1].to_broadcast([P, TG, 3]), ALU.subtract).then_inc(S["d_shift"], 1)
                f()
                c(dve.tensor_copy(tixf, tix))
                f()
                c(TT(oh, iota12[:, :].unsqueeze(1).unsqueeze(1).to_broadcast([P, TG, 3, E]),
                     tixf[:, :, 0:3].unsqueeze(3).to_broadcast([P, TG, 3, E]), ALU.is_equal))
                f()
                c(TT(sel, oh[:, :, 0, :], oh[:, :, 1, :], ALU.add))
                f()
                TT(sel, sel, oh[:, :, 2, :], ALU.add).then_inc(S["sel_ready"], 1)
                dve.wait_ge(S["d_exp"], g + 1 + 1)
                c(dve.tensor_reduce(tsum, tex, AX, ALU.add))
                f()
                c(dve.reciprocal(trs, tsum))
                f()
                c(TT(tw, tex, over(trs, 3), ALU.mult))
                f()
                c(TT(pick, oh, tw.unsqueeze(3).to_broadcast([P, TG, 3, E]), ALU.mult))
                f()
                c(TT(pick[:, :, 0, :], pick[:, :, 0, :], pick[:, :, 1, :], ALU.add))
                f()
                TT(rowx[:, :, D + 1:RW], pick[:, :, 0, :], pick[:, :, 2, :], ALU.add).then_inc(S["cw_ready"], 1)
                dve.wait_ge(S["pos_ps"], g + 1 + 1)
                c(TT(pos, ps[:, 3, 0:TG * E].rearrange("p (j e) -> p j e", j=TG),
                     run.unsqueeze(1).to_broadcast([P, TG, E]), ALU.add))
                f()
                c(TT(run, run, ps[:, 3, TG * E:(TG + 1) * E], ALU.add))
                c(TT(pick, oh, pos.unsqueeze(2).to_broadcast([P, TG, 3, E]), ALU.mult))
                f()
                c(dve.tensor_reduce(posf, pick, AX, ALU.add))
                f()
                dve.tensor_copy(posk, posf.rearrange("p j k -> p (j k)")).then_inc(S["pos_ready"], 1)
                dve.wait_ge(S["cwT_ps"], g + 1 + 1)
                dve.tensor_copy(cwT, ps[0:E, 4, :].rearrange("p (j n) -> p j n", j=TG)).then_inc(S["cwT_ready"], 1)
                for j in range(TG):
                    i = TG * g + j
                    xr = X[:, ds(i, 1), :].squeeze(1)
                    dve.wait_ge(S["db_ps"], i + 1 + 1)
                    TT(xr, xr, ps[:, 5 + j % 2, 0:D], ALU.add).then_inc(S["d_bias"], 1)
                dve.wait_ge(S["d_bias"], TG * g + TG + 1)
                dve.sem_inc(dve_pad, 1)
                restart()
            c(TT(cnt, run, rowv[:, RO["tstart"]:RO["tstart"] + E], ALU.subtract))
            f()
            NK = NTOK // TW
            cv = cwork[:, 0:E * NK].rearrange("p (e k) -> p e k", e=E)
            c(TT(cv, over(cnt, NK), rowv[:, RO["tstart"] + E:RO["tstart"] + E + NK].unsqueeze(1).to_broadcast([P, E, NK]), ALU.is_gt))
            f()
            c(dve.tensor_reduce(tabf[:, 0:E], cv, AX, ALU.add))
            f()
            c(TS(tabf[:, 0:E], tabf[:, 0:E], 1.0, None, ALU.max))
            f()
            cv = cwork[:, 0:E * E].rearrange("p (e k) -> p e k", e=E)
            c(TT(cv, tabf[:, 0:E].unsqueeze(1).to_broadcast([P, E, E]),
                 rowv[:, RO["tri"]:RO["tri"] + E * E].rearrange("p (e k) -> p e k", e=E), ALU.mult))
            f()
            c(dve.tensor_reduce(tabf[:, E:2 * E], cv, AX, ALU.add))
            f()
            c(TT(tabf[:, 2 * E:2 * E + 1], tabf[:, E - 1:E], tabf[:, 2 * E - 1:2 * E], ALU.add))
            c(dve.tensor_copy(tabf[:, 2 * E + 1:], cnt))
            f()
            c(dve.memset(tstep, 0.0))
            f()
            c(TS(tstep[:, 1:E], tabf[:, 0:E - 1], -float(TW), float(ROWS), ALU.mult, ALU.add))
            c(TS(cwork[:, 0:1], tabf[:, 2 * E:2 * E + 1], -1.0, None, ALU.add))
            f()
            c(TS(tk, rowv[:, RO["tstart"] + E + NK:RO["tstart"] + E + NK + MT], cwork[:, 0:1], None, ALU.min))
            f()
            c(TT(tcmp, over(tk, E), tabf[:, E:2 * E].unsqueeze(1).to_broadcast([P, MT, E]), ALU.is_ge))
            f()
            c(TT(tcmp, tcmp, tstep.unsqueeze(1).to_broadcast([P, MT, E]), ALU.mult))
            f()
            c(dve.tensor_reduce(tilef, tcmp, AX, ALU.add))
            f()
            c(STT(tilef, tk, float(TW), tilef, ALU.mult, ALU.add))
            f()
            c(dve.tensor_copy(tiletab, tilef))
            f()
            dve.tensor_copy(tab, tabf).then_inc(S["tab_ready"], 1)
            dve.wait_ge(S["tab_ready"], 1 + 1)

            def take_rows(k):
                dve.wait_ge(S["t_ps"], k + 1 + 1)
                dve.tensor_copy(xT, ps[:, 0, 0:KB * TW].rearrange("p (k n) -> p k n", k=KB)).then_inc(S["xT_ready"], 1)

            def take_meta(k):
                dve.tensor_copy(meta, xt[:, :, D:RW]).then_inc(S["meta_ready"], 1)

            take_rows(0)
            take_meta(0)
            with dve.Fori(0, E) as e:
                tiles = dve.value_load(tab[0:1, ds(e, 1)], min_val=1, max_val=NTOK // TW)
                first = dve.value_load(tab[0:1, ds(E + e, 1)], min_val=0, max_val=60)
                with dve.Fori(0, tiles) as j:
                    k = dve.snap(first + j)
                    dve.wait_ge(S["u_ps"], HB * k + HB + 1)
                    take_rows(k + 1)
                    for r in range(SUB):
                        dve.wait_ge(S["y_gone"], SUB * k + 1)
                        dve.wait_ge(S["meta_ready"], k + 1 + 1)
                        dve.wait_ge(S["dn_ps"], SUB * k + r + 1 + 1)
                        dve.sem_inc(dve_pad, 1)
                        TS(ysc[:, r, :], ps[:, 6 + r, 0:D], meta[:, r, ds(e + 1, 1)], None, ALU.mult).then_inc(S["y_ready"], 1)
                        dve.tensor_copy(ytok[:, r:r + 1], meta[:, r, 0:1]).then_inc(S["y_ready"], 1)
                    dve.wait_ge(S["y_ready"], 2 * SUB * (k + 1) + 1)
                    dve.sem_inc(dve_pad, 1)
                    take_meta(k + 1)

        @block.scalar
        def _(act):
            A = act.activation
            for name in act_names:
                act.sem_inc(S[name], 1)
            for r in range(2):
                act.wait_ge(S["ln_var"], r + 1 + 1)
                A(std[:, :], var[:, :], ACT.Sqrt).then_inc(S["ln_std"], 1)
                if r == 0:
                    act.wait_ge(S["aneg_in"], 1 + 1)
                    A(aneg[:, :], aneg[:, :], ACT.Exp).then_inc(S["aneg_exp"], 1)
            with act.Fori(0, NG) as g:
                act.wait_ge(S["dt_abs"], g + 1 + 1)
                A(small["e"][:, :, :], small["abs"][:, :, :], ACT.Exp, scale=-1.0).then_inc(S["dt_e"], 1)
                act.wait_ge(S["dt_w"], g + 1 + 1)
                A(small["lw"][:, :, :], small["w"][:, :, :], ACT.Ln).then_inc(S["dt_lw"], 1)
                act.wait_ge(S["conv_done"], XB * g + 1)
                for k in range(XB):
                    pp = P if k < IB else NS
                    act.wait_ge(S["x_ps"], XB * g + k + 1 + 1)
                    A(pre[0:pp, k, TAPS - 1:TAPS - 1 + GW], ps[0:pp, k % 2, :], ACT.Copy).then_inc(S["x_ev"], 1)
                for j in range(TG):
                    act.wait_ge(S["z_ps"], TG * g + j + 1 + 1)
                    A(zs[:, j, :], bank(j % 2), ACT.Silu).then_inc(S["z_act"], 1)
                for k in range(XB):
                    pp = P if k < IB else NS
                    act.wait_ge(S["conv_done"], XB * g + k + 1 + 1)
                    A(xbc[0:pp, k, :], xbc[0:pp, k, :], ACT.Silu,
                      bias=colv[0:pp, CO["convb"] + k:CO["convb"] + k + 1]).then_inc(S["x_act"], 1)
                act.wait_ge(S["c_ps"], g + 1 + 1)
                A(cexp[:, :, :, :].rearrange("p a j h -> p (a j h)"), bank(7, 3 * TG * NH), ACT.Exp).then_inc(S["c_exp"], 1)

                def before(j):
                    s = j % 2
                    i = TG * g + j
                    act.wait_ge(S["xT_ps"], i + 1 + 1)
                    A(xs[s], bank(4), ACT.Copy).then_inc(S["xs_ready"], 1)
                    act.wait_ge(S["seg_ps"], i + 1 + 1)
                    A(wgt[s].rearrange("p (c h) n -> p c (h n)", c=2), ps[:, 2:4, :], ACT.Exp).then_inc(S["e_ready"], 1)

                def after_(j):
                    i = TG * g + j
                    act.wait_ge(S["yg_ready"], i + 1 + 1)
                    act.wait_ge(S["ss_ready"], i + 1)
                    A(sq[:, :], ygat[:, j, :], ACT.Square, accum_out=ss[:, j:j + 1]).then_inc(S["ss_ready"], 1)

                before(0)
                for j in range(TG):
                    if j + 1 < TG:
                        before(j + 1)
                    after_(j)
                act.wait_ge(S["rms_var"], g + 1 + 1)
                A(sstd[:, :], sv[:, :], ACT.Sqrt).then_inc(S["rms_std"], 1)
                for j in range(TG):
                    i = TG * g + j
                    act.wait_ge(S["yT_ps"], i + 1 + 1)
                    A(yT[:, :, :].rearrange("p k n -> p (k n)"), bank(1 + 6 * (j % 2)), ACT.Copy).then_inc(S["yT_ready"], 1)
            with act.Fori(0, NG) as g:
                act.wait_ge(S["b_var"], g + 1 + 1)
                A(std[:, 0:TG], var[:, 0:TG], ACT.Sqrt).then_inc(S["b_std"], 1)
                act.wait_ge(S["b_dn_ps"], TG * g + 1)
                for m in range(FB):
                    act.wait_ge(S["b_up_ps"], FB * g + m + 1 + 1)
                    A(gT[:, m, :], bank(2 + m % 4), ACT.Gelu, bias=col("fcb", m)).then_inc(S["b_gel"], 1)
            act.wait_ge(S["c_var"], 1 + 1)
            A(std[:, :], var[:, :], ACT.Sqrt).then_inc(S["c_std"], 1)

            def att_exp(g, u):
                s = u % 2
                act.wait_ge(S["c_sub"], 16 * g + u + 1 + 1)
                act.sem_inc(act_pad, 1)
                A(pr[s], sc[s], ACT.Exp).then_inc(S["p_ready"], 1)

            def att_group(g, following):
                for u in range(16):
                    act.wait_ge(S["pT_ps"], 16 * g + u + 1 + 1)
                    A(pT[u % 2][0:KT, :, :].rearrange("p (c h) n -> p c (h n)", c=2), ps[0:KT, 6:8, :], ACT.Copy).then_inc(S["pT_ready"], 1)
                    if u % 4 == 1 and u > 4:
                        att_turn(g, u // 4 - 1)
                    if u < 14:
                        att_exp(g, u + 2)
                att_turn(g, TG - 1)
                if following is not None:
                    for u in range(2):
                        att_exp(following, u)

            def att_turn(g, j):
                act.wait_ge(S["cxT_ps"], TG * g + j + 1 + 1)
                A(cxT.rearrange("p k n -> p (k n)"), ps[:, 0, 0:D], ACT.Copy).then_inc(S["cxT_ready"], 1)

            for u in range(2):
                att_exp(0, u)
            with act.Fori(0, NG - 1) as g:
                att_group(g, act.snap(g + 1))
            att_group(NG - 1, None)
            with act.Fori(0, NG) as g:
                act.wait_ge(S["d_var"], g + 1 + 1)
                A(std[:, 0:TG], var[:, 0:TG], ACT.Sqrt).then_inc(S["d_std"], 1)
                act.wait_ge(S["d_shift"], g + 1 + 1)
                A(tex[:, :, :], tsh[:, :, :], ACT.Exp).then_inc(S["d_exp"], 1)
            act.wait_ge(S["tab_ready"], 1 + 1)

            def hidden(e, s, ep):
                first = act.value_load(tab[0:1, ds(E + e, 1)], min_val=0, max_val=60)
                tiles = act.value_load(tab[0:1, ds(e, 1)], min_val=1, max_val=NTOK // TW)
                act.wait_ge(exp_in[s], 3 * 16 * ep + 3 * 16)
                act.sem_inc(act_pad, 1)
                with act.Fori(0, tiles) as j:
                    k = act.snap(first + j)
                    act.wait_ge(S["dn_ps"], SUB * k + 1)
                    for m in range(HB):
                        act.wait_ge(S["u_ps"], HB * k + m + 1 + 1)
                        A(eT[:, m, :], bank(2 + m % 4, TW), ACT.Gelu, bias=bup[s][:, m:m + 1]).then_inc(S["d_gel"], 1)

            with act.Fori(0, E // 2) as ep:
                for s in range(2):
                    hidden(act.snap(2 * ep + s), s, ep)

        @block.gpsimd
        def _(pool):
            TT = pool.tensor_tensor
            for name in pool_names:
                pool.sem_inc(S[name], 1)
            with batch_groups(pool) as (b, _, g):
                def before(j):
                    s = j % 2
                    i = TG * g + j
                    if j == 0:
                        pool.wait_ge(S["a_ready"], g + 1 + 1)
                    pool.wait_ge(S["seg_ps"], i + 1)
                    TT(aU, upto.unsqueeze(1).to_broadcast([P, NH, P]), over(small["a"][:, j, :], P), ALU.mult).then_inc(S["aU_ready"], 1)
                    pool.wait_ge(S["xs_ready"], i + 1 + 1)
                    TT(xsD[s], xs[s], rowv[:, RO["dpar"]:RO["dpar"] + DI], ALU.mult).then_inc(S["xsD_ready"], 1)
                    if j == 0:
                        pool.wait_ge(S["c_exp"], g + 1 + 1)
                    pool.wait_ge(S["xdt_ready"], i + 1 + 1)
                    TT(heads(xw[s]), heads(xdt[s]), over(cexp[:, 1, j, :], HD), ALU.mult).then_inc(S["xw_ready"], 1)

                def main(j):
                    s = j % 2
                    i = TG * g + j
                    pool.wait_ge(S["state_ready"], i + b + 1 + 1)
                    pool.wait_ge(S["off_ps"], i + 1 + 1)
                    TT(heads(sdec[0:NS, :]), heads(state[0:NS, :]), over(cexp[0:NS, 2, j, :], HD), ALU.mult).then_inc(S["sdec_ready"], 1)
                    pool.wait_ge(S["y1_ready"], i + 1 + 1)
                    pool.wait_ge(S["xsD_ready"], i + 1 + 1)
                    TT(y1, y1, xsD[s], ALU.add).then_inc(S["y1d_ready"], 1)

                before(0)
                for j in range(TG):
                    if j + 1 < TG:
                        before(j + 1)
                    main(j)
            with pool.Fori(0, NT) as i:
                pool.wait_ge(S["b_res"], i + 1 + 1)
                pool.sem_inc(pool_pad, 1)
                xr = X[:, ds(i, 1), :].squeeze(1)
                TT(xr, xr, HR[:, ds(i, 1), :].squeeze(1), ALU.add).then_inc(S["b_x"], 1)
            pool.wait_ge(S["kv_ready"], 1 + 1)
            with pool.Fori(0, NG) as g:
                for u in range(16):
                    s = u % 2
                    pool.wait_ge(S["c_max"], 16 * g + u + 1 + 1)
                    TT(sc[s], sc[s], over(smx[s][:, :], S2), ALU.subtract).then_inc(S["c_sub"], 1)
            with pool.Fori(0, NG) as g:
                pool.wait_ge(S["cw_ready"], g + 1 + 1)
                pool.wait_ge(S["pos_ready"], g + 1 + 1)
                pool.sem_inc(pool_pad, 1)
                for j in range(TG):
                    for r in range(3):
                        pool.indirect_dma_start(slots, bass.IndirectOffsetOnAxis(ap=posk[:, 3 * j + r:3 * j + r + 1], axis=0),
                                                rowx[:, j, :], None).then_inc(rows_out, 16)
                pool.wait_ge(rows_out, 3 * TG * 16 * g + 3 * TG * 16)
                pool.sem_inc(S["rows_gone"], 1)
            pool.wait_ge(acc_in, 16 * (NG + 1))
            pool.wait_ge(S["tab_ready"], 1 + 1)
            with pool.Fori(0, E) as e:
                tiles = pool.value_load(tab[0:1, ds(e, 1)], min_val=1, max_val=NTOK // TW)
                first = pool.value_load(tab[0:1, ds(E + e, 1)], min_val=0, max_val=60)
                with pool.Fori(0, tiles) as j:
                    k = pool.snap(first + j)
                    for r in range(SUB):
                        pool.wait_ge(S["y_ready"], 2 * (SUB * k + r + 1) + 1)
                        pool.sem_inc(pool_pad, 1)
                        pool.indirect_dma_start(t["out"], bass.IndirectOffsetOnAxis(ap=ytok[:, r:r + 1], axis=0),
                                                ysc[:, r, :], None, compute_op=ALU.add).then_inc(acc_out, 16)
                        pool.wait_ge(acc_out, 16 * (SUB * k + r + 1))
                        pool.sem_inc(S["y_gone"], 1)

        @block.tensor
        def _(pe):
            mm = pe.matmul
            for name in pe_names:
                pe.sem_inc(S[name], 1)
            pe.wait_ge(prm_in, 8 * 16)

            def turn_group(ready, done, g, src=nrm):
                pe.wait_ge(S[ready], g + 1 + 1)
                for k in range(KB):
                    for j in range(TG):
                        ins = pe.transpose(ps[:, k, j * P:(j + 1) * P], src[:, j, k * P:(k + 1) * P], ident)
                    ins.then_inc(S[done], 1)

            pe.wait_ge(S["wout_ready"], 1 + 1)
            with batch_groups(pe) as (b, _, g):
                pe.wait_ge(S["h_done"], TG * g + 1)
                turn_group("n_ready", "nT_ps", g)
                pe.wait_ge(S["nT_ready"], KB * g + KB + 1)
                for j in range(TG):
                    for k in range(KB):
                        ins = mm(ps[:, 7, j * NH:(j + 1) * NH], nT[:, k, j * P:(j + 1) * P], win[:, k, EP - NH:EP],
                                 start=(k == 0), stop=(k == KB - 1))
                ins.then_inc(S["dt_ps"], 1)
                for m in range(XB):
                    c0 = DI + (m * P if m < IB else DI + (m - IB) * NS)
                    w = P if m < IB else NS
                    if m >= 2:
                        pe.wait_ge(S["x_ev"], XB * g + m - 1 + 1)
                    for k in range(KB):
                        ins = mm(ps[0:w, m % 2, :], win[:, k, c0:c0 + w], nT[:, k, :], start=(k == 0), stop=(k == KB - 1))
                    ins.then_inc(S["x_ps"], 1)
                for j in range(TG):
                    if j < 2:
                        pe.wait_ge(S["x_ev"], XB * g + XB - 1 + j + 1)
                    else:
                        pe.wait_ge(S["z_act"], TG * g + j - 1 + 1)
                    for k in range(KB):
                        ins = mm(bank(j % 2), nT[:, k, j * P:(j + 1) * P], win[:, k, 0:DI], start=(k == 0), stop=(k == KB - 1))
                    ins.then_inc(S["z_ps"], 1)
                pe.wait_ge(S["a_ready"], g + 1 + 1)
                av = small["a"][:, :, :].rearrange("p j h -> p (j h)")
                for r, lhs in enumerate((upto, after, ones)):
                    ins = mm(ps[:, 7, r * TG * NH:(r + 1) * TG * NH], lhs, av, start=True, stop=True)
                ins.then_inc(S["c_ps"], 1)

                def before(j):
                    i = TG * g + j
                    tok = slice(j * P, (j + 1) * P)
                    if j == 0:
                        pe.wait_ge(S["x_act"], XB * g + XB + 1)
                    pe.wait_ge(S["xs_ready"], i + 1)
                    for k in range(IB):
                        ins = pe.transpose(ps[:, 4, k * P:(k + 1) * P], xbc[:, k, tok], ident)
                    ins.then_inc(S["xT_ps"], 1)
                    pe.wait_ge(S["gm_ready"], i + 1)
                    mm(ps[:, 5, P:2 * P], xbc[0:NS, IB, tok], xbc[0:NS, IB + 1, tok], start=True, stop=True)
                    pe.transpose(ps[:, 5, 0:NS], xbc[0:NS, IB, tok], ident[0:NS, 0:NS]).then_inc(S["bg_ps"], 1)
                    pe.wait_ge(S["aU_ready"], i + 1 + 1)
                    pe.wait_ge(S["e_ready"], i + 1)
                    for r in range(2):
                        ins = mm(bank(2 + r), after, aU[:, r * 4:(r + 1) * 4, :].rearrange("p h n -> p (h n)"), start=True, stop=True)
                    ins.then_inc(S["seg_ps"], 1)

                def main(j):
                    s = j % 2
                    i = TG * g + j
                    tok = slice(j * P, (j + 1) * P)
                    if j == 0:
                        pe.wait_ge(S["c_exp"], g + 1 + 1)
                        pe.wait_ge(S["z_act"], TG * g + TG + 1)
                    pe.wait_ge(S["y1_ready"], i + 1)
                    pe.wait_ge(S["state_ready"], i + b + 1 + 1)
                    mm(bank(7), xbc[0:NS, IB + 1, tok], state[0:NS, :], start=True, stop=True).then_inc(S["off_ps"], 1)
                    pe.wait_ge(S["xw_ready"], i + 1 + 1)
                    pe.wait_ge(S["gm_ready"], i + 1 + 1)
                    mm(ps[0:NS, 0, :], bst[s], xw[s], start=True, stop=True).then_inc(S["st_ps"], 1)
                    pe.wait_ge(S["yg_ready"], i + 1)
                    pe.wait_ge(S["w_ready"], i + 1 + 1)
                    for h in range(NH):
                        ins = mm(ps[:, 6, h * HD:(h + 1) * HD], wgt[s][:, h, :], xdt[s][:, h * HD:(h + 1) * HD], start=True, stop=True)
                    ins.then_inc(S["y_ps"], 1)

                before(0)
                for j in range(TG):
                    if j + 1 < TG:
                        before(j + 1)
                    main(j)
                pe.wait_ge(S["yg_ready"], TG * g + TG + 1)
                pe.wait_ge(S["state_ready"], TG * g + TG + b + 1 + 1)
                for j in range(TG):
                    i = TG * g + j
                    if j >= 2:
                        pe.wait_ge(S["h_done"], i - 1 + 1)
                    for k in range(IB):
                        ins = pe.transpose(ps[:, 1 + 6 * (j % 2), k * P:(k + 1) * P], ygat[:, j, k * P:(k + 1) * P], ident)
                    ins.then_inc(S["yT_ps"], 1)
                    pe.wait_ge(S["yT_ready"], i + 1 + 1)
                    for k in range(IB):
                        ins = mm(ps[:, 6 * (j % 2), 0:D], yT[:, k, :], wout[:, k, :], start=(k == 0), stop=(k == IB - 1))
                    ins.then_inc(S["op_ps"], 1)

            pe.wait_ge(mlp_in, 2 * 16)
            pe.wait_ge(S["h_done"], NT + 1)
            with pe.Fori(0, NG) as g:
                turn_group("b_n", "b_nT_ps", g)
                pe.wait_ge(S["b_nT"], KB * g + KB + 1)
                for m in range(FB):
                    pe.wait_ge(S["b_gel"], FB * g + max(m - 3, 0) + 1)
                    for k in range(KB):
                        ins = mm(bank(2 + m % 4), wfc[:, k, m * P:(m + 1) * P], nT[:, k, :], start=(k == 0), stop=(k == KB - 1))
                    ins.then_inc(S["b_up_ps"], 1)
                pe.wait_ge(S["b_gel"], FB * g + FB + 1)
                for j in range(TG):
                    i = TG * g + j
                    pe.wait_ge(S["b_res"], TG * g + max(j - 1, 0) + 1)
                    for m in range(FB):
                        ins = mm(ps[:, 6 + j % 2, 0:D], gT[:, m, j * P:(j + 1) * P], wproj[:, m, :], start=(m == 0), stop=(m == FB - 1))
                    ins.then_inc(S["b_dn_ps"], 1)

            pe.wait_ge(att_in, 9 * 16)
            pe.wait_ge(S["b_nT"], KB * NG + 1)
            for m in range(KB):
                for k in range(KB):
                    ins = mm(ps[:, m, 0:B * S2], wk[:, k, m * P:(m + 1) * P], ctxT[:, k, :], start=(k == 0), stop=(k == KB - 1))
                ins.then_inc(S["k_ps"], 1)
            for kt in range(2):
                for b in range(B):
                    for k in range(KB):
                        c0 = b * S2 + kt * KT
                        ins = mm(ps[0:KT, 2 + kt * B + b, 0:D], ctxT[:, k, c0:c0 + KT], wv[:, k, :], start=(k == 0), stop=(k == KB - 1))
                    ins.then_inc(S["v_ps"], 1)

            def att_turn(g, k):
                pe.wait_ge(S["c_n"], g + 1 + 1)
                if isinstance(g, int):
                    if k == 1:
                        pe.wait_ge(S["c_nT"], 1 + 1)
                else:
                    pe.wait_ge(S["c_out"], TG * (g - 1) + k + 1)
                for j in range(TG):
                    ins = pe.transpose(ps[:, 0, j * P:(j + 1) * P], nrm[:, j, k * P:(k + 1) * P], ident)
                ins.then_inc(S["c_nT_ps"], 1)

            def att_query(g):
                pe.wait_ge(S["c_nT"], KB * g + KB + 1)
                for m in range(KB):
                    for k in range(KB):
                        ins = mm(bank(2 + m), wq[:, k, m * P:(m + 1) * P], nT[:, k, :], start=(k == 0), stop=(k == KB - 1))
                    ins.then_inc(S["q_ps"], 1)

            def att_scores(g, u):
                s, j, k, q = u % 2, u // 4, u % 4 // 2, u % 2
                if u < 2:
                    pe.wait_ge(S["c_q"], KB * g + KB + 1)
                if not (isinstance(g, int) and u < 2):
                    pe.wait_ge(S["c_sc"], 16 * g + u - 1 + 1)
                for r in range(2):
                    c0 = (4 * q + 2 * r) * S2
                    ins = mm(ps[:, 2 + 2 * s + r, 0:2 * S2], qT[:, k, j * P:(j + 1) * P],
                             kbd[:, k, ds(g // GPB, 1), c0:c0 + 2 * S2].squeeze(1), start=True, stop=True)
                ins.then_inc(S["sc_ps"], 1)

            def att_weights(g, u):
                s = u % 2
                pe.wait_ge(S["p_ready"], 16 * g + u + 1 + 1)
                pe.wait_ge(S["pT_ready"], 16 * g + u + 1)
                for h in range(4):
                    for kt in range(2):
                        w = 2 * h + kt
                        ins = pe.transpose(ps[0:KT, 6 + w // 4, (w % 4) * P:(w % 4 + 1) * P],
                                           pr[s][:, h, kt * KT:(kt + 1) * KT], ident)
                ins.then_inc(S["pT_ps"], 1)

            def att_values(g, u):
                s, j, q = u % 2, u // 4, u % 4
                pe.wait_ge(S["pT_ready"], 16 * g + u + 1 + 1)
                if q == 0:
                    pe.wait_ge(S["cx_ready"], TG * g + j + 1)
                for h in range(4):
                    hh = 4 * q + h
                    for kt in range(2):
                        ins = mm(ps[:, 1, hh * (DK + 1):(hh + 1) * (DK + 1)], pT[s][0:KT, 2 * h + kt, :],
                                 vone[0:KT, kt, ds(g // GPB, 1), hh, :].squeeze(1), start=(kt == 0), stop=(kt == 1))
                ins.then_inc(S["val_ps"], 1) if q < 3 else ins.then_inc(S["ctx_ps"], 1)

            def att_context(g, j, following):
                i = TG * g + j
                if following is not None and j < KB:
                    pe.wait_ge(S["c_nT"], KB * following + j + 1 + 1)
                pe.wait_ge(S["cx_ready"], i + 1 + 1)
                pe.wait_ge(S["c_out"], i + 1)
                for k in range(KB):
                    ins = pe.transpose(ps[:, 0, k * P:(k + 1) * P], cx[:, k * P:(k + 1) * P], ident)
                ins.then_inc(S["cxT_ps"], 1)

            def att_output(g, j):
                i = TG * g + j
                pe.wait_ge(S["cxT_ready"], i + 1 + 1)
                for k in range(KB):
                    ins = mm(ps[:, 0, D:2 * D], cxT[:, k, :], wo[:, k, :], start=(k == 0), stop=(k == KB - 1))
                ins.then_inc(S["co_ps"], 1)

            def att_group(g, following):
                for u in range(16):
                    if u < 14:
                        att_scores(g, u + 2)
                    elif u == 14 and following is not None:
                        pe.wait_ge(S["c_sc"], 16 * g + 14 + 1 + 1)
                        att_query(following)
                    att_weights(g, u)
                    if u > 0:
                        att_values(g, u - 1)
                    if following is not None and u == 3:
                        att_turn(following, 0)
                    if following is not None and u == 8:
                        att_turn(following, 1)
                    if u % 4 == 1 and u > 4:
                        att_context(g, u // 4 - 1, following)
                    if u % 4 == 2 and u > 4:
                        att_output(g, u // 4 - 1)
                if following is not None:
                    att_scores(following, 0)
                att_values(g, 15)
                if following is not None:
                    att_scores(following, 1)
                att_context(g, TG - 1, following)
                att_output(g, TG - 1)

            for k in range(KB):
                att_turn(0, k)
            att_query(0)
            pe.wait_ge(S["kv_ready"], 1 + 1)
            for u in range(2):
                att_scores(0, u)
            with pe.Fori(0, NG - 1) as g:
                att_group(g, pe.snap(g + 1))
            att_group(NG - 1, None)

            pe.wait_ge(S["c_out"], NT + 1)
            with pe.Fori(0, NG) as g:
                turn_group("d_n", "d_nT_ps", g, rowx)
                pe.wait_ge(S["d_nT"], KB * g + KB + 1)
                for j in range(TG):
                    for k in range(KB):
                        ins = mm(ps[:, 2, j * E:(j + 1) * E], nT[:, k, j * P:(j + 1) * P], wg[:, k, :], start=(k == 0), stop=(k == KB - 1))
                ins.then_inc(S["lg_ps"], 1)
                pe.wait_ge(S["sel_ready"], g + 1 + 1)
                for j in range(TG + 1):
                    parts = [(ones, i) for i in range(j)] + ([(upto, j)] if j < TG else [])
                    for n, (lhs, i) in enumerate(parts):
                        ins = mm(ps[:, 3, j * E:(j + 1) * E], lhs, sel[:, i, :], start=(n == 0), stop=(n == len(parts) - 1))
                ins.then_inc(S["pos_ps"], 1)
                pe.wait_ge(S["cw_ready"], g + 1 + 1)
                for j in range(TG):
                    ins = pe.transpose(ps[0:E, 4, j * P:(j + 1) * P], rowx[:, j, D + 1:RW], ident)
                ins.then_inc(S["cwT_ps"], 1)
                pe.wait_ge(S["cwT_ready"], g + 1 + 1)
                for j in range(TG):
                    pe.wait_ge(S["d_bias"], TG * g + max(j - 1, 0) + 1)
                    mm(ps[:, 5 + j % 2, 0:D], cwT[:, j, :], bdn[:, :], start=True, stop=True).then_inc(S["db_ps"], 1)

            def turn_tile(k):
                pe.wait_ge(xt_in, 16 * (k + 1))
                pe.wait_ge(S["xT_ready"], k + 1)
                for m in range(KB):
                    for r in range(SUB):
                        ins = pe.transpose(ps[:, 0, m * TW + r * P:m * TW + (r + 1) * P], xt[:, r, m * P:(m + 1) * P], ident)
                ins.then_inc(S["t_ps"], 1)

            pe.wait_ge(S["d_bias"], NT + 1)
            pe.wait_ge(S["tab_ready"], 1 + 1)
            turn_tile(0)
            with pe.Fori(0, E // 2) as ep:
                for s in range(2):
                    e = pe.snap(2 * ep + s)
                    pe.wait_ge(exp_in[s], 3 * 16 * ep + 3 * 16)
                    pe.sem_inc(pe_pad, 1)
                    tiles = pe.value_load(tab[0:1, ds(e, 1)], min_val=1, max_val=NTOK // TW)
                    first = pe.value_load(tab[0:1, ds(E + e, 1)], min_val=0, max_val=60)
                    with pe.Fori(0, tiles) as j:
                        k = pe.snap(first + j)
                        pe.wait_ge(S["xT_ready"], k + 1 + 1)
                        for m in range(HB):
                            pe.wait_ge(S["d_gel"], HB * k + max(m - 3, 0) + 1)
                            for c in range(KB):
                                ins = mm(bank(2 + m % 4, TW), wup[s][:, c, m * P:(m + 1) * P], xT[:, c, :], start=(c == 0), stop=(c == KB - 1))
                            ins.then_inc(S["u_ps"], 1)
                        pe.wait_ge(S["y_ready"], 2 * SUB * k + 1)
                        for r in range(SUB):
                            for m in range(HB):
                                if r == 0:
                                    pe.wait_ge(S["d_gel"], HB * k + m + 1 + 1)
                                if r == 0 and m == HB // 2:
                                    turn_tile(k + 1)
                                ins = mm(ps[:, 6 + r, 0:D], eT[:, m, r * P:(r + 1) * P], wdn[s][:, m, :], start=(m == 0), stop=(m == HB - 1))
                            ins.then_inc(S["dn_ps"], 1)



def kernel(**inputs):
    import numpy as np
    import concourse.bacc as bacc
    from concourse import mybir
    from concourse.bass_utils import run_bass_kernel_spmd as run

    g = {k: np.asarray(v) for k, v in inputs.items()}
    a = {k[len("L0_attn_"):]: v for k, v in g.items() if k.startswith("L0_attn_")}
    xa = {k[len("L0_xattn_"):]: v for k, v in g.items() if k.startswith("L0_xattn_")}
    ff = {k[len("L0_ffn_"):]: v for k, v in g.items() if k.startswith("L0_ffn_")}
    P = 128
    idx = np.arange(P)

    def cols(v):
        return v.reshape(-1, P).T

    def halves(v):
        out = np.zeros((P, v.shape[1]), v.dtype)
        out[:v.shape[0]] = v
        return out

    cw, cb = a["conv_w"], a["conv_b"][:, None]
    blocks_w = [cw[k * P:(k + 1) * P] for k in range(4)] + [halves(cw[512:576]), halves(cw[576:640])]
    blocks_b = [cb[k * P:(k + 1) * P] for k in range(4)] + [halves(cb[512:576]), halves(cb[576:640])]
    arrays = {
        "x": g["x"],
        "consts": np.stack([np.eye(P), idx[:, None] <= idx[None, :], idx[:, None] > idx[None, :],
                            np.ones((P, P))]).astype(np.float32),
        "headmask": (idx[:, None] // 16 == np.arange(8)[None, :]).astype(np.float32),
        "iota12": np.broadcast_to(np.arange(12, dtype=np.float32), (P, 12)),
        "cols": np.concatenate([cols(a["ln1_w"]), cols(a["ln1_b"]), cols(a["ln2_w"]), cols(a["ln2_b"]),
                                cols(a["fc_b"]), cols(xa["bq"]), cols(xa["bk"]), cols(a["norm_w"])]
                               + blocks_w + blocks_b, axis=1),
        "rows": np.concatenate([a["dt_bias"], a["A_log"], np.repeat(a["D_param"], 64), a["proj_b"],
                                xa["bo"], xa["bv"],
                                (np.arange(12)[:, None] > np.arange(12)[None, :]).astype(np.float32).ravel(),
                                (np.arange(12) * (2048 + TW) - 1).astype(np.float32),
                                (np.arange(2048 // TW) * TW).astype(np.float32),
                                np.arange(80, dtype=np.float32)]),
        "tokid": np.arange(17)[None, :].astype(np.float32) * P + idx[:, None].astype(np.float32),
        "in_proj": a["in_proj_w"].T, "out_proj": a["out_proj_w"].T,
        "fc": a["fc_w"].T, "proj": a["proj_w"].T,
        "Wq": xa["Wq"].T, "Wk": xa["Wk"].T, "Wv": xa["Wv"].T, "Wo": xa["Wo"].T,
        "ctxT": g["ctx_1024"].transpose(2, 0, 1),
        "qmask": g["mask_1xSxS2_ik1"], "kmask": g["mask_BxS2_ik1"],
        "Wg": ff["Wg"], "Wup": ff["Wup"], "Wdown": ff["Wdown"], "bdown": ff["bdown"],
        "bup": ff["bup"].reshape(12, 8, P).transpose(0, 2, 1),
    }
    arrays = {k: np.ascontiguousarray(v) for k, v in arrays.items()}
    nc = bacc.Bacc("TRN2", target_bir_lowering=False, num_devices=1)
    t = {k: nc.dram_tensor("in_" + k, v.shape, mybir.dt.from_np(v.dtype), kind="ExternalInput").ap()
         for k, v in arrays.items()}
    t["out"] = nc.dram_tensor("out_x", (2048 + P, 256), mybir.dt.float32, kind="ExternalOutput").ap()
    build(nc, t)
    r = run(nc, [{"in_" + k: v for k, v in arrays.items()}], core_ids=[0])
    return r.results[0]["out_x"][:2048].reshape(2, 1024, 256)
```

```python
TW = 128


def build(nc, t):
    import concourse.bass as bass
    from concourse import mybir
    from concourse.alu_op_type import AluOpType as ALU
    from contextlib import ExitStack, contextmanager

    F32, U32, I32 = mybir.dt.float32, mybir.dt.uint32, mybir.dt.int32
    ACT = mybir.ActivationFunctionType
    AX = mybir.AxisListType.X
    ds = bass.ds

    P = 128
    B, L, D = t["x"].shape
    NT = B * L // P
    TG = 4
    NG = NT // TG
    GPB = NG // B
    GW = TG * P
    KB = D // P
    DI = t["out_proj"].shape[0]
    IB = DI // P
    NH = 8
    HD = DI // NH
    NS = 64
    TAPS = 4
    XB = IB + 2
    F = t["fc"].shape[1]
    FB = F // P
    AH, DK = 16, 16
    S2 = t["ctxT"].shape[2]
    KT = S2 // 2
    E, _, H = t["Wup"].shape
    HB = H // P
    NTOK = B * L
    SUB = TW // P
    ROWS = NTOK + TW
    MT = 80
    RW = D + 1 + E
    EPS = 1e-5
    NEG = -3.4028234663852886e38

    with ExitStack() as ctx:
        def sb(name, shape, dt=F32):
            return ctx.enter_context(nc.sbuf_tensor(name, shape, dt))

        def sem(name):
            return ctx.enter_context(nc.semaphore(name))

        ps = ctx.enter_context(nc.psum_tensor("ps", [P, 8, 512], F32))

        X = sb("X", [P, NT, D])
        HR = sb("HR", [P, NT, D])
        consts = sb("consts", [P, 4, P])
        ident, upto, after, ones = (consts[:, i, :] for i in range(4))
        headmask = sb("headmask", [P, 8])
        iota12 = sb("iota12", [P, E])
        tokid = sb("tokid", [P, NT + 1])
        colv = sb("colv", [P, t["cols"].shape[1]])
        rowv = sb("rowv", [P, t["rows"].shape[0]])
        r1 = sb("r1", [P, 4096])
        r2 = sb("r2", [P, 4096])
        EP = t["in_proj"].shape[1]
        win = r1[:, 0:KB * EP].rearrange("p (k e) -> p k e", k=KB)
        wout = r1[:, KB * EP:KB * EP + IB * D].rearrange("p (k d) -> p k d", k=IB)
        wfc = r2[:, 0:2048].rearrange("p (k f) -> p k f", k=KB)
        wproj = r2[:, 2048:4096].rearrange("p (k d) -> p k d", k=FB)
        wup = [r[:, 0:2048].rearrange("p (k f) -> p k f", k=KB) for r in (r1, r2)]
        wdn = [r[:, 2048:4096].rearrange("p (k d) -> p k d", k=HB) for r in (r1, r2)]
        bup = [sb(f"bup{s}", [P, HB]) for s in range(2)]
        wq, wk, wv, wo = (sb(n, [P, KB, D]) for n in ("wq", "wk", "wv", "wo"))
        ctxT = sb("ctxT", [P, KB, B * S2])
        kbd = sb("kbd", [P, KB, B, 8 * S2])
        vone = sb("vone", [P, 2, B, AH, DK + 1])
        qmask_i = sb("qmask_i", [P, L // P, S2], I32)
        qmask = qmask_i[:, :, :].bitcast(F32)
        kmask_i = sb("kmask_i", [P, B, S2], I32)
        kmask = kmask_i[:, :, :].bitcast(F32)
        wg = sb("wg", [P, KB, E])
        bdn = [sb(f"bdn{s}", [P, D]) for s in range(2)]

        CO = {"ln1w": 0, "ln1b": 2, "ln2w": 4, "ln2b": 6, "fcb": 8, "bq": 16, "bk": 18, "normw": 20,
              "convw": 24, "convb": 24 + XB * TAPS}
        RO = {"dtb": 0, "alog": 8, "dpar": 16, "projb": 16 + DI, "bo": 16 + DI + D, "bv": 16 + DI + 2 * D, "tri": 16 + DI + 3 * D,
              "tstart": 16 + DI + 3 * D + E * E}
        slots = nc.dram_tensor("slots", [E * ROWS, RW], F32, kind="Internal").ap()

        def col(name, i):
            return colv[:, CO[name] + i:CO[name] + i + 1]

        st = sb("st", [P, NT, 6])
        mean = sb("mean", [P, NT])
        var = sb("var", [P, NT])
        std = sb("std", [P, NT])
        rstd = sb("rstd", [P, NT])
        la = sb("la", [P, NT])
        lb = sb("lb", [P, NT])
        lc = sb("lc", [P, NT])
        nrm = sb("nrm", [P, TG, D])
        nT = sb("nT", [P, KB, GW])

        reg = sb("reg", [P, XB * (GW + 3) + XB * GW + TG * DI])
        o1 = XB * (GW + 3)
        o2 = o1 + XB * GW
        pre = reg[:, 0:o1].rearrange("p (k n) -> p k n", k=XB)
        xbc = reg[:, o1:o2].rearrange("p (k n) -> p k n", k=XB)
        zs = reg[:, o2:o2 + TG * DI].rearrange("p (k n) -> p k n", k=TG)
        gT = reg[:, 0:FB * GW].rearrange("p (k n) -> p k n", k=FB)

        SCR = 11136
        scr = sb("scr", [P, SCR])
        at = [0]

        def cut(n):
            at[0] += n
            assert at[0] <= SCR, at
            return scr[:, at[0] - n:at[0]]

        xs = [cut(DI) for _ in range(2)]
        xdt = [cut(DI) for _ in range(2)]
        xw = [cut(DI) for _ in range(2)]
        xsD = [cut(DI) for _ in range(2)]
        bst = [cut(NS) for _ in range(2)]
        gm = [cut(P) for _ in range(2)]
        wgt = [cut(NH * P).rearrange("p (h n) -> p h n", h=NH) for _ in range(2)]
        aU = cut(NH * P).rearrange("p (h n) -> p h n", h=NH)
        state = cut(DI)
        sdec = cut(DI)
        y1 = cut(DI)
        ygat = cut(TG * DI).rearrange("p (k n) -> p k n", k=TG)
        at[0] = 0
        qT = cut(KB * GW).rearrange("p (k n) -> p k n", k=KB)
        sc = [cut(4 * S2).rearrange("p (h n) -> p h n", h=4) for _ in range(2)]
        pr = [cut(4 * S2).rearrange("p (h n) -> p h n", h=4) for _ in range(2)]
        pT = [cut(8 * P).rearrange("p (h n) -> p h n", h=8) for _ in range(2)]
        cx = cut(D)
        cxT = cut(KB * P).rearrange("p (k n) -> p k n", k=KB)
        yT = sb("yT", [P, IB, P])
        sq = sb("sq", [P, DI])
        mk = sb("mk", [P, S2])
        kTs = sb("kTs", [P, B * S2])
        small = {n: sb("s_" + n, [P, TG, NH]) for n in
                 ("raw", "abs", "e", "w", "lw", "wm", "eq", "den", "q", "dt", "a")}
        aneg = sb("aneg", [P, NH])
        cexp = sb("cexp", [P, 3, TG, NH])
        ss = sb("ss", [P, TG])
        sv = sb("sv", [P, TG])
        sstd = sb("sstd", [P, TG])
        srs = sb("srs", [P, TG])
        smx = [sb(f"smx{i}", [P, 4]) for i in range(2)]
        rsum = sb("rsum", [P, AH])
        gst = cut(TG * 6).rearrange("p (j n) -> p j n", j=TG)
        gmean, gvar, gstd, grstd = (cut(TG) for _ in range(4))
        rowx = cut(TG * RW).rearrange("p (j n) -> p j n", j=TG)
        padrow = cut(RW)
        lg = cut(TG * E).rearrange("p (j n) -> p j n", j=TG)
        top = cut(TG * 8).rearrange("p (j n) -> p j n", j=TG)
        tix = cut(TG * 8).rearrange("p (j n) -> p j n", j=TG).bitcast(U32)
        tixf = cut(TG * 8).rearrange("p (j n) -> p j n", j=TG)
        tsh = cut(TG * 3).rearrange("p (j n) -> p j n", j=TG)
        tex = cut(TG * 3).rearrange("p (j n) -> p j n", j=TG)
        tsum = cut(TG)
        trs = cut(TG)
        tw = cut(TG * 3).rearrange("p (j n) -> p j n", j=TG)
        oh = cut(TG * 3 * E).rearrange("p (j k n) -> p j k n", j=TG, k=3)
        pick = cut(TG * 3 * E).rearrange("p (j k n) -> p j k n", j=TG, k=3)
        sel = cut(TG * E).rearrange("p (j n) -> p j n", j=TG)
        csel = cut(TG * E).rearrange("p (j n) -> p j n", j=TG)
        pos = cut(TG * E).rearrange("p (j n) -> p j n", j=TG)
        posf = cut(TG * 3).rearrange("p (j n) -> p j n", j=TG)
        posk = cut(TG * 3).bitcast(U32)
        run = cut(E)
        cnt = cut(E)
        cwork = cut(E * max(E, NTOK // TW))
        tabf = cut(3 * E + 1)
        tab = cut(3 * E + 1).bitcast(I32)
        tilef = cut(MT)
        tiletab = cut(MT).bitcast(I32)
        tstep = cut(E)
        tcmp = cut(MT * E).rearrange("p (k e) -> p k e", k=MT)
        tk = cut(MT)
        xt = cut(SUB * RW).rearrange("p (j n) -> p j n", j=SUB)
        xT = cut(KB * TW).rearrange("p (k n) -> p k n", k=KB)
        meta = cut(SUB * (1 + E)).rearrange("p (j n) -> p j n", j=SUB)
        ysc = cut(SUB * D).rearrange("p (j n) -> p j n", j=SUB)
        ytok = cut(SUB).bitcast(U32)
        eT = gT[:, :, 0:TW]

        x_in, prm_in, mlp_in, att_in = (sem(n) for n in ("x_in", "prm_in", "mlp_in", "att_in"))
        exp_in = [sem(f"exp_in{s}") for s in range(2)]
        acc_in, rows_out, pad_out, xt_in, acc_out = (sem(n) for n in ("acc_in", "rows_out", "pad_out", "xt_in", "acc_out"))
        dve_step = sem("dve_step")
        dve_pad, pool_pad, act_pad, pe_pad, sp_pad = (sem(n) for n in ("dve_pad", "pool_pad", "act_pad", "pe_pad", "sp_pad"))
        dve_names = ("ln_var n_ready nT_ready dt_abs dt_w a_ready conv_done xdt_ready gm_ready w_ready y1_ready "
                     "state_ready yg_ready rms_var h_done wout_ready "
                     "b_var b_n b_nT b_res "
                     "kv_ready c_var c_n c_nT c_q c_sc cx_ready c_out c_max "
                     "d_var d_n d_nT d_lg d_shift sel_ready pos_taken pos_ready cw_ready tab_ready xT_ready meta_ready y_sum y_ready aneg_in").split()
        pe_names = ("nT_ps dt_ps x_ps z_ps c_ps xT_ps bg_ps seg_ps off_ps st_ps y_ps yT_ps op_ps "
                    "b_nT_ps b_up_ps b_dn_ps k_ps v_ps c_nT_ps q_ps sc_ps pT_ps val_ps ctx_ps cxT_ps co_ps "
                    "d_nT_ps lg_ps pos_ps t_ps u_ps dn_ps").split()
        act_names = ("ln_std dt_e dt_lw x_ev x_act z_act c_exp xs_ready e_ready ss_ready rms_std yT_ready "
                     "b_std b_gel c_std p_ready pT_ready cxT_ready d_ln d_std d_exp d_gel aneg_exp").split()
        pool_names = "aU_ready xsD_ready xw_ready sdec_ready y1d_ready b_x c_sub rows_gone y_gone".split()
        S = {n: sem(n) for n in dve_names + pe_names + act_names + pool_names}

        def bank(i, n=512):
            return ps[:, i, 0:n]

        def heads(ap):
            return ap.rearrange("p (h n) -> p h n", h=NH)

        def over(ap, n):
            return ap.unsqueeze(2).to_broadcast([ap.shape[0], ap.shape[1], n])

        @contextmanager
        def batch_groups(eng):
            with eng.Fori(0, B) as b:
                with eng.Fori(0, GPB) as gi:
                    yield b, gi, eng.snap(b * GPB + gi)

        def load_expert(eng, e, s):
            for dst, src in ((wup[s], t["Wup"].rearrange("e (k p) f -> e p k f", p=P)),
                             (wdn[s], t["Wdown"].rearrange("e (k p) d -> e p k d", p=P)),
                             (bup[s][:, :], t["bup"])):
                eng.dma_start(dst, src[ds(e, 1)].squeeze(0)).then_inc(exp_in[s], 16)
            eng.dma_start(bdn[s][:, :], t["bdown"][ds(e, 1)].squeeze(0).partition_broadcast(P)).then_inc(exp_in[s], 16)

        block = ctx.enter_context(nc.Block())

        @block.sync
        def _(sp):
            xv = t["x"].rearrange("b (t p) d -> p (b t) d", p=P)
            sp.dma_start(X[:, :, :], xv).then_inc(x_in, 16)
            prm = [(consts[:, :, :], t["consts"].rearrange("c p n -> p c n")),
                   (headmask[:, :], t["headmask"]), (iota12[:, :], t["iota12"]), (tokid[:, :], t["tokid"]),
                   (colv[:, :], t["cols"]), (rowv[:, :], t["rows"].partition_broadcast(P)),
                   (win, t["in_proj"].rearrange("(k p) e -> p k e", p=P)),
                   (wout, t["out_proj"].rearrange("(k p) d -> p k d", p=P))]
            for dst, src in prm:
                sp.dma_start(dst, src).then_inc(prm_in, 16)
            assert len(prm) == 8
            sp.dma_start(wfc, t["fc"].rearrange("(k p) f -> p k f", p=P)).then_inc(mlp_in, 16)
            sp.dma_start(wproj, t["proj"].rearrange("(k p) d -> p k d", p=P)).then_inc(mlp_in, 16)
            att = [(w[:, :, :], t[n].rearrange("(k p) d -> p k d", p=P)) for w, n in
                   ((wq, "Wq"), (wk, "Wk"), (wv, "Wv"), (wo, "Wo"), (wg, "Wg"))]
            att += [(ctxT[:, :, :], t["ctxT"].rearrange("(k p) b s -> p k (b s)", p=P)),
                    (qmask_i[:, :, :], t["qmask"].rearrange("o (t p) s -> p (o t) s", p=P)),
                    (kmask_i[:, :, :], t["kmask"].partition_broadcast(P))]
            for dst, src in att:
                sp.dma_start(dst, src).then_inc(att_in, 16)
            assert len(att) == 8
            sp.wait_ge(S["h_done"], NT + 1)
            sp.wait_ge(S["b_dn_ps"], NT + 1)
            load_expert(sp, 0, 0)
            acc = t["out"].rearrange("(t p) d -> p t d", p=P)
            with sp.Fori(0, NG) as g:
                sp.wait_ge(S["c_out"], TG * g + TG + 1)
                sp.dma_start(acc[:, ds(TG * g, TG), :], X[:, ds(TG * g, TG), :]).then_inc(acc_in, 16)
            sp.wait_ge(S["tab_ready"], 1 + 1)
            sp.dma_start(t["out"][NTOK:NTOK + P, :], padrow[:, 0:D]).then_inc(acc_in, 16)
            with sp.Fori(0, E) as e:
                used = sp.value_load(tab[0:1, ds(2 * E + 1 + e, 1)], min_val=0, max_val=NTOK)
                for r in range(SUB):
                    sp.dma_start(slots[ds(e * ROWS + used + r * P, P), :], padrow).then_inc(pad_out, 16)
            sp.wait_ge(rows_out, NT * 3 * 16)
            sp.wait_ge(pad_out, E * SUB * 16)

            def read_tile(k):
                at_row = sp.value_load(tiletab[0:1, ds(k, 1)], min_val=0, max_val=E * ROWS - TW)
                sp.wait_ge(S["t_ps"], k + 1)
                sp.wait_ge(S["meta_ready"], k + 1)
                sp.sem_inc(sp_pad, 1)
                sp.dma_start(xt, slots[ds(at_row, TW), :].rearrange("(r p) n -> p r n", p=P)).then_inc(xt_in, 16)

            def feed(e, s, another):
                first = sp.value_load(tab[0:1, ds(E + e, 1)], min_val=0, max_val=60)
                tiles = sp.value_load(tab[0:1, ds(e, 1)], min_val=1, max_val=NTOK // TW)
                read_tile(first + 1)
                if another:
                    sp.wait_ge(S["dn_ps"], first * SUB + 1)
                    sp.sem_inc(sp_pad, 1)
                    load_expert(sp, e + 1, 1 - s)
                with sp.Fori(1, tiles) as j:
                    read_tile(sp.snap(first + j) + 1)

            read_tile(0)
            with sp.Fori(0, E // 2 - 1) as ep:
                for s in range(2):
                    feed(sp.snap(2 * ep + s), s, True)
            for s in range(2):
                feed(E - 2 + s, s, s == 0)

        @block.vector
        def _(dve):
            n = [0]

            def c(ins):
                n[0] += 1
                ins.then_inc(dve_step, 1)

            def f():
                dve.wait_ge(dve_step, n[0])

            def restart():
                if n[0]:
                    f()
                dve.sem_clear(dve_step)
                n[0] = 0

            TT, TS, STT = dve.tensor_tensor, dve.tensor_scalar, dve.scalar_tensor_tensor

            def moments(a, m, st=st, mean=mean, var=var):
                s = slice(a, a + m)
                c(TT(la[:, s], st[:, s, 1], st[:, s, 4], ALU.add))
                c(TT(lb[:, s], st[:, s, 1], st[:, s, 4], ALU.subtract))
                c(TT(lc[:, s], st[:, s, 2], st[:, s, 5], ALU.add))
                f()
                c(TS(mean[:, s], la[:, s], 0.5, None, ALU.mult))
                c(STT(var[:, s], lb[:, s], 0.25, lb[:, s], ALU.mult, ALU.mult))
                c(TS(lc[:, s], lc[:, s], 1.0 / D, EPS, ALU.mult, ALU.add))
                f()
                return TT(var[:, s], lc[:, s], var[:, s], ALU.add)

            for name in dve_names:
                dve.sem_inc(S[name], 1)
            dve.wait_ge(x_in, 16)
            restart()
            with dve.Fori(0, NT) as i:
                dve.bn_stats(st[:, ds(i, 1), :].squeeze(1), X[:, ds(i, 1), :].squeeze(1)).then_inc(dve_step, 1)
            n[0] = NT
            f()
            moments(0, NT).then_inc(S["ln_var"], 1)
            dve.wait_ge(S["ln_std"], 1 + 1)
            c(dve.reciprocal(rstd[:, :], std[:, :]))
            restart()
            with dve.Fori(0, NT) as i:
                dve.sem_clear(dve_step)
                TS(HR[:, ds(i, 1), :].squeeze(1), X[:, ds(i, 1), :].squeeze(1), mean[:, ds(i, 1)], rstd[:, ds(i, 1)],
                   ALU.subtract, ALU.mult).then_inc(dve_step, 1)
                dve.wait_ge(dve_step, 1)
                dve.bn_stats(st[:, ds(i, 1), :].squeeze(1), HR[:, ds(i, 1), :].squeeze(1)).then_inc(dve_step, 1)
                dve.wait_ge(dve_step, 2)
            n[0] = 2
            restart()
            moments(0, NT).then_inc(S["ln_var"], 1)
            dve.wait_ge(prm_in, 8 * 16)
            TS(aneg[:, :], rowv[:, RO["alog"]:RO["alog"] + NH], 80.0, None, ALU.min).then_inc(S["aneg_in"], 1)
            dve.wait_ge(S["aneg_exp"], 1 + 1)
            c(TS(aneg[:, :], aneg[:, :], -1.0, None, ALU.mult))
            for k in range(IB):
                ins = TS(wout[:, k, :], wout[:, k, :], col("normw", k), None, ALU.mult)
                c(ins) if k < IB - 1 else ins.then_inc(S["wout_ready"], 1)
            dve.wait_ge(S["ln_std"], 2 + 1)
            c(dve.reciprocal(rstd[:, :], std[:, :]))
            restart()

            sm = {k: v[:, :, :] for k, v in small.items()}
            with dve.Fori(0, B) as b:
                dve.memset(state[0:NS, :], 0.0).then_inc(S["state_ready"], 1)
                dve.memset(pre[:, :, 0:TAPS - 1], 0.0).then_inc(dve_step, 1)
                dve.wait_ge(dve_step, 1)
                dve.sem_clear(dve_step)
                with dve.Fori(0, GPB) as gi:
                    g = dve.snap(b * GPB + gi)
                    dve.wait_ge(S["nT_ps"], KB * g + 1)
                    for j in range(TG):
                        i = TG * g + j
                        ins = TS(nrm[:, j, :], HR[:, ds(i, 1), :].squeeze(1), mean[:, ds(i, 1)], rstd[:, ds(i, 1)],
                                 ALU.subtract, ALU.mult)
                        c(ins) if j < TG - 1 else ins.then_inc(S["n_ready"], 1)
                    for k in range(KB):
                        dve.wait_ge(S["nT_ps"], KB * g + k + 1 + 1)
                        TS(nT[:, k, :], bank(k), col("ln1w", k), col("ln1b", k), ALU.mult, ALU.add).then_inc(S["nT_ready"], 1)
                    dve.wait_ge(S["dt_ps"], g + 1 + 1)
                    c(TT(sm["raw"], bank(7, TG * NH).rearrange("p (j h) -> p j h", j=TG),
                         rowv[:, RO["dtb"]:RO["dtb"] + NH].unsqueeze(1).to_broadcast([P, TG, NH]), ALU.add))
                    f()
                    STT(sm["abs"], sm["raw"], -1.0, sm["raw"], ALU.mult, ALU.max).then_inc(S["dt_abs"], 1)
                    dve.wait_ge(S["dt_e"], g + 1 + 1)
                    TS(sm["w"], sm["e"], 1.0, None, ALU.add).then_inc(S["dt_w"], 1)
                    dve.wait_ge(S["dt_w"], g + 1 + 1)
                    c(TS(sm["wm"], sm["w"], -1.0, None, ALU.add))
                    f()
                    c(TS(sm["eq"], sm["wm"], 0.0, None, ALU.is_equal))
                    f()
                    c(TT(sm["den"], sm["wm"], sm["eq"], ALU.add))
                    f()
                    c(dve.reciprocal(sm["q"], sm["den"]))
                    f()
                    c(TT(sm["q"], sm["q"], sm["e"], ALU.mult))
                    c(TT(sm["eq"], sm["eq"], sm["e"], ALU.mult))
                    f()
                    dve.wait_ge(S["dt_lw"], g + 1 + 1)
                    c(TT(sm["q"], sm["q"], sm["lw"], ALU.mult))
                    f()
                    c(TT(sm["q"], sm["q"], sm["eq"], ALU.add))
                    f()
                    c(STT(sm["dt"], sm["raw"], 0.0, sm["q"], ALU.max, ALU.add))
                    f()
                    c(TT(sm["a"], sm["dt"], aneg[:, :].unsqueeze(1).to_broadcast([P, TG, NH]), ALU.mult))
                    f()
                    TS(sm["a"], sm["a"], -104.0, None, ALU.max).then_inc(S["a_ready"], 1)
                    for k in range(XB):
                        pp = P if k < IB else NS
                        dve.wait_ge(S["x_ev"], XB * g + k + 1 + 1)
                        for w in range(TAPS):
                            wc = colv[0:pp, CO["convw"] + k * TAPS + w:CO["convw"] + k * TAPS + w + 1]
                            src = pre[0:pp, k, w:w + GW]
                            if w == 0:
                                c(TS(xbc[0:pp, k, :], src, wc, None, ALU.mult))
                            else:
                                f()
                                ins = STT(xbc[0:pp, k, :], src, wc, xbc[0:pp, k, :], ALU.mult, ALU.add)
                                c(ins) if w < TAPS - 1 else ins.then_inc(S["conv_done"], 1)
                    dve.wait_ge(S["conv_done"], XB * g + XB + 1)
                    c(dve.tensor_copy(pre[:, 0:IB, 0:TAPS - 1], pre[:, 0:IB, GW:GW + TAPS - 1]))
                    c(dve.tensor_copy(pre[0:NS, IB:XB, 0:TAPS - 1], pre[0:NS, IB:XB, GW:GW + TAPS - 1]))

                    def before(j):
                        s = j % 2
                        i = TG * g + j
                        dve.wait_ge(S["xs_ready"], i + 1 + 1)
                        TT(heads(xdt[s]), heads(xs[s]), over(small["dt"][:, j, :], HD), ALU.mult).then_inc(S["xdt_ready"], 1)
                        dve.wait_ge(S["bg_ps"], i + 1 + 1)
                        c(dve.tensor_copy(bst[s], ps[:, 5, 0:NS]))
                        TT(gm[s], ps[:, 5, P:2 * P], upto, ALU.mult).then_inc(S["gm_ready"], 1)

                    def main(j):
                        s = j % 2
                        i = TG * g + j
                        dve.wait_ge(S["gm_ready"], i + 1 + 1)
                        dve.wait_ge(S["e_ready"], i + 1 + 1)
                        TT(wgt[s], wgt[s], gm[s].unsqueeze(1).to_broadcast([P, NH, P]), ALU.mult).then_inc(S["w_ready"], 1)
                        dve.wait_ge(S["off_ps"], i + 1 + 1)
                        dve.wait_ge(S["yg_ready"], i + 1)
                        TT(heads(y1), heads(bank(7)), over(cexp[:, 0, j, :], HD), ALU.mult).then_inc(S["y1_ready"], 1)
                        dve.wait_ge(S["sdec_ready"], i + 1 + 1)
                        dve.wait_ge(S["st_ps"], i + 1 + 1)
                        TT(state[0:NS, :], sdec[0:NS, :], ps[0:NS, 0, :], ALU.add).then_inc(S["state_ready"], 1)
                        dve.wait_ge(S["y_ps"], i + 1 + 1)
                        dve.wait_ge(S["y1d_ready"], i + 1 + 1)
                        c(TT(y1, bank(6), y1, ALU.add))
                        f()
                        TT(ygat[:, j, :], y1, zs[:, j, :], ALU.mult).then_inc(S["yg_ready"], 1)

                    dve.wait_ge(S["c_exp"], g + 1 + 1)
                    dve.wait_ge(S["z_act"], TG * g + TG + 1)
                    before(0)
                    for j in range(TG):
                        if j + 1 < TG:
                            before(j + 1)
                        main(j)
                    dve.wait_ge(S["ss_ready"], TG * g + TG + 1)
                    TS(sv[:, :], ss[:, :], 1.0 / DI, EPS, ALU.mult, ALU.add).then_inc(S["rms_var"], 1)
                    dve.wait_ge(S["rms_std"], g + 1 + 1)
                    c(dve.reciprocal(srs[:, :], sstd[:, :]))
                    f()
                    for j in range(TG):
                        i = TG * g + j
                        dve.wait_ge(S["op_ps"], i + 1 + 1)
                        hr = HR[:, ds(i, 1), :].squeeze(1)
                        STT(hr, ps[:, 6 * (j % 2), 0:D], srs[:, j:j + 1], hr, ALU.mult, ALU.add).then_inc(S["h_done"], 1)
                    restart()

            dve.wait_ge(S["h_done"], NT + 1)
            with dve.Fori(0, NG) as g:
                for j in range(TG):
                    i = TG * g + j
                    c(dve.bn_stats(st[:, j, :], HR[:, ds(i, 1), :].squeeze(1)))
                f()
                moments(0, TG).then_inc(S["b_var"], 1)
                dve.wait_ge(S["b_std"], g + 1 + 1)
                c(dve.reciprocal(rstd[:, 0:TG], std[:, 0:TG]))
                f()
                dve.wait_ge(S["b_nT_ps"], KB * g + 1)
                for j in range(TG):
                    i = TG * g + j
                    ins = TS(nrm[:, j, :], HR[:, ds(i, 1), :].squeeze(1), mean[:, j:j + 1], rstd[:, j:j + 1],
                             ALU.subtract, ALU.mult)
                    c(ins) if j < TG - 1 else ins.then_inc(S["b_n"], 1)
                for k in range(KB):
                    dve.wait_ge(S["b_nT_ps"], KB * g + k + 1 + 1)
                    TS(nT[:, k, :], bank(k), col("ln2w", k), col("ln2b", k), ALU.mult, ALU.add).then_inc(S["b_nT"], 1)
                for j in range(TG):
                    i = TG * g + j
                    hr = HR[:, ds(i, 1), :].squeeze(1)
                    dve.wait_ge(S["b_dn_ps"], i + 1 + 1)
                    c(TT(hr, hr, ps[:, 6 + j % 2, 0:D], ALU.add))
                    f()
                    TT(hr, hr, rowv[:, RO["projb"]:RO["projb"] + D], ALU.add).then_inc(S["b_res"], 1)
                restart()

            dve.wait_ge(att_in, 8 * 16)
            for k in range(KB):
                dve.wait_ge(S["k_ps"], k + 1 + 1)
                c(TS(kTs[:, :], ps[:, k, 0:B * S2], col("bk", k), None, ALU.add))
                f()
                for b in range(B):
                    c(TT(kbd[:, k, b, :].rearrange("p (h s) -> p h s", h=8),
                         kTs[:, b * S2:(b + 1) * S2].unsqueeze(1).to_broadcast([P, 8, S2]),
                         over(headmask[:, :], S2), ALU.mult))
                f()
            c(dve.memset(vone[:, :, :, :, DK:DK + 1], 1.0))
            for kt in range(2):
                for b in range(B):
                    u = kt * B + b
                    dve.wait_ge(S["v_ps"], u + 1 + 1)
                    c(TT(vone[0:KT, kt, b, :, 0:DK], ps[0:KT, 2 + u, 0:D].rearrange("p (h n) -> p h n", h=AH),
                         rowv[0:KT, RO["bv"]:RO["bv"] + D].rearrange("p (h n) -> p h n", h=AH), ALU.add))
            c(TS(qmask, qmask_i[:, :, :], 1, NEG, ALU.is_equal, ALU.mult))
            TS(kmask, kmask_i[:, :, :], 1, NEG, ALU.is_equal, ALU.mult).then_inc(S["kv_ready"], 1)
            restart()

            with dve.Fori(0, NG) as g:
                dve.wait_ge(S["b_x"], TG * g + TG + 1)
                dve.sem_inc(dve_pad, 1)
                for j in range(TG):
                    c(dve.bn_stats(st[:, ds(TG * g + j, 1), :].squeeze(1), X[:, ds(TG * g + j, 1), :].squeeze(1)))
                restart()
            moments(0, NT).then_inc(S["c_var"], 1)
            dve.wait_ge(S["c_std"], 1 + 1)
            c(dve.reciprocal(rstd[:, :], std[:, :]))
            f()

            c(dve.memset(padrow, 0.0))
            f()
            c(dve.tensor_copy(padrow[:, D:D + 1], tokid[:, NT:NT + 1]))
            c(dve.tensor_copy(run, rowv[:, RO["tstart"]:RO["tstart"] + E]))
            f()

            def gate_rows(gg):
                dve.wait_ge(S["d_std"], gg + 1 + 1)
                dve.wait_ge(S["rows_gone"], gg + 1)
                dve.sem_inc(dve_pad, 1)
                c(dve.tensor_copy(rowx[:, :, D], tokid[:, ds(TG * gg, TG)]))
                for j in range(TG):
                    ins = TS(rowx[:, j, 0:D], X[:, ds(TG * gg + j, 1), :].squeeze(1), gmean[:, j:j + 1], grstd[:, j:j + 1],
                             ALU.subtract, ALU.mult)
                    c(ins) if j < TG - 1 else ins.then_inc(S["d_n"], 1)

            def gate_turned(gg, k):
                dve.wait_ge(S["d_nT_ps"], KB * gg + k + 1 + 1)
                dve.sem_inc(dve_pad, 1)
                dve.tensor_copy(nT[:, k, :], bank(0)).then_inc(S["d_nT"], 1)

            def gate_top(gg):
                dve.wait_ge(S["lg_ps"], gg + 1 + 1)
                dve.sem_inc(dve_pad, 1)
                dve.tensor_copy(lg, ps[:, 0, 0:TG * E].rearrange("p (j e) -> p j e", j=TG)).then_inc(S["d_lg"], 1)
                dve.wait_ge(S["d_lg"], gg + 1 + 1)
                dve.sem_inc(dve_pad, 1)
                for j in range(TG):
                    c(dve.max(top[:, j, :], lg[:, j, :]))
                f()
                for j in range(TG):
                    c(dve.max_index(tix[:, j, :], top[:, j, :], lg[:, j, :]))
                TT(tsh, top[:, :, 0:3], top[:, :, 0:1].to_broadcast([P, TG, 3]), ALU.subtract).then_inc(S["d_shift"], 1)
                f()
                c(dve.tensor_copy(tixf, tix))

            def gate_select(gg):
                f()
                c(TT(oh, iota12[:, :].unsqueeze(1).unsqueeze(1).to_broadcast([P, TG, 3, E]),
                     tixf[:, :, 0:3].unsqueeze(3).to_broadcast([P, TG, 3, E]), ALU.is_equal))
                f()
                c(TT(sel, oh[:, :, 0, :], oh[:, :, 1, :], ALU.add))
                f()
                c(TT(sel, sel, oh[:, :, 2, :], ALU.add))
                f()
                c(dve.tensor_copy(csel[:, 0, :], sel[:, 0, :]))
                f()
                for j in range(1, TG):
                    ins = TT(csel[:, j, :], csel[:, j - 1, :], sel[:, j, :], ALU.add)
                    if j < TG - 1:
                        c(ins)
                        f()
                ins.then_inc(S["sel_ready"], 1)

            def gate_weights(gg):
                dve.wait_ge(S["d_exp"], gg + 1 + 1)
                dve.sem_inc(dve_pad, 1)
                c(dve.tensor_reduce(tsum, tex, AX, ALU.add))
                f()
                c(dve.reciprocal(trs, tsum))
                f()
                c(TT(tw, tex, over(trs, 3), ALU.mult))
                f()
                c(TT(pick, oh, tw.unsqueeze(3).to_broadcast([P, TG, 3, E]), ALU.mult))
                f()
                c(TT(pick[:, :, 0, :], pick[:, :, 0, :], pick[:, :, 1, :], ALU.add))
                f()
                TT(rowx[:, :, D + 1:RW], pick[:, :, 0, :], pick[:, :, 2, :], ALU.add).then_inc(S["cw_ready"], 1)

            def gate_slots(gg):
                dve.wait_ge(S["cw_ready"], gg + 1 + 1)
                dve.wait_ge(S["pos_ps"], gg + 1 + 1)
                dve.sem_inc(dve_pad, 1)
                c(TT(pos, ps[:, 0, 0:TG * E].rearrange("p (j e) -> p j e", j=TG),
                     run.unsqueeze(1).to_broadcast([P, TG, E]), ALU.add))
                f()
                TT(run, run, ps[:, 0, TG * E:(TG + 1) * E], ALU.add).then_inc(S["pos_taken"], 1)
                c(TT(pick, oh, pos.unsqueeze(2).to_broadcast([P, TG, 3, E]), ALU.mult))
                f()
                c(dve.tensor_reduce(posf, pick, AX, ALU.add))
                f()
                dve.tensor_copy(posk, posf.rearrange("p j k -> p (j k)")).then_inc(S["pos_ready"], 1)

            def att_norm(g, j):
                i = TG * g + j
                dve.wait_ge(S["c_nT_ps"], KB * g + 1)
                ins = TS(nrm[:, j, :], X[:, ds(i, 1), :].squeeze(1), mean[:, ds(i, 1)], rstd[:, ds(i, 1)],
                         ALU.subtract, ALU.mult)
                c(ins) if j < TG - 1 else ins.then_inc(S["c_n"], 1)

            def att_turned(g, k):
                dve.wait_ge(S["c_nT_ps"], KB * g + k + 1 + 1)
                dve.tensor_copy(nT[:, k, :], bank(0)).then_inc(S["c_nT"], 1)

            def att_query(g):
                for k in range(KB):
                    dve.wait_ge(S["q_ps"], KB * g + k + 1 + 1)
                    TS(qT[:, k, :], bank(2 + k), col("bq", k), 1.0 / DK ** 0.5, ALU.add, ALU.mult).then_inc(S["c_q"], 1)

            def att_scores(g, u):
                s = u % 2
                if u % 4 == 0:
                    c(TT(mk[:, :], qmask[:, ds((g % GPB) * TG + u // 4, 1), :].squeeze(1),
                         kmask[:, ds(g // GPB, 1), :].squeeze(1), ALU.min))
                    f()
                dve.wait_ge(S["sc_ps"], 16 * g + u + 1 + 1)
                if not (first_group(g) and u < 2):
                    dve.wait_ge(S["p_ready"], 16 * g + u - 1 + 1)
                TT(sc[s].rearrange("p (c h) n -> p c h n", c=2),
                   ps[:, 2 + 2 * s:4 + 2 * s, 0:2 * S2].rearrange("p c (h n) -> p c h n", h=2),
                   mk[:, :].unsqueeze(1).unsqueeze(1).to_broadcast([P, 2, 2, S2]), ALU.add).then_inc(S["c_sc"], 1)
                dve.wait_ge(S["c_sc"], 16 * g + u + 1 + 1)
                dve.sem_inc(dve_pad, 1)
                dve.tensor_reduce(smx[s][:, :], sc[s], AX, ALU.max).then_inc(S["c_max"], 1)

            def first_group(g):
                return isinstance(g, int) and g == 0

            def att_normalise(g, j):
                dve.wait_ge(S["ctx_ps"], TG * g + j + 1 + 1)
                dve.sem_inc(dve_pad, 1)
                acc = ps[:, 1, 0:AH * (DK + 1)].rearrange("p (h n) -> p h n", h=AH)
                c(dve.reciprocal(rsum[:, :], acc[:, :, DK]))
                f()
                TT(cx.rearrange("p (h n) -> p h n", h=AH), acc[:, :, 0:DK], over(rsum[:, :], DK), ALU.mult).then_inc(S["cx_ready"], 1)

            def att_output(g, j):
                i = TG * g + j
                xr = X[:, ds(i, 1), :].squeeze(1)
                dve.wait_ge(S["co_ps"], i + 1 + 1)
                c(TT(xr, xr, ps[:, 0, D:2 * D], ALU.add))
                f()
                TT(xr, xr, rowv[:, RO["bo"]:RO["bo"] + D], ALU.add).then_inc(S["c_out"], 1)
                dve.wait_ge(S["c_out"], i + 1 + 1)
                dve.sem_inc(dve_pad, 1)
                c(dve.bn_stats(gst[:, j, :], xr))

            def att_group(g, following, gated):
                for u in range(16):
                    if u % 4 == 1 and u > 4:
                        att_normalise(g, u // 4 - 1)
                    if gated is not None:
                        if u == 3:
                            gate_turned(gated, 0)
                        if u == 4:
                            gate_top(gated)
                        if u == 8:
                            gate_slots(gated)
                    if following is not None:
                        if u == 5:
                            att_turned(following, 0)
                        if u == 9:
                            att_turned(following, 1)
                        if u == 14:
                            att_query(following)
                    if u % 4 == 3 and u > 4:
                        att_output(g, u // 4 - 1)
                    if u < 14:
                        att_scores(g, u + 2)
                    if following is not None and u in (1, 2):
                        att_norm(following, 2 * u - 2)
                        att_norm(following, 2 * u - 1)
                    if gated is not None:
                        if u == 0:
                            gate_rows(gated)
                        if u == 3:
                            gate_turned(gated, 1)
                        if u == 5:
                            gate_select(gated)
                        if u == 6:
                            gate_weights(gated)
                if following is not None:
                    att_scores(following, 0)
                att_normalise(g, TG - 1)
                if following is not None:
                    att_scores(following, 1)
                att_output(g, TG - 1)
                f()
                moments(0, TG, gst, gmean, gvar).then_inc(S["d_var"], 1)
                restart()

            for j in range(TG):
                att_norm(0, j)
            for k in range(KB):
                att_turned(0, k)
            att_query(0)
            for u in range(2):
                att_scores(0, u)
            restart()
            att_group(0, 1, None)
            with dve.Fori(1, NG - 1) as g:
                att_group(g, dve.snap(g + 1), dve.snap(g - 1))
            att_group(NG - 1, None, NG - 2)
            gate_rows(NG - 1)
            for k in range(KB):
                gate_turned(NG - 1, k)
            gate_top(NG - 1)
            gate_select(NG - 1)
            gate_weights(NG - 1)
            gate_slots(NG - 1)

            c(TT(cnt, run, rowv[:, RO["tstart"]:RO["tstart"] + E], ALU.subtract))
            f()
            NK = NTOK // TW
            cv = cwork[:, 0:E * NK].rearrange("p (e k) -> p e k", e=E)
            c(TT(cv, over(cnt, NK), rowv[:, RO["tstart"] + E:RO["tstart"] + E + NK].unsqueeze(1).to_broadcast([P, E, NK]), ALU.is_gt))
            f()
            c(dve.tensor_reduce(tabf[:, 0:E], cv, AX, ALU.add))
            f()
            c(TS(tabf[:, 0:E], tabf[:, 0:E], 1.0, None, ALU.max))
            f()
            cv = cwork[:, 0:E * E].rearrange("p (e k) -> p e k", e=E)
            c(TT(cv, tabf[:, 0:E].unsqueeze(1).to_broadcast([P, E, E]),
                 rowv[:, RO["tri"]:RO["tri"] + E * E].rearrange("p (e k) -> p e k", e=E), ALU.mult))
            f()
            c(dve.tensor_reduce(tabf[:, E:2 * E], cv, AX, ALU.add))
            f()
            c(TT(tabf[:, 2 * E:2 * E + 1], tabf[:, E - 1:E], tabf[:, 2 * E - 1:2 * E], ALU.add))
            c(dve.tensor_copy(tabf[:, 2 * E + 1:], cnt))
            f()
            c(dve.memset(tstep, 0.0))
            f()
            c(TS(tstep[:, 1:E], tabf[:, 0:E - 1], -float(TW), float(ROWS), ALU.mult, ALU.add))
            c(TS(cwork[:, 0:1], tabf[:, 2 * E:2 * E + 1], -1.0, None, ALU.add))
            f()
            c(TS(tk, rowv[:, RO["tstart"] + E + NK:RO["tstart"] + E + NK + MT], cwork[:, 0:1], None, ALU.min))
            f()
            c(TT(tcmp, over(tk, E), tabf[:, E:2 * E].unsqueeze(1).to_broadcast([P, MT, E]), ALU.is_ge))
            f()
            c(TT(tcmp, tcmp, tstep.unsqueeze(1).to_broadcast([P, MT, E]), ALU.mult))
            f()
            c(dve.tensor_reduce(tilef, tcmp, AX, ALU.add))
            f()
            c(STT(tilef, tk, float(TW), tilef, ALU.mult, ALU.add))
            f()
            c(dve.tensor_copy(tiletab, tilef))
            f()
            dve.tensor_copy(tab, tabf).then_inc(S["tab_ready"], 1)
            dve.wait_ge(S["tab_ready"], 1 + 1)

            def take_rows(k):
                dve.wait_ge(S["t_ps"], k + 1 + 1)
                dve.tensor_copy(xT, ps[:, 0, 0:KB * TW].rearrange("p (k n) -> p k n", k=KB)).then_inc(S["xT_ready"], 1)

            def take_meta(k):
                dve.tensor_copy(meta, xt[:, :, D:RW]).then_inc(S["meta_ready"], 1)

            take_rows(0)
            take_meta(0)
            with dve.Fori(0, E // 2) as ep:
                for s in range(2):
                    e = dve.snap(2 * ep + s)
                    dve.wait_ge(exp_in[s], 4 * 16 * ep + 4 * 16)
                    dve.sem_inc(dve_pad, 1)
                    tiles = dve.value_load(tab[0:1, ds(e, 1)], min_val=1, max_val=NTOK // TW)
                    first = dve.value_load(tab[0:1, ds(E + e, 1)], min_val=0, max_val=60)
                    with dve.Fori(0, tiles) as j:
                        k = dve.snap(first + j)
                        dve.wait_ge(S["u_ps"], HB * k + HB + 1)
                        take_rows(k + 1)
                        for r in range(SUB):
                            dve.wait_ge(S["y_gone"], SUB * k + 1)
                            dve.wait_ge(S["meta_ready"], k + 1 + 1)
                            dve.wait_ge(S["dn_ps"], SUB * k + r + 1 + 1)
                            dve.sem_inc(dve_pad, 1)
                            TT(ysc[:, r, :], ps[:, 6 + r, 0:D], bdn[s][:, :], ALU.add).then_inc(S["y_sum"], 1)
                            dve.tensor_copy(ytok[:, r:r + 1], meta[:, r, 0:1]).then_inc(S["y_ready"], 1)
                            dve.wait_ge(S["y_sum"], SUB * k + r + 1 + 1)
                            TS(ysc[:, r, :], ysc[:, r, :], meta[:, r, ds(e + 1, 1)], None, ALU.mult).then_inc(S["y_ready"], 1)
                        dve.wait_ge(S["y_ready"], 2 * SUB * (k + 1) + 1)
                        dve.sem_inc(dve_pad, 1)
                        take_meta(k + 1)

        @block.scalar
        def _(act):
            A = act.activation
            for name in act_names:
                act.sem_inc(S[name], 1)
            for r in range(2):
                act.wait_ge(S["ln_var"], r + 1 + 1)
                A(std[:, :], var[:, :], ACT.Sqrt).then_inc(S["ln_std"], 1)
                if r == 0:
                    act.wait_ge(S["aneg_in"], 1 + 1)
                    A(aneg[:, :], aneg[:, :], ACT.Exp).then_inc(S["aneg_exp"], 1)
            with act.Fori(0, NG) as g:
                act.wait_ge(S["dt_abs"], g + 1 + 1)
                A(small["e"][:, :, :], small["abs"][:, :, :], ACT.Exp, scale=-1.0).then_inc(S["dt_e"], 1)
                act.wait_ge(S["dt_w"], g + 1 + 1)
                A(small["lw"][:, :, :], small["w"][:, :, :], ACT.Ln).then_inc(S["dt_lw"], 1)
                act.wait_ge(S["conv_done"], XB * g + 1)
                for k in range(XB):
                    pp = P if k < IB else NS
                    act.wait_ge(S["x_ps"], XB * g + k + 1 + 1)
                    A(pre[0:pp, k, TAPS - 1:TAPS - 1 + GW], ps[0:pp, k % 2, :], ACT.Copy).then_inc(S["x_ev"], 1)
                for j in range(TG):
                    act.wait_ge(S["z_ps"], TG * g + j + 1 + 1)
                    A(zs[:, j, :], bank(j % 2), ACT.Silu).then_inc(S["z_act"], 1)
                for k in range(XB):
                    pp = P if k < IB else NS
                    act.wait_ge(S["conv_done"], XB * g + k + 1 + 1)
                    A(xbc[0:pp, k, :], xbc[0:pp, k, :], ACT.Silu,
                      bias=colv[0:pp, CO["convb"] + k:CO["convb"] + k + 1]).then_inc(S["x_act"], 1)
                act.wait_ge(S["c_ps"], g + 1 + 1)
                A(cexp[:, :, :, :].rearrange("p a j h -> p (a j h)"), bank(7, 3 * TG * NH), ACT.Exp).then_inc(S["c_exp"], 1)

                def before(j):
                    s = j % 2
                    i = TG * g + j
                    act.wait_ge(S["xT_ps"], i + 1 + 1)
                    A(xs[s], bank(4), ACT.Copy).then_inc(S["xs_ready"], 1)
                    act.wait_ge(S["seg_ps"], i + 1 + 1)
                    A(wgt[s].rearrange("p (c h) n -> p c (h n)", c=2), ps[:, 2:4, :], ACT.Exp).then_inc(S["e_ready"], 1)

                def after_(j):
                    i = TG * g + j
                    act.wait_ge(S["yg_ready"], i + 1 + 1)
                    act.wait_ge(S["ss_ready"], i + 1)
                    A(sq[:, :], ygat[:, j, :], ACT.Square, accum_out=ss[:, j:j + 1]).then_inc(S["ss_ready"], 1)

                before(0)
                for j in range(TG):
                    if j + 1 < TG:
                        before(j + 1)
                    after_(j)
                act.wait_ge(S["rms_var"], g + 1 + 1)
                A(sstd[:, :], sv[:, :], ACT.Sqrt).then_inc(S["rms_std"], 1)
                for j in range(TG):
                    i = TG * g + j
                    act.wait_ge(S["yT_ps"], i + 1 + 1)
                    A(yT[:, :, :].rearrange("p k n -> p (k n)"), bank(1 + 6 * (j % 2)), ACT.Copy).then_inc(S["yT_ready"], 1)
            with act.Fori(0, NG) as g:
                act.wait_ge(S["b_var"], g + 1 + 1)
                A(std[:, 0:TG], var[:, 0:TG], ACT.Sqrt).then_inc(S["b_std"], 1)
                act.wait_ge(S["b_dn_ps"], TG * g + 1)
                for m in range(FB):
                    act.wait_ge(S["b_up_ps"], FB * g + m + 1 + 1)
                    A(gT[:, m, :], bank(2 + m % 4), ACT.Gelu, bias=col("fcb", m)).then_inc(S["b_gel"], 1)
            act.wait_ge(S["c_var"], 1 + 1)
            A(std[:, :], var[:, :], ACT.Sqrt).then_inc(S["c_std"], 1)

            def att_exp(g, u):
                s = u % 2
                act.wait_ge(S["c_sub"], 16 * g + u + 1 + 1)
                act.sem_inc(act_pad, 1)
                A(pr[s], sc[s], ACT.Exp).then_inc(S["p_ready"], 1)

            def gate_std(gg):
                act.wait_ge(S["d_var"], gg + 1 + 1)
                act.sem_inc(act_pad, 1)
                A(gstd, gvar, ACT.Ln).then_inc(S["d_ln"], 1)
                act.wait_ge(S["d_ln"], gg + 1 + 1)
                act.sem_inc(act_pad, 1)
                A(grstd, gstd, ACT.Exp, scale=-0.5).then_inc(S["d_std"], 1)

            def gate_exp(gg):
                act.wait_ge(S["d_shift"], gg + 1 + 1)
                act.sem_inc(act_pad, 1)
                A(tex[:, :, :], tsh[:, :, :], ACT.Exp).then_inc(S["d_exp"], 1)

            def att_group(g, following, gated):
                for u in range(16):
                    act.wait_ge(S["pT_ps"], 16 * g + u + 1 + 1)
                    A(pT[u % 2][0:KT, :, :].rearrange("p (c h) n -> p c (h n)", c=2), ps[0:KT, 6:8, :], ACT.Copy).then_inc(S["pT_ready"], 1)
                    if u % 4 == 1 and u > 4:
                        att_turn(g, u // 4 - 1)
                    if u == 0 and gated is not None:
                        gate_std(gated)
                    if u < 14:
                        att_exp(g, u + 2)
                    if u == 4 and gated is not None:
                        gate_exp(gated)
                att_turn(g, TG - 1)
                if following is not None:
                    for u in range(2):
                        att_exp(following, u)

            def att_turn(g, j):
                act.wait_ge(S["cxT_ps"], TG * g + j + 1 + 1)
                A(cxT.rearrange("p k n -> p (k n)"), ps[:, 0, 0:D], ACT.Copy).then_inc(S["cxT_ready"], 1)

            for u in range(2):
                att_exp(0, u)
            att_group(0, 1, None)
            with act.Fori(1, NG - 1) as g:
                att_group(g, act.snap(g + 1), act.snap(g - 1))
            att_group(NG - 1, None, NG - 2)
            gate_std(NG - 1)
            gate_exp(NG - 1)
            act.wait_ge(S["tab_ready"], 1 + 1)

            def hidden(e, s, ep):
                first = act.value_load(tab[0:1, ds(E + e, 1)], min_val=0, max_val=60)
                tiles = act.value_load(tab[0:1, ds(e, 1)], min_val=1, max_val=NTOK // TW)
                act.wait_ge(exp_in[s], 4 * 16 * ep + 4 * 16)
                act.sem_inc(act_pad, 1)
                with act.Fori(0, tiles) as j:
                    k = act.snap(first + j)
                    act.wait_ge(S["dn_ps"], SUB * k + 1)
                    for m in range(HB):
                        act.wait_ge(S["u_ps"], HB * k + m + 1 + 1)
                        A(eT[:, m, :], bank(2 + m % 4, TW), ACT.Gelu, bias=bup[s][:, m:m + 1]).then_inc(S["d_gel"], 1)

            with act.Fori(0, E // 2) as ep:
                for s in range(2):
                    hidden(act.snap(2 * ep + s), s, ep)

        @block.gpsimd
        def _(pool):
            TT = pool.tensor_tensor
            for name in pool_names:
                pool.sem_inc(S[name], 1)
            with batch_groups(pool) as (b, _, g):
                def before(j):
                    s = j % 2
                    i = TG * g + j
                    if j == 0:
                        pool.wait_ge(S["a_ready"], g + 1 + 1)
                    pool.wait_ge(S["seg_ps"], i + 1)
                    TT(aU, upto.unsqueeze(1).to_broadcast([P, NH, P]), over(small["a"][:, j, :], P), ALU.mult).then_inc(S["aU_ready"], 1)
                    pool.wait_ge(S["xs_ready"], i + 1 + 1)
                    TT(xsD[s], xs[s], rowv[:, RO["dpar"]:RO["dpar"] + DI], ALU.mult).then_inc(S["xsD_ready"], 1)
                    if j == 0:
                        pool.wait_ge(S["c_exp"], g + 1 + 1)
                    pool.wait_ge(S["xdt_ready"], i + 1 + 1)
                    TT(heads(xw[s]), heads(xdt[s]), over(cexp[:, 1, j, :], HD), ALU.mult).then_inc(S["xw_ready"], 1)

                def main(j):
                    s = j % 2
                    i = TG * g + j
                    pool.wait_ge(S["state_ready"], i + b + 1 + 1)
                    pool.wait_ge(S["off_ps"], i + 1 + 1)
                    TT(heads(sdec[0:NS, :]), heads(state[0:NS, :]), over(cexp[0:NS, 2, j, :], HD), ALU.mult).then_inc(S["sdec_ready"], 1)
                    pool.wait_ge(S["y1_ready"], i + 1 + 1)
                    pool.wait_ge(S["xsD_ready"], i + 1 + 1)
                    TT(y1, y1, xsD[s], ALU.add).then_inc(S["y1d_ready"], 1)

                before(0)
                for j in range(TG):
                    if j + 1 < TG:
                        before(j + 1)
                    main(j)
            with pool.Fori(0, NT) as i:
                pool.wait_ge(S["b_res"], i + 1 + 1)
                pool.sem_inc(pool_pad, 1)
                xr = X[:, ds(i, 1), :].squeeze(1)
                TT(xr, xr, HR[:, ds(i, 1), :].squeeze(1), ALU.add).then_inc(S["b_x"], 1)
            pool.wait_ge(S["kv_ready"], 1 + 1)

            def att_shift(g, u):
                s = u % 2
                pool.wait_ge(S["c_max"], 16 * g + u + 1 + 1)
                TT(sc[s], sc[s], over(smx[s][:, :], S2), ALU.subtract).then_inc(S["c_sub"], 1)

            def scatter(j, r):
                pool.indirect_dma_start(slots, bass.IndirectOffsetOnAxis(ap=posk[:, 3 * j + r:3 * j + r + 1], axis=0),
                                        rowx[:, j, :], None).then_inc(rows_out, 16)

            def scattered(gg):
                pool.wait_ge(rows_out, 3 * TG * 16 * gg + 3 * TG * 16)
                pool.sem_inc(S["rows_gone"], 1)

            def att_group(g, following, gated):
                for u in range(2, 16):
                    att_shift(g, u)
                    if gated is not None and u >= 10:
                        if u == 10:
                            pool.wait_ge(S["pos_ready"], gated + 1 + 1)
                            pool.sem_inc(pool_pad, 1)
                        for n in (2 * (u - 10), 2 * (u - 10) + 1):
                            scatter(n // 3, n % 3)
                if following is not None:
                    for u in range(2):
                        att_shift(following, u)
                if gated is not None:
                    scattered(gated)

            for u in range(2):
                att_shift(0, u)
            att_group(0, 1, None)
            with pool.Fori(1, NG - 1) as g:
                att_group(g, pool.snap(g + 1), pool.snap(g - 1))
            att_group(NG - 1, None, NG - 2)
            pool.wait_ge(S["pos_ready"], NG + 1)
            for n in range(3 * TG):
                scatter(n // 3, n % 3)
            pool.wait_ge(acc_in, 16 * (NG + 1))
            pool.wait_ge(S["tab_ready"], 1 + 1)
            with pool.Fori(0, E) as e:
                tiles = pool.value_load(tab[0:1, ds(e, 1)], min_val=1, max_val=NTOK // TW)
                first = pool.value_load(tab[0:1, ds(E + e, 1)], min_val=0, max_val=60)
                with pool.Fori(0, tiles) as j:
                    k = pool.snap(first + j)
                    for r in range(SUB):
                        pool.wait_ge(S["y_ready"], 2 * (SUB * k + r + 1) + 1)
                        pool.sem_inc(pool_pad, 1)
                        pool.indirect_dma_start(t["out"], bass.IndirectOffsetOnAxis(ap=ytok[:, r:r + 1], axis=0),
                                                ysc[:, r, :], None, compute_op=ALU.add).then_inc(acc_out, 16)
                        pool.wait_ge(acc_out, 16 * (SUB * k + r + 1))
                        pool.sem_inc(S["y_gone"], 1)

        @block.tensor
        def _(pe):
            mm = pe.matmul
            for name in pe_names:
                pe.sem_inc(S[name], 1)
            pe.wait_ge(prm_in, 8 * 16)

            def turn_group(ready, done, g, src=nrm):
                pe.wait_ge(S[ready], g + 1 + 1)
                for k in range(KB):
                    for j in range(TG):
                        ins = pe.transpose(ps[:, k, j * P:(j + 1) * P], src[:, j, k * P:(k + 1) * P], ident)
                    ins.then_inc(S[done], 1)

            pe.wait_ge(S["wout_ready"], 1 + 1)
            with batch_groups(pe) as (b, _, g):
                pe.wait_ge(S["h_done"], TG * g + 1)
                turn_group("n_ready", "nT_ps", g)
                pe.wait_ge(S["nT_ready"], KB * g + KB + 1)
                for j in range(TG):
                    for k in range(KB):
                        ins = mm(ps[:, 7, j * NH:(j + 1) * NH], nT[:, k, j * P:(j + 1) * P], win[:, k, EP - NH:EP],
                                 start=(k == 0), stop=(k == KB - 1))
                ins.then_inc(S["dt_ps"], 1)
                for m in range(XB):
                    c0 = DI + (m * P if m < IB else DI + (m - IB) * NS)
                    w = P if m < IB else NS
                    if m >= 2:
                        pe.wait_ge(S["x_ev"], XB * g + m - 1 + 1)
                    for k in range(KB):
                        ins = mm(ps[0:w, m % 2, :], win[:, k, c0:c0 + w], nT[:, k, :], start=(k == 0), stop=(k == KB - 1))
                    ins.then_inc(S["x_ps"], 1)
                for j in range(TG):
                    if j < 2:
                        pe.wait_ge(S["x_ev"], XB * g + XB - 1 + j + 1)
                    else:
                        pe.wait_ge(S["z_act"], TG * g + j - 1 + 1)
                    for k in range(KB):
                        ins = mm(bank(j % 2), nT[:, k, j * P:(j + 1) * P], win[:, k, 0:DI], start=(k == 0), stop=(k == KB - 1))
                    ins.then_inc(S["z_ps"], 1)
                pe.wait_ge(S["a_ready"], g + 1 + 1)
                av = small["a"][:, :, :].rearrange("p j h -> p (j h)")
                for r, lhs in enumerate((upto, after, ones)):
                    ins = mm(ps[:, 7, r * TG * NH:(r + 1) * TG * NH], lhs, av, start=True, stop=True)
                ins.then_inc(S["c_ps"], 1)

                def before(j):
                    i = TG * g + j
                    tok = slice(j * P, (j + 1) * P)
                    if j == 0:
                        pe.wait_ge(S["x_act"], XB * g + XB + 1)
                    pe.wait_ge(S["xs_ready"], i + 1)
                    for k in range(IB):
                        ins = pe.transpose(ps[:, 4, k * P:(k + 1) * P], xbc[:, k, tok], ident)
                    ins.then_inc(S["xT_ps"], 1)
                    pe.wait_ge(S["gm_ready"], i + 1)
                    mm(ps[:, 5, P:2 * P], xbc[0:NS, IB, tok], xbc[0:NS, IB + 1, tok], start=True, stop=True)
                    pe.transpose(ps[:, 5, 0:NS], xbc[0:NS, IB, tok], ident[0:NS, 0:NS]).then_inc(S["bg_ps"], 1)
                    pe.wait_ge(S["aU_ready"], i + 1 + 1)
                    pe.wait_ge(S["e_ready"], i + 1)
                    for r in range(2):
                        ins = mm(bank(2 + r), after, aU[:, r * 4:(r + 1) * 4, :].rearrange("p h n -> p (h n)"), start=True, stop=True)
                    ins.then_inc(S["seg_ps"], 1)

                def main(j):
                    s = j % 2
                    i = TG * g + j
                    tok = slice(j * P, (j + 1) * P)
                    if j == 0:
                        pe.wait_ge(S["c_exp"], g + 1 + 1)
                        pe.wait_ge(S["z_act"], TG * g + TG + 1)
                    pe.wait_ge(S["y1_ready"], i + 1)
                    pe.wait_ge(S["state_ready"], i + b + 1 + 1)
                    mm(bank(7), xbc[0:NS, IB + 1, tok], state[0:NS, :], start=True, stop=True).then_inc(S["off_ps"], 1)
                    pe.wait_ge(S["xw_ready"], i + 1 + 1)
                    pe.wait_ge(S["gm_ready"], i + 1 + 1)
                    mm(ps[0:NS, 0, :], bst[s], xw[s], start=True, stop=True).then_inc(S["st_ps"], 1)
                    pe.wait_ge(S["yg_ready"], i + 1)
                    pe.wait_ge(S["w_ready"], i + 1 + 1)
                    for h in range(NH):
                        ins = mm(ps[:, 6, h * HD:(h + 1) * HD], wgt[s][:, h, :], xdt[s][:, h * HD:(h + 1) * HD], start=True, stop=True)
                    ins.then_inc(S["y_ps"], 1)

                before(0)
                for j in range(TG):
                    if j + 1 < TG:
                        before(j + 1)
                    main(j)
                pe.wait_ge(S["yg_ready"], TG * g + TG + 1)
                pe.wait_ge(S["state_ready"], TG * g + TG + b + 1 + 1)
                for j in range(TG):
                    i = TG * g + j
                    if j >= 2:
                        pe.wait_ge(S["h_done"], i - 1 + 1)
                    for k in range(IB):
                        ins = pe.transpose(ps[:, 1 + 6 * (j % 2), k * P:(k + 1) * P], ygat[:, j, k * P:(k + 1) * P], ident)
                    ins.then_inc(S["yT_ps"], 1)
                    pe.wait_ge(S["yT_ready"], i + 1 + 1)
                    for k in range(IB):
                        ins = mm(ps[:, 6 * (j % 2), 0:D], yT[:, k, :], wout[:, k, :], start=(k == 0), stop=(k == IB - 1))
                    ins.then_inc(S["op_ps"], 1)

            pe.wait_ge(mlp_in, 2 * 16)
            pe.wait_ge(S["h_done"], NT + 1)
            with pe.Fori(0, NG) as g:
                turn_group("b_n", "b_nT_ps", g)
                pe.wait_ge(S["b_nT"], KB * g + KB + 1)
                for m in range(FB):
                    pe.wait_ge(S["b_gel"], FB * g + max(m - 3, 0) + 1)
                    for k in range(KB):
                        ins = mm(bank(2 + m % 4), wfc[:, k, m * P:(m + 1) * P], nT[:, k, :], start=(k == 0), stop=(k == KB - 1))
                    ins.then_inc(S["b_up_ps"], 1)
                pe.wait_ge(S["b_gel"], FB * g + FB + 1)
                for j in range(TG):
                    i = TG * g + j
                    pe.wait_ge(S["b_res"], TG * g + max(j - 1, 0) + 1)
                    for m in range(FB):
                        ins = mm(ps[:, 6 + j % 2, 0:D], gT[:, m, j * P:(j + 1) * P], wproj[:, m, :], start=(m == 0), stop=(m == FB - 1))
                    ins.then_inc(S["b_dn_ps"], 1)

            pe.wait_ge(att_in, 8 * 16)
            pe.wait_ge(S["b_nT"], KB * NG + 1)
            for m in range(KB):
                for k in range(KB):
                    ins = mm(ps[:, m, 0:B * S2], wk[:, k, m * P:(m + 1) * P], ctxT[:, k, :], start=(k == 0), stop=(k == KB - 1))
                ins.then_inc(S["k_ps"], 1)
            for kt in range(2):
                for b in range(B):
                    for k in range(KB):
                        c0 = b * S2 + kt * KT
                        ins = mm(ps[0:KT, 2 + kt * B + b, 0:D], ctxT[:, k, c0:c0 + KT], wv[:, k, :], start=(k == 0), stop=(k == KB - 1))
                    ins.then_inc(S["v_ps"], 1)

            def gate_turn(gg, k):
                pe.wait_ge(S["d_n"], gg + 1 + 1)
                if k == 0:
                    pe.wait_ge(S["c_out"], TG * gg + TG + 1)
                else:
                    pe.wait_ge(S["d_nT"], KB * gg + k + 1)
                for j in range(TG):
                    ins = pe.transpose(ps[:, 0, j * P:(j + 1) * P], rowx[:, j, k * P:(k + 1) * P], ident)
                ins.then_inc(S["d_nT_ps"], 1)

            def gate_logits(gg):
                pe.wait_ge(S["d_nT"], KB * gg + KB + 1)
                for j in range(TG):
                    for k in range(KB):
                        ins = mm(ps[:, 0, j * E:(j + 1) * E], nT[:, k, j * P:(j + 1) * P], wg[:, k, :], start=(k == 0), stop=(k == KB - 1))
                ins.then_inc(S["lg_ps"], 1)

            def gate_slots(gg):
                pe.wait_ge(S["sel_ready"], gg + 1 + 1)
                own = sel.rearrange("p j n -> p (j n)")
                prior = csel.rearrange("p j n -> p (j n)")
                mm(ps[:, 0, 0:E], upto, own[:, 0:E], start=True, stop=True)
                mm(ps[:, 0, E:TG * E], upto, own[:, E:], start=True, stop=False)
                mm(ps[:, 0, E:TG * E], ones, prior[:, 0:(TG - 1) * E], start=False, stop=True)
                ins = mm(ps[:, 0, TG * E:(TG + 1) * E], ones, prior[:, (TG - 1) * E:], start=True, stop=True)
                ins.then_inc(S["pos_ps"], 1)

            def att_turn(g, k, gated=None):
                pe.wait_ge(S["c_n"], g + 1 + 1)
                if gated is not None:
                    pe.wait_ge(S["d_lg" if k == 0 else "pos_taken"], gated + 1 + 1)
                elif k == 1:
                    pe.wait_ge(S["c_nT" if g == 0 else "c_out"], 1 + 1)
                for j in range(TG):
                    ins = pe.transpose(ps[:, 0, j * P:(j + 1) * P], nrm[:, j, k * P:(k + 1) * P], ident)
                ins.then_inc(S["c_nT_ps"], 1)

            def att_query(g):
                pe.wait_ge(S["c_nT"], KB * g + KB + 1)
                for m in range(KB):
                    for k in range(KB):
                        ins = mm(bank(2 + m), wq[:, k, m * P:(m + 1) * P], nT[:, k, :], start=(k == 0), stop=(k == KB - 1))
                    ins.then_inc(S["q_ps"], 1)

            def att_scores(g, u):
                s, j, k, q = u % 2, u // 4, u % 4 // 2, u % 2
                if u < 2:
                    pe.wait_ge(S["c_q"], KB * g + KB + 1)
                if not (isinstance(g, int) and u < 2):
                    pe.wait_ge(S["c_sc"], 16 * g + u - 1 + 1)
                for r in range(2):
                    c0 = (4 * q + 2 * r) * S2
                    ins = mm(ps[:, 2 + 2 * s + r, 0:2 * S2], qT[:, k, j * P:(j + 1) * P],
                             kbd[:, k, ds(g // GPB, 1), c0:c0 + 2 * S2].squeeze(1), start=True, stop=True)
                ins.then_inc(S["sc_ps"], 1)

            def att_weights(g, u):
                s = u % 2
                pe.wait_ge(S["p_ready"], 16 * g + u + 1 + 1)
                pe.wait_ge(S["pT_ready"], 16 * g + u + 1)
                for h in range(4):
                    for kt in range(2):
                        w = 2 * h + kt
                        ins = pe.transpose(ps[0:KT, 6 + w // 4, (w % 4) * P:(w % 4 + 1) * P],
                                           pr[s][:, h, kt * KT:(kt + 1) * KT], ident)
                ins.then_inc(S["pT_ps"], 1)

            def att_values(g, u):
                s, j, q = u % 2, u // 4, u % 4
                pe.wait_ge(S["pT_ready"], 16 * g + u + 1 + 1)
                if q == 0:
                    pe.wait_ge(S["cx_ready"], TG * g + j + 1)
                for h in range(4):
                    hh = 4 * q + h
                    for kt in range(2):
                        ins = mm(ps[:, 1, hh * (DK + 1):(hh + 1) * (DK + 1)], pT[s][0:KT, 2 * h + kt, :],
                                 vone[0:KT, kt, ds(g // GPB, 1), hh, :].squeeze(1), start=(kt == 0), stop=(kt == 1))
                ins.then_inc(S["val_ps"], 1) if q < 3 else ins.then_inc(S["ctx_ps"], 1)

            def att_context(g, j, following, gated):
                i = TG * g + j
                if gated is not None and j == 1:
                    pe.wait_ge(S["pos_taken"], gated + 1 + 1)
                if following is not None and j < KB:
                    pe.wait_ge(S["c_nT"], KB * following + j + 1 + 1)
                pe.wait_ge(S["cx_ready"], i + 1 + 1)
                pe.wait_ge(S["c_out"], i + 1)
                for k in range(KB):
                    ins = pe.transpose(ps[:, 0, k * P:(k + 1) * P], cx[:, k * P:(k + 1) * P], ident)
                ins.then_inc(S["cxT_ps"], 1)

            def att_output(g, j):
                i = TG * g + j
                pe.wait_ge(S["cxT_ready"], i + 1 + 1)
                for k in range(KB):
                    ins = mm(ps[:, 0, D:2 * D], cxT[:, k, :], wo[:, k, :], start=(k == 0), stop=(k == KB - 1))
                ins.then_inc(S["co_ps"], 1)

            def att_group(g, following, gated):
                for u in range(16):
                    if u < 14:
                        att_scores(g, u + 2)
                    elif u == 14 and following is not None:
                        pe.wait_ge(S["c_sc"], 16 * g + 14 + 1 + 1)
                        att_query(following)
                    if gated is not None and u == 3:
                        gate_turn(gated, 1)
                    att_weights(g, u)
                    if u > 0:
                        att_values(g, u - 1)
                    if gated is not None:
                        if u == 2:
                            gate_turn(gated, 0)
                        if u == 3:
                            gate_logits(gated)
                        if u == 7:
                            pe.wait_ge(S["c_out"], TG * g + 1 + 1)
                            gate_slots(gated)
                    if following is not None and u == 4:
                        att_turn(following, 0, gated)
                    if following is not None and u == 8:
                        att_turn(following, 1, gated)
                    if u % 4 == 1 and u > 4:
                        att_context(g, u // 4 - 1, following, gated)
                    if u % 4 == 2 and u > 4:
                        att_output(g, u // 4 - 1)
                if following is not None:
                    att_scores(following, 0)
                att_values(g, 15)
                if following is not None:
                    att_scores(following, 1)
                att_context(g, TG - 1, following, gated)
                att_output(g, TG - 1)

            for k in range(KB):
                att_turn(0, k)
            att_query(0)
            pe.wait_ge(S["kv_ready"], 1 + 1)
            for u in range(2):
                att_scores(0, u)
            att_group(0, 1, None)
            with pe.Fori(1, NG - 1) as g:
                att_group(g, pe.snap(g + 1), pe.snap(g - 1))
            att_group(NG - 1, None, NG - 2)
            for k in range(KB):
                gate_turn(NG - 1, k)
            gate_logits(NG - 1)
            pe.wait_ge(S["d_lg"], NG + 1)
            gate_slots(NG - 1)

            def turn_tile(k):
                pe.wait_ge(xt_in, 16 * (k + 1))
                pe.wait_ge(S["xT_ready"], k + 1)
                for m in range(KB):
                    for r in range(SUB):
                        ins = pe.transpose(ps[:, 0, m * TW + r * P:m * TW + (r + 1) * P], xt[:, r, m * P:(m + 1) * P], ident)
                ins.then_inc(S["t_ps"], 1)

            pe.wait_ge(S["tab_ready"], 1 + 1)
            turn_tile(0)
            with pe.Fori(0, E // 2) as ep:
                for s in range(2):
                    e = pe.snap(2 * ep + s)
                    pe.wait_ge(exp_in[s], 4 * 16 * ep + 4 * 16)
                    pe.sem_inc(pe_pad, 1)
                    tiles = pe.value_load(tab[0:1, ds(e, 1)], min_val=1, max_val=NTOK // TW)
                    first = pe.value_load(tab[0:1, ds(E + e, 1)], min_val=0, max_val=60)
                    with pe.Fori(0, tiles) as j:
                        k = pe.snap(first + j)
                        pe.wait_ge(S["xT_ready"], k + 1 + 1)
                        for m in range(HB):
                            pe.wait_ge(S["d_gel"], HB * k + max(m - 3, 0) + 1)
                            for c in range(KB):
                                ins = mm(bank(2 + m % 4, TW), wup[s][:, c, m * P:(m + 1) * P], xT[:, c, :], start=(c == 0), stop=(c == KB - 1))
                            ins.then_inc(S["u_ps"], 1)
                        pe.wait_ge(S["y_ready"], 2 * SUB * k + 1)
                        for r in range(SUB):
                            for m in range(HB):
                                if r == 0:
                                    pe.wait_ge(S["d_gel"], HB * k + m + 1 + 1)
                                if r == 0 and m == HB // 2:
                                    turn_tile(k + 1)
                                ins = mm(ps[:, 6 + r, 0:D], eT[:, m, r * P:(r + 1) * P], wdn[s][:, m, :], start=(m == 0), stop=(m == HB - 1))
                            ins.then_inc(S["dn_ps"], 1)



def kernel(**inputs):
    import numpy as np
    import concourse.bacc as bacc
    from concourse import mybir
    from concourse.bass_utils import run_bass_kernel_spmd as run

    g = {k: np.asarray(v) for k, v in inputs.items()}
    a = {k[len("L0_attn_"):]: v for k, v in g.items() if k.startswith("L0_attn_")}
    xa = {k[len("L0_xattn_"):]: v for k, v in g.items() if k.startswith("L0_xattn_")}
    ff = {k[len("L0_ffn_"):]: v for k, v in g.items() if k.startswith("L0_ffn_")}
    P = 128
    idx = np.arange(P)

    def cols(v):
        return v.reshape(-1, P).T

    def halves(v):
        out = np.zeros((P, v.shape[1]), v.dtype)
        out[:v.shape[0]] = v
        return out

    cw, cb = a["conv_w"], a["conv_b"][:, None]
    blocks_w = [cw[k * P:(k + 1) * P] for k in range(4)] + [halves(cw[512:576]), halves(cw[576:640])]
    blocks_b = [cb[k * P:(k + 1) * P] for k in range(4)] + [halves(cb[512:576]), halves(cb[576:640])]
    arrays = {
        "x": g["x"],
        "consts": np.stack([np.eye(P), idx[:, None] <= idx[None, :], idx[:, None] > idx[None, :],
                            np.ones((P, P))]).astype(np.float32),
        "headmask": (idx[:, None] // 16 == np.arange(8)[None, :]).astype(np.float32),
        "iota12": np.broadcast_to(np.arange(12, dtype=np.float32), (P, 12)),
        "cols": np.concatenate([cols(a["ln1_w"]), cols(a["ln1_b"]), cols(a["ln2_w"]), cols(a["ln2_b"]),
                                cols(a["fc_b"]), cols(xa["bq"]), cols(xa["bk"]), cols(a["norm_w"])]
                               + blocks_w + blocks_b, axis=1),
        "rows": np.concatenate([a["dt_bias"], a["A_log"], np.repeat(a["D_param"], 64), a["proj_b"],
                                xa["bo"], xa["bv"],
                                (np.arange(12)[:, None] > np.arange(12)[None, :]).astype(np.float32).ravel(),
                                (np.arange(12) * (2048 + TW) - 1).astype(np.float32),
                                (np.arange(2048 // TW) * TW).astype(np.float32),
                                np.arange(80, dtype=np.float32)]),
        "tokid": np.arange(17)[None, :].astype(np.float32) * P + idx[:, None].astype(np.float32),
        "in_proj": a["in_proj_w"].T, "out_proj": a["out_proj_w"].T,
        "fc": a["fc_w"].T, "proj": a["proj_w"].T,
        "Wq": xa["Wq"].T, "Wk": xa["Wk"].T, "Wv": xa["Wv"].T, "Wo": xa["Wo"].T,
        "ctxT": g["ctx_1024"].transpose(2, 0, 1),
        "qmask": g["mask_1xSxS2_ik1"], "kmask": g["mask_BxS2_ik1"],
        "Wg": ff["Wg"], "Wup": ff["Wup"], "Wdown": ff["Wdown"], "bdown": ff["bdown"],
        "bup": ff["bup"].reshape(12, 8, P).transpose(0, 2, 1),
    }
    arrays = {k: np.ascontiguousarray(v) for k, v in arrays.items()}
    nc = bacc.Bacc("TRN2", target_bir_lowering=False, num_devices=1)
    t = {k: nc.dram_tensor("in_" + k, v.shape, mybir.dt.from_np(v.dtype), kind="ExternalInput").ap()
         for k, v in arrays.items()}
    t["out"] = nc.dram_tensor("out_x", (2048 + P, 256), mybir.dt.float32, kind="ExternalOutput").ap()
    build(nc, t)
    r = run(nc, [{"in_" + k: v for k, v in arrays.items()}], core_ids=[0])
    return r.results[0]["out_x"][:2048].reshape(2, 1024, 256)
```

```python
TW = 128


def build(nc, t):
    import concourse.bass as bass
    from concourse import mybir
    from concourse.alu_op_type import AluOpType as ALU
    from contextlib import ExitStack, contextmanager

    F32, U32, I32 = mybir.dt.float32, mybir.dt.uint32, mybir.dt.int32
    ACT = mybir.ActivationFunctionType
    AX = mybir.AxisListType.X
    ds = bass.ds

    P = 128
    B, L, D = t["x"].shape
    NT = B * L // P
    TG = 4
    NG = NT // TG
    GPB = NG // B
    GW = TG * P
    KB = D // P
    DI = t["out_proj"].shape[0]
    IB = DI // P
    NH = 8
    HD = DI // NH
    NS = 64
    TAPS = 4
    XB = IB + 2
    F = t["fc"].shape[1]
    FB = F // P
    AH, DK = 16, 16
    S2 = t["ctxT"].shape[2]
    KT = S2 // 2
    E, _, H = t["Wup"].shape
    HB = H // P
    NTOK = B * L
    SUB = TW // P
    ROWS = NTOK + 2 * TW
    MAXT = 3 * NTOK // TW + 2 * E
    MT = MAXT + NTOK // TW + 1
    RW = D + 1 + E
    EPS = 1e-5
    NEG = -3.4028234663852886e38

    with ExitStack() as ctx:
        def sb(name, shape, dt=F32):
            return ctx.enter_context(nc.sbuf_tensor(name, shape, dt))

        def sem(name):
            return ctx.enter_context(nc.semaphore(name))

        ps = ctx.enter_context(nc.psum_tensor("ps", [P, 8, 512], F32))

        X = sb("X", [P, NT, D])
        HR = sb("HR", [P, NT, D])
        consts = sb("consts", [P, 4, P])
        ident, upto, after, ones = (consts[:, i, :] for i in range(4))
        headmask = sb("headmask", [P, 8])
        iota12 = sb("iota12", [P, E])
        tokid = sb("tokid", [P, NT + 1])
        colv = sb("colv", [P, t["cols"].shape[1]])
        rowv = sb("rowv", [P, t["rows"].shape[0]])
        r1 = sb("r1", [P, 4096])
        r2 = sb("r2", [P, 4096])
        EP = t["in_proj"].shape[1]
        win = r1[:, 0:KB * EP].rearrange("p (k e) -> p k e", k=KB)
        wout = r1[:, KB * EP:KB * EP + IB * D].rearrange("p (k d) -> p k d", k=IB)
        wfc = r2[:, 0:2048].rearrange("p (k f) -> p k f", k=KB)
        wproj = r2[:, 2048:4096].rearrange("p (k d) -> p k d", k=FB)
        wup = [r[:, 0:2048].rearrange("p (k f) -> p k f", k=KB) for r in (r1, r2)]
        wdn = [r[:, 2048:4096].rearrange("p (k d) -> p k d", k=HB) for r in (r1, r2)]
        bup = [sb(f"bup{s}", [P, HB]) for s in range(2)]
        wq, wk, wv, wo = (sb(n, [P, KB, D]) for n in ("wq", "wk", "wv", "wo"))
        ctxT = sb("ctxT", [P, KB, B * S2])
        kbd = sb("kbd", [P, KB, B, 8 * S2])
        vone = sb("vone", [P, 2, B, AH, DK + 1])
        qmask_i = sb("qmask_i", [P, L // P, S2], I32)
        qmask = qmask_i[:, :, :].bitcast(F32)
        kmask_i = sb("kmask_i", [P, B, S2], I32)
        kmask = kmask_i[:, :, :].bitcast(F32)
        wg = sb("wg", [P, KB, E])
        bdn = [sb(f"bdn{s}", [P, D]) for s in range(2)]

        CO = {"ln1w": 0, "ln1b": 2, "ln2w": 4, "ln2b": 6, "fcb": 8, "bq": 16, "bk": 18, "normw": 20,
              "convw": 24, "convb": 24 + XB * TAPS}
        RO = {"dtb": 0, "alog": 8, "dpar": 16, "projb": 16 + DI, "bo": 16 + DI + D, "bv": 16 + DI + 2 * D, "tri": 16 + DI + 3 * D,
              "tstart": 16 + DI + 3 * D + E * E}
        slots = nc.dram_tensor("slots", [E * ROWS, RW], F32, kind="Internal").ap()

        def col(name, i):
            return colv[:, CO[name] + i:CO[name] + i + 1]

        st = sb("st", [P, NT, 6])
        mean = sb("mean", [P, NT])
        var = sb("var", [P, NT])
        std = sb("std", [P, NT])
        rstd = sb("rstd", [P, NT])
        la = sb("la", [P, NT])
        lb = sb("lb", [P, NT])
        lc = sb("lc", [P, NT])
        nrm = sb("nrm", [P, TG, D])
        nT = sb("nT", [P, KB, GW])

        reg = sb("reg", [P, XB * (GW + 3) + XB * GW + TG * DI])
        o1 = XB * (GW + 3)
        o2 = o1 + XB * GW
        pre = reg[:, 0:o1].rearrange("p (k n) -> p k n", k=XB)
        xbc = reg[:, o1:o2].rearrange("p (k n) -> p k n", k=XB)
        zs = reg[:, o2:o2 + TG * DI].rearrange("p (k n) -> p k n", k=TG)
        gT = reg[:, 0:FB * GW].rearrange("p (k n) -> p k n", k=FB)

        SCR = 11136
        scr = sb("scr", [P, SCR])
        at = [0]

        def cut(n):
            at[0] += n
            assert at[0] <= SCR, at
            return scr[:, at[0] - n:at[0]]

        xs = [cut(DI) for _ in range(2)]
        xdt = [cut(DI) for _ in range(2)]
        xw = [cut(DI) for _ in range(2)]
        xsD = [cut(DI) for _ in range(2)]
        bst = [cut(NS) for _ in range(2)]
        gm = [cut(P) for _ in range(2)]
        wgt = [cut(NH * P).rearrange("p (h n) -> p h n", h=NH) for _ in range(2)]
        aU = [cut(NH * P).rearrange("p (h n) -> p h n", h=NH) for _ in range(2)]
        state = cut(DI)
        sdec = cut(DI)
        y1 = cut(DI)
        ygat = [cut(DI) for _ in range(2)]
        at[0] = 0
        qT = cut(KB * GW).rearrange("p (k n) -> p k n", k=KB)
        sc = [cut(4 * S2).rearrange("p (h n) -> p h n", h=4) for _ in range(2)]
        pr = [cut(4 * S2).rearrange("p (h n) -> p h n", h=4) for _ in range(2)]
        pT = [cut(8 * P).rearrange("p (h n) -> p h n", h=8) for _ in range(2)]
        cx = cut(D)
        cxT = cut(KB * P).rearrange("p (k n) -> p k n", k=KB)
        yT = sb("yT", [P, IB, P])
        sq = sb("sq", [P, DI])
        warm = sb("warm", [P, 1])
        mk = sb("mk", [P, S2])
        small = {n: sb("s_" + n, [P, TG, NH]) for n in
                 ("raw", "abs", "e", "w", "lw", "wm", "eq", "den", "q", "dt", "a")}
        aneg = sb("aneg", [P, NH])
        cexp = sb("cexp", [P, 3, TG, NH])
        ss = sb("ss", [P, TG])
        sv = sb("sv", [P, TG])
        sstd = sb("sstd", [P, TG])
        srs = sb("srs", [P, TG])
        smx = [sb(f"smx{i}", [P, 4]) for i in range(2)]
        rsum = sb("rsum", [P, AH])
        kTs = [cut(B * S2) for _ in range(KB)]
        gst = cut(TG * 6).rearrange("p (j n) -> p j n", j=TG)
        gmean, gvar, gstd, grstd = (cut(TG) for _ in range(4))
        rowx = cut(TG * RW).rearrange("p (j n) -> p j n", j=TG)
        padrow = cut(RW)
        lg = cut(TG * E).rearrange("p (j n) -> p j n", j=TG)
        top = cut(TG * 8).rearrange("p (j n) -> p j n", j=TG)
        tix = cut(TG * 8).rearrange("p (j n) -> p j n", j=TG).bitcast(U32)
        tixf = cut(TG * 8).rearrange("p (j n) -> p j n", j=TG)
        tsh = cut(TG * 3).rearrange("p (j n) -> p j n", j=TG)
        tex = cut(TG * 3).rearrange("p (j n) -> p j n", j=TG)
        tsum = cut(TG)
        trs = cut(TG)
        tw = cut(TG * 3).rearrange("p (j n) -> p j n", j=TG)
        oh = cut(TG * 3 * E).rearrange("p (j k n) -> p j k n", j=TG, k=3)
        pick = cut(TG * 3 * E).rearrange("p (j k n) -> p j k n", j=TG, k=3)
        sel = cut(TG * E).rearrange("p (j n) -> p j n", j=TG)
        csel = cut(TG * E).rearrange("p (j n) -> p j n", j=TG)
        pos = cut(TG * E).rearrange("p (j n) -> p j n", j=TG)
        posf = cut(TG * 3).rearrange("p (j n) -> p j n", j=TG)
        posk = cut(TG * 3).bitcast(U32)
        run = cut(E)
        cnt = cut(E)
        cwork = cut(E * max(E, NTOK // TW))
        tabf = cut(2 * E + 1)
        tab = cut(2 * E + 1).bitcast(I32)
        tabc = cut(E).bitcast(I32)
        tilef = cut(MT)
        tiletab = cut(MT).bitcast(I32)
        tstep = cut(E)
        tcmp = cut(MT * E).rearrange("p (k e) -> p k e", k=MT)
        tk = cut(MT)
        xt = cut(SUB * RW).rearrange("p (j n) -> p j n", j=SUB)
        xT = cut(KB * TW).rearrange("p (k n) -> p k n", k=KB)
        meta = cut(SUB * (1 + E)).rearrange("p (j n) -> p j n", j=SUB)
        ysc = cut(SUB * D).rearrange("p (j n) -> p j n", j=SUB)
        ytok = cut(SUB).bitcast(U32)
        eT = gT[:, :, 0:TW]

        x_in = [sem(f"x_in{g}") for g in range(NG)]
        prm_in, mlp_in, att_in = (sem(n) for n in ("prm_in", "mlp_in", "att_in"))
        exp_in = [sem(f"exp_in{s}") for s in range(2)]
        acc_in, rows_out, pad_out, xt_in, acc_out = (sem(n) for n in ("acc_in", "rows_out", "pad_out", "xt_in", "acc_out"))
        dve_step = sem("dve_step")
        dve_pad, pool_pad, act_pad, pe_pad, sp_pad = (sem(n) for n in ("dve_pad", "pool_pad", "act_pad", "pe_pad", "sp_pad"))
        dve_names = ("ln_var n_ready nT_ready dt_abs dt_w a_ready conv_done xdt_ready gm_ready w_ready y1_ready "
                     "state_ready yg_ready rms_var h_done "
                     "b_var b_n b_nT b_res "
                     "k_flat v_flat kv_ready c_var c_n c_nT c_q c_sc cx_ready c_out c_max "
                     "d_var d_n d_nT d_lg d_shift sel_ready pos_taken pos_ready cw_ready cnt_ready tab_ready xT_ready meta_ready y_sum y_ready aneg_in").split()
        pe_names = ("nT_ps dt_ps x_ps z_ps c_ps xT_ps bg_ps seg_ps off_ps st_ps y_ps yT_ps op_ps "
                    "b_nT_ps b_up_ps b_dn_ps k_ps v_ps c_nT_ps q_ps sc_ps pT_ps val_ps ctx_ps cxT_ps co_ps "
                    "d_nT_ps lg_ps pos_ps t_ps u_ps dn_ps").split()
        act_names = ("op_ready ln_std dt_e dt_lw x_ev x_act z_act c_exp xs_ready e_ready ss_ready rms_std yT_ready "
                     "b_std b_gel c_std p_ready pT_ready cxT_ready d_ln d_std d_exp d_gel aneg_exp").split()
        pool_names = "wout_ready aU_ready xsD_ready xw_ready sdec_ready b_x c_sub rows_gone y_gone".split()
        S = {n: sem(n) for n in dve_names + pe_names + act_names + pool_names}

        def bank(i, n=512):
            return ps[:, i, 0:n]

        def heads(ap):
            return ap.rearrange("p (h n) -> p h n", h=NH)

        def over(ap, n):
            return ap.unsqueeze(2).to_broadcast([ap.shape[0], ap.shape[1], n])

        @contextmanager
        def batch_groups(eng):
            with eng.Fori(0, B) as b:
                with eng.Fori(0, GPB) as gi:
                    yield b, gi, eng.snap(b * GPB + gi)

        def pad_experts(eng, first):
            eng.wait_ge(S["cnt_ready"], 1 + 1)
            with eng.Fori(first, first + E // 2) as e:
                used = eng.value_load(tabc[0:1, ds(e, 1)], min_val=0, max_val=NTOK)
                eng.dma_start(slots[ds(e * ROWS + used, 2 * TW), :].rearrange("(r p) n -> p r n", p=P),
                              padrow.unsqueeze(1).to_broadcast([P, 2 * SUB, RW])).then_inc(pad_out, 16)

        def tap(k, w):
            pp = P if k < IB else NS
            return colv[0:pp, CO["convw"] + k * TAPS + w:CO["convw"] + k * TAPS + w + 1]

        def load_expert(eng, e, s):
            for dst, src in ((wup[s], t["Wup"].rearrange("e (k p) f -> e p k f", p=P)),
                             (wdn[s], t["Wdown"].rearrange("e (k p) d -> e p k d", p=P)),
                             (bup[s][:, :], t["bup"])):
                eng.dma_start(dst, src[ds(e, 1)].squeeze(0)).then_inc(exp_in[s], 16)
            eng.dma_start(bdn[s][:, :], t["bdown"][ds(e, 1)].squeeze(0).partition_broadcast(P)).then_inc(exp_in[s], 16)

        block = ctx.enter_context(nc.Block())

        @block.sync
        def _(sp):
            xv = t["x"].rearrange("b (t p) d -> p (b t) d", p=P)
            for g in range(NG):
                sp.dma_start(X[:, g * TG:(g + 1) * TG, :], xv[:, g * TG:(g + 1) * TG, :]).then_inc(x_in[g], 16)
            prm = [(consts[:, :, :], t["consts"].rearrange("c p n -> p c n")),
                   (headmask[:, :], t["headmask"]), (iota12[:, :], t["iota12"]), (tokid[:, :], t["tokid"]),
                   (colv[:, :], t["cols"]), (rowv[:, :], t["rows"].partition_broadcast(P)),
                   (win, t["in_proj"].rearrange("(k p) e -> p k e", p=P)),
                   (wout, t["out_proj"].rearrange("(k p) d -> p k d", p=P))]
            for dst, src in prm:
                sp.dma_start(dst, src).then_inc(prm_in, 16)
            assert len(prm) == 8
            sp.dma_start(wfc, t["fc"].rearrange("(k p) f -> p k f", p=P)).then_inc(mlp_in, 16)
            sp.dma_start(wproj, t["proj"].rearrange("(k p) d -> p k d", p=P)).then_inc(mlp_in, 16)
            att = [(w[:, :, :], t[n].rearrange("(k p) d -> p k d", p=P)) for w, n in
                   ((wq, "Wq"), (wk, "Wk"), (wv, "Wv"), (wo, "Wo"), (wg, "Wg"))]
            att += [(ctxT[:, :, :], t["ctxT"].rearrange("(k p) b s -> p k (b s)", p=P)),
                    (qmask_i[:, :, :], t["qmask"].rearrange("o (t p) s -> p (o t) s", p=P)),
                    (kmask_i[:, :, :], t["kmask"].partition_broadcast(P))]
            for dst, src in att:
                sp.dma_start(dst, src).then_inc(att_in, 16)
            assert len(att) == 8
            sp.wait_ge(S["h_done"], NT + 1)
            sp.wait_ge(S["b_dn_ps"], NT + 1)
            load_expert(sp, 0, 0)
            acc = t["out"].rearrange("(t p) d -> p t d", p=P)
            with sp.Fori(0, NG) as g:
                sp.wait_ge(S["c_out"], TG * g + TG + 1)
                sp.dma_start(acc[:, ds(TG * g, TG), :], X[:, ds(TG * g, TG), :]).then_inc(acc_in, 16)
            sp.dma_start(t["out"][NTOK:NTOK + P, :], padrow[:, 0:D]).then_inc(acc_in, 16)
            pad_experts(sp, 0)
            sp.wait_ge(S["tab_ready"], 1 + 1)
            sp.wait_ge(rows_out, NT * 3 * 16)
            sp.wait_ge(pad_out, E * 16)

            def read_tile(k):
                at_row = sp.value_load(tiletab[0:1, ds(k, 1)], min_val=0, max_val=E * ROWS - TW)
                sp.wait_ge(S["t_ps"], k + 1)
                sp.wait_ge(S["meta_ready"], k + 1)
                sp.sem_inc(sp_pad, 1)
                sp.dma_start(xt, slots[ds(at_row, TW), :].rearrange("(r p) n -> p r n", p=P)).then_inc(xt_in, 16)

            def feed(e, s, another):
                first = sp.value_load(tab[0:1, ds(E + e, 1)], min_val=0, max_val=MAXT)
                tiles = sp.value_load(tab[0:1, ds(e, 1)], min_val=2, max_val=NTOK // TW)
                read_tile(first + 1)
                if another:
                    sp.wait_ge(S["dn_ps"], first * SUB + 1)
                    sp.sem_inc(sp_pad, 1)
                    load_expert(sp, e + 1, 1 - s)
                with sp.Fori(1, tiles) as j:
                    read_tile(sp.snap(first + j) + 1)

            read_tile(0)
            with sp.Fori(0, E // 2 - 1) as ep:
                for s in range(2):
                    feed(sp.snap(2 * ep + s), s, True)
            for s in range(2):
                feed(E - 2 + s, s, s == 0)

        @block.vector
        def _(dve):
            n = [0]

            def c(ins):
                n[0] += 1
                ins.then_inc(dve_step, 1)

            def f():
                dve.wait_ge(dve_step, n[0])

            def restart():
                if n[0]:
                    f()
                dve.sem_clear(dve_step)
                n[0] = 0

            TT, TS, STT = dve.tensor_tensor, dve.tensor_scalar, dve.scalar_tensor_tensor

            def moments(a, m, st=st, mean=mean, var=var):
                s = slice(a, a + m)
                c(TT(la[:, s], st[:, s, 1], st[:, s, 4], ALU.add))
                c(TT(lb[:, s], st[:, s, 1], st[:, s, 4], ALU.subtract))
                c(TT(lc[:, s], st[:, s, 2], st[:, s, 5], ALU.add))
                f()
                c(TS(mean[:, s], la[:, s], 0.5, None, ALU.mult))
                c(STT(var[:, s], lb[:, s], 0.25, lb[:, s], ALU.mult, ALU.mult))
                c(TS(lc[:, s], lc[:, s], 1.0 / D, EPS, ALU.mult, ALU.add))
                f()
                return TT(var[:, s], lc[:, s], var[:, s], ALU.add)

            for name in dve_names:
                dve.sem_inc(S[name], 1)
            restart()
            for i in range(NT):
                if i % TG == 0:
                    dve.wait_ge(x_in[i // TG], 16)
                c(dve.bn_stats(st[:, i, :], X[:, i, :]))
            f()
            moments(0, NT).then_inc(S["ln_var"], 1)
            dve.wait_ge(S["ln_std"], 1 + 1)
            c(dve.reciprocal(rstd[:, :], std[:, :]))
            restart()
            for i in range(NT):
                c(TS(HR[:, i, :], X[:, i, :], mean[:, i:i + 1], rstd[:, i:i + 1], ALU.subtract, ALU.mult))
            f()
            for i in range(NT):
                c(dve.bn_stats(st[:, i, :], HR[:, i, :]))
            f()
            moments(0, NT).then_inc(S["ln_var"], 1)
            dve.wait_ge(prm_in, 8 * 16)
            TS(aneg[:, :], rowv[:, RO["alog"]:RO["alog"] + NH], 80.0, None, ALU.min).then_inc(S["aneg_in"], 1)
            dve.wait_ge(S["ln_std"], 2 + 1)
            c(dve.reciprocal(rstd[:, :], std[:, :]))
            dve.wait_ge(S["aneg_exp"], 1 + 1)
            c(TS(aneg[:, :], aneg[:, :], -1.0, None, ALU.mult))
            restart()

            sm = {k: v[:, :, :] for k, v in small.items()}
            with dve.Fori(0, B) as b:
                dve.memset(state[0:NS, :], 0.0).then_inc(S["state_ready"], 1)
                dve.memset(pre[:, :, 0:TAPS - 1], 0.0).then_inc(dve_step, 1)
                dve.wait_ge(dve_step, 1)
                dve.sem_clear(dve_step)
                with dve.Fori(0, GPB) as gi:
                    g = dve.snap(b * GPB + gi)
                    dve.wait_ge(S["nT_ps"], KB * g + 1)
                    dve.wait_ge(S["h_done"], TG * g + 1)
                    dve.sem_inc(dve_pad, 1)
                    for j in range(TG):
                        i = TG * g + j
                        ins = TS(nrm[:, j, :], HR[:, ds(i, 1), :].squeeze(1), mean[:, ds(i, 1)], rstd[:, ds(i, 1)],
                                 ALU.subtract, ALU.mult)
                        c(ins) if j < TG - 1 else ins.then_inc(S["n_ready"], 1)
                    for k in range(KB):
                        dve.wait_ge(S["nT_ps"], KB * g + k + 1 + 1)
                        TS(nT[:, k, :], bank(k), col("ln1w", k), col("ln1b", k), ALU.mult, ALU.add).then_inc(S["nT_ready"], 1)
                    def convolve(blocks):
                        for k in blocks:
                            dve.wait_ge(S["x_ev"], XB * g + k + 1 + 1)
                        for w in range(TAPS - 1):
                            for k in blocks:
                                pp = P if k < IB else NS
                                ins = STT(xbc[0:pp, k, :], pre[0:pp, k, w:w + GW], tap(k, w), xbc[0:pp, k, :], ALU.mult, ALU.add)
                                c(ins) if w < TAPS - 2 else ins.then_inc(S["conv_done"], 1)
                            f()

                    dve.wait_ge(S["dt_ps"], g + 1 + 1)
                    c(TT(sm["raw"], bank(7, TG * NH).rearrange("p (j h) -> p j h", j=TG),
                         rowv[:, RO["dtb"]:RO["dtb"] + NH].unsqueeze(1).to_broadcast([P, TG, NH]), ALU.add))
                    f()
                    STT(sm["abs"], sm["raw"], -1.0, sm["raw"], ALU.mult, ALU.max).then_inc(S["dt_abs"], 1)
                    dve.wait_ge(S["dt_e"], g + 1 + 1)
                    TS(sm["w"], sm["e"], 1.0, None, ALU.add).then_inc(S["dt_w"], 1)
                    dve.wait_ge(S["dt_w"], g + 1 + 1)
                    c(TS(sm["wm"], sm["w"], -1.0, None, ALU.add))
                    f()
                    c(TS(sm["eq"], sm["wm"], 0.0, None, ALU.is_equal))
                    f()
                    c(TT(sm["den"], sm["wm"], sm["eq"], ALU.add))
                    f()
                    c(dve.reciprocal(sm["q"], sm["den"]))
                    f()
                    c(TT(sm["q"], sm["q"], sm["e"], ALU.mult))
                    c(TT(sm["eq"], sm["eq"], sm["e"], ALU.mult))
                    f()
                    convolve((0,))
                    convolve((1,))
                    dve.wait_ge(S["dt_lw"], g + 1 + 1)
                    c(TT(sm["q"], sm["q"], sm["lw"], ALU.mult))
                    f()
                    c(TT(sm["q"], sm["q"], sm["eq"], ALU.add))
                    f()
                    c(STT(sm["dt"], sm["raw"], 0.0, sm["q"], ALU.max, ALU.add))
                    f()
                    c(TT(sm["a"], sm["dt"], aneg[:, :].unsqueeze(1).to_broadcast([P, TG, NH]), ALU.mult))
                    f()
                    TS(sm["a"], sm["a"], -104.0, None, ALU.max).then_inc(S["a_ready"], 1)
                    convolve((2, 3))
                    convolve((4, 5))
                    dve.wait_ge(S["conv_done"], XB * g + XB + 1)
                    dve.sem_inc(dve_pad, 1)
                    c(dve.tensor_copy(pre[:, 0:IB, 0:TAPS - 1], pre[:, 0:IB, GW:GW + TAPS - 1]))
                    c(dve.tensor_copy(pre[0:NS, IB:XB, 0:TAPS - 1], pre[0:NS, IB:XB, GW:GW + TAPS - 1]))

                    def before(j):
                        s = j % 2
                        i = TG * g + j
                        dve.wait_ge(S["xs_ready"], i + 1 + 1)
                        TT(heads(xdt[s]), heads(xs[s]), over(small["dt"][:, j, :], HD), ALU.mult).then_inc(S["xdt_ready"], 1)
                        dve.wait_ge(S["bg_ps"], i + 1 + 1)
                        c(dve.tensor_copy(bst[s], ps[:, 5, 0:NS]))
                        TT(gm[s], ps[:, 5, P:2 * P], upto, ALU.mult).then_inc(S["gm_ready"], 1)

                    def weights(j):
                        s = j % 2
                        i = TG * g + j
                        dve.wait_ge(S["gm_ready"], i + 1 + 1)
                        dve.wait_ge(S["e_ready"], i + 1 + 1)
                        TT(wgt[s], wgt[s], gm[s].unsqueeze(1).to_broadcast([P, NH, P]), ALU.mult).then_inc(S["w_ready"], 1)

                    def main(j):
                        s = j % 2
                        i = TG * g + j
                        dve.wait_ge(S["off_ps"], i + 1 + 1)
                        dve.wait_ge(S["yg_ready"], i + 1)
                        TT(heads(y1), heads(bank(7)), over(cexp[:, 0, j, :], HD), ALU.mult).then_inc(S["y1_ready"], 1)
                        if j + 1 < TG:
                            weights(j + 1)
                        dve.wait_ge(S["sdec_ready"], i + 1 + 1)
                        dve.wait_ge(S["st_ps"], i + 1 + 1)
                        TT(state[0:NS, :], sdec[0:NS, :], ps[0:NS, 0, :], ALU.add).then_inc(S["state_ready"], 1)
                        dve.wait_ge(S["xsD_ready"], i + 1 + 1)
                        dve.wait_ge(S["y1_ready"], i + 1 + 1)
                        c(TT(y1, y1, xsD[s], ALU.add))
                        f()
                        dve.wait_ge(S["y_ps"], i + 1 + 1)
                        c(TT(y1, bank(6), y1, ALU.add))
                        f()
                        if j >= 2:
                            dve.wait_ge(S["ss_ready"], i - 1 + 1)
                            dve.wait_ge(S["yT_ps"], i - 1 + 1)
                        TT(ygat[s], y1, zs[:, j, :], ALU.mult).then_inc(S["yg_ready"], 1)

                    dve.wait_ge(S["c_exp"], g + 1 + 1)
                    dve.wait_ge(S["z_act"], TG * g + TG + 1)
                    before(0)
                    weights(0)
                    for j in range(TG):
                        if j + 1 < TG:
                            before(j + 1)
                        main(j)
                    dve.wait_ge(S["ss_ready"], TG * g + TG + 1)
                    TS(sv[:, :], ss[:, :], 1.0 / DI, EPS, ALU.mult, ALU.add).then_inc(S["rms_var"], 1)
                    dve.wait_ge(S["rms_std"], g + 1 + 1)
                    c(dve.reciprocal(srs[:, :], sstd[:, :]))
                    f()
                    for j in range(TG):
                        i = TG * g + j
                        dve.wait_ge(S["op_ready"], i + 1 + 1)
                        hr = HR[:, ds(i, 1), :].squeeze(1)
                        STT(hr, nrm[:, j, :], srs[:, j:j + 1], hr, ALU.mult, ALU.add).then_inc(S["h_done"], 1)
                    restart()

            def att_norm(g, j):
                i = TG * g + j
                dve.wait_ge(S["c_nT_ps"], KB * g + 1)
                ins = TS(nrm[:, j, :], X[:, ds(i, 1), :].squeeze(1), mean[:, ds(i, 1)], rstd[:, ds(i, 1)],
                         ALU.subtract, ALU.mult)
                c(ins) if j < TG - 1 else ins.then_inc(S["c_n"], 1)

            def att_turned(g, k):
                dve.wait_ge(S["c_nT_ps"], KB * g + k + 1 + 1)
                dve.tensor_copy(nT[:, k, :], bank(0)).then_inc(S["c_nT"], 1)

            def mlp_norm(g):
                for j in range(TG):
                    c(dve.bn_stats(gst[:, j, :], HR[:, ds(TG * g + j, 1), :].squeeze(1)))
                f()
                moments(0, TG, gst, gmean, gvar).then_inc(S["b_var"], 1)
                dve.wait_ge(S["b_std"], g + 1 + 1)
                c(dve.reciprocal(grstd, gstd))
                f()
                dve.wait_ge(S["b_nT_ps"], KB * g + 1)
                for j in range(TG):
                    ins = TS(nrm[:, j, :], HR[:, ds(TG * g + j, 1), :].squeeze(1), gmean[:, j:j + 1], grstd[:, j:j + 1],
                             ALU.subtract, ALU.mult)
                    c(ins) if j < TG - 1 else ins.then_inc(S["b_n"], 1)

            def mlp_turned(g):
                for k in range(KB):
                    dve.wait_ge(S["b_nT_ps"], KB * g + k + 1 + 1)
                    TS(nT[:, k, :], bank(k), col("ln2w", k), col("ln2b", k), ALU.mult, ALU.add).then_inc(S["b_nT"], 1)

            def mlp_residual(g, j):
                i = TG * g + j
                hr = HR[:, ds(i, 1), :].squeeze(1)
                dve.wait_ge(S["b_dn_ps"], i + 1 + 1)
                c(TT(hr, hr, ps[:, 6 + j % 2, 0:D], ALU.add))
                f()
                TT(hr, hr, rowv[:, RO["projb"]:RO["projb"] + D], ALU.add).then_inc(S["b_res"], 1)

            def block_stats(g):
                dve.wait_ge(S["b_x"], TG * g + TG + 1)
                dve.sem_inc(dve_pad, 1)
                for j in range(TG):
                    i = TG * g + j
                    c(dve.bn_stats(st[:, ds(i, 1), :].squeeze(1), X[:, ds(i, 1), :].squeeze(1)))

            def mlp_group(g, following, done):
                if following is not None:
                    mlp_norm(following)
                if done is not None:
                    block_stats(done)
                if following is None:
                    f()
                    moments(0, NT - TG).then_inc(S["c_var"], 1)
                for j in range(TG):
                    mlp_residual(g, j)
                    if j == 1 and following is not None:
                        mlp_turned(following)
                    if j == 1 and following is None:
                        dve.wait_ge(S["c_std"], 1 + 1)
                        c(dve.reciprocal(rstd[:, 0:NT - TG], std[:, 0:NT - TG]))
                        f()
                        dve.wait_ge(S["b_nT_ps"], KB * NG + 1)
                        for jj in range(TG):
                            att_norm(0, jj)
                    if j >= 2 and following is None:
                        att_turned(0, j - 2)
                restart()

            dve.wait_ge(S["h_done"], NT + 1)
            mlp_norm(0)
            dve.wait_ge(att_in, 8 * 16)
            for k in range(KB):
                dve.wait_ge(S["k_ps"], k + 1 + 1)
                TS(kTs[k], ps[:, k, 0:B * S2], col("bk", k), None, ALU.add).then_inc(S["k_flat"], 1)
            mlp_turned(0)
            for kt in range(2):
                for b in range(B):
                    u = kt * B + b
                    dve.wait_ge(S["v_ps"], u + 1 + 1)
                    TT(vone[0:KT, kt, b, :, 0:DK], ps[0:KT, 2 + u, 0:D].rearrange("p (h n) -> p h n", h=AH),
                       rowv[0:KT, RO["bv"]:RO["bv"] + D].rearrange("p (h n) -> p h n", h=AH), ALU.add).then_inc(S["v_flat"], 1)
            c(dve.memset(vone[:, :, :, :, DK:DK + 1], 1.0))
            dve.wait_ge(S["k_flat"], KB + 1)
            for k in range(KB):
                for b in range(B):
                    c(TT(kbd[:, k, b, :].rearrange("p (h s) -> p h s", h=8),
                         kTs[k][:, b * S2:(b + 1) * S2].unsqueeze(1).to_broadcast([P, 8, S2]),
                         over(headmask[:, :], S2), ALU.mult))
            c(TS(qmask, qmask_i[:, :, :], 1, NEG, ALU.is_equal, ALU.mult))
            TS(kmask, kmask_i[:, :, :], 1, NEG, ALU.is_equal, ALU.mult).then_inc(S["kv_ready"], 1)
            restart()
            mlp_group(0, 1, None)
            with dve.Fori(1, NG - 1) as g:
                mlp_group(g, dve.snap(g + 1), dve.snap(g - 1))
            mlp_group(NG - 1, None, NG - 2)

            c(dve.memset(padrow, 0.0))
            f()
            c(dve.tensor_copy(padrow[:, D:D + 1], tokid[:, NT:NT + 1]))
            c(dve.tensor_copy(run, rowv[:, RO["tstart"]:RO["tstart"] + E]))
            f()

            def gate_rows(gg):
                dve.wait_ge(S["d_std"], gg + 1 + 1)
                dve.wait_ge(S["rows_gone"], gg + 1)
                dve.sem_inc(dve_pad, 1)
                c(dve.tensor_copy(rowx[:, :, D], tokid[:, ds(TG * gg, TG)]))
                for j in range(TG):
                    ins = TS(rowx[:, j, 0:D], X[:, ds(TG * gg + j, 1), :].squeeze(1), gmean[:, j:j + 1], grstd[:, j:j + 1],
                             ALU.subtract, ALU.mult)
                    c(ins) if j < TG - 1 else ins.then_inc(S["d_n"], 1)

            def gate_turned(gg, k):
                dve.wait_ge(S["d_nT_ps"], KB * gg + k + 1 + 1)
                dve.sem_inc(dve_pad, 1)
                dve.tensor_copy(nT[:, k, :], bank(0)).then_inc(S["d_nT"], 1)

            def gate_top(gg):
                dve.wait_ge(S["lg_ps"], gg + 1 + 1)
                dve.sem_inc(dve_pad, 1)
                dve.tensor_copy(lg, ps[:, 0, 0:TG * E].rearrange("p (j e) -> p j e", j=TG)).then_inc(S["d_lg"], 1)
                dve.wait_ge(S["d_lg"], gg + 1 + 1)
                dve.sem_inc(dve_pad, 1)
                for j in range(TG):
                    c(dve.max(top[:, j, :], lg[:, j, :]))
                f()
                for j in range(TG):
                    c(dve.max_index(tix[:, j, :], top[:, j, :], lg[:, j, :]))
                TT(tsh, top[:, :, 0:3], top[:, :, 0:1].to_broadcast([P, TG, 3]), ALU.subtract).then_inc(S["d_shift"], 1)
                f()
                c(dve.tensor_copy(tixf, tix))

            def gate_select(gg):
                f()
                c(TT(oh, iota12[:, :].unsqueeze(1).unsqueeze(1).to_broadcast([P, TG, 3, E]),
                     tixf[:, :, 0:3].unsqueeze(3).to_broadcast([P, TG, 3, E]), ALU.is_equal))
                f()
                c(TT(sel, oh[:, :, 0, :], oh[:, :, 1, :], ALU.add))
                f()
                c(TT(sel, sel, oh[:, :, 2, :], ALU.add))
                f()
                c(dve.tensor_copy(csel[:, 0, :], sel[:, 0, :]))
                f()
                for j in range(1, TG):
                    ins = TT(csel[:, j, :], csel[:, j - 1, :], sel[:, j, :], ALU.add)
                    if j < TG - 1:
                        c(ins)
                        f()
                ins.then_inc(S["sel_ready"], 1)

            def gate_weights(gg):
                dve.wait_ge(S["d_exp"], gg + 1 + 1)
                dve.sem_inc(dve_pad, 1)
                c(dve.tensor_reduce(tsum, tex, AX, ALU.add))
                f()
                c(dve.reciprocal(trs, tsum))
                f()
                c(TT(tw, tex, over(trs, 3), ALU.mult))
                f()
                c(TT(pick, oh, tw.unsqueeze(3).to_broadcast([P, TG, 3, E]), ALU.mult))
                f()
                c(TT(pick[:, :, 0, :], pick[:, :, 0, :], pick[:, :, 1, :], ALU.add))
                f()
                TT(rowx[:, :, D + 1:RW], pick[:, :, 0, :], pick[:, :, 2, :], ALU.add).then_inc(S["cw_ready"], 1)

            def gate_slots(gg):
                dve.wait_ge(S["cw_ready"], gg + 1 + 1)
                dve.wait_ge(S["pos_ps"], gg + 1 + 1)
                dve.sem_inc(dve_pad, 1)
                c(TT(pos, ps[:, 0, 0:TG * E].rearrange("p (j e) -> p j e", j=TG),
                     run.unsqueeze(1).to_broadcast([P, TG, E]), ALU.add))
                f()
                TT(run, run, ps[:, 0, TG * E:(TG + 1) * E], ALU.add).then_inc(S["pos_taken"], 1)
                c(TT(pick, oh, pos.unsqueeze(2).to_broadcast([P, TG, 3, E]), ALU.mult))
                f()
                c(dve.tensor_reduce(posf, pick, AX, ALU.add))
                f()
                dve.tensor_copy(posk, posf.rearrange("p j k -> p (j k)")).then_inc(S["pos_ready"], 1)

            def att_query(g):
                for k in range(KB):
                    dve.wait_ge(S["q_ps"], KB * g + k + 1 + 1)
                    TS(qT[:, k, :], bank(2 + k), col("bq", k), 1.0 / DK ** 0.5, ALU.add, ALU.mult).then_inc(S["c_q"], 1)

            def att_scores(g, u):
                s = u % 2
                if u % 4 == 0:
                    c(TT(mk[:, :], qmask[:, ds((g % GPB) * TG + u // 4, 1), :].squeeze(1),
                         kmask[:, ds(g // GPB, 1), :].squeeze(1), ALU.min))
                    f()
                dve.wait_ge(S["sc_ps"], 16 * g + u + 1 + 1)
                if not (first_group(g) and u < 2):
                    dve.wait_ge(S["p_ready"], 16 * g + u - 1 + 1)
                TT(sc[s].rearrange("p (c h) n -> p c h n", c=2),
                   ps[:, 2 + 2 * s:4 + 2 * s, 0:2 * S2].rearrange("p c (h n) -> p c h n", h=2),
                   mk[:, :].unsqueeze(1).unsqueeze(1).to_broadcast([P, 2, 2, S2]), ALU.add).then_inc(S["c_sc"], 1)
                dve.wait_ge(S["c_sc"], 16 * g + u + 1 + 1)
                dve.sem_inc(dve_pad, 1)
                dve.tensor_reduce(smx[s][:, :], sc[s], AX, ALU.max).then_inc(S["c_max"], 1)

            def first_group(g):
                return isinstance(g, int) and g == 0

            def att_normalise(g, j):
                dve.wait_ge(S["ctx_ps"], TG * g + j + 1 + 1)
                dve.sem_inc(dve_pad, 1)
                acc = ps[:, 1, 0:AH * (DK + 1)].rearrange("p (h n) -> p h n", h=AH)
                c(dve.reciprocal(rsum[:, :], acc[:, :, DK]))
                f()
                TT(cx.rearrange("p (h n) -> p h n", h=AH), acc[:, :, 0:DK], over(rsum[:, :], DK), ALU.mult).then_inc(S["cx_ready"], 1)

            def att_output(g, j):
                i = TG * g + j
                xr = X[:, ds(i, 1), :].squeeze(1)
                dve.wait_ge(S["co_ps"], i + 1 + 1)
                c(TT(xr, xr, ps[:, 0, D:2 * D], ALU.add))
                f()
                TT(xr, xr, rowv[:, RO["bo"]:RO["bo"] + D], ALU.add).then_inc(S["c_out"], 1)
                dve.wait_ge(S["c_out"], i + 1 + 1)
                dve.sem_inc(dve_pad, 1)
                c(dve.bn_stats(gst[:, j, :], xr))

            def att_group(g, following, gated):
                for u in range(16):
                    if u % 4 == 1 and u > 4:
                        att_normalise(g, u // 4 - 1)
                    if gated is not None:
                        if u == 3:
                            gate_turned(gated, 0)
                        if u == 4:
                            gate_top(gated)
                        if u == 8:
                            gate_slots(gated)
                    if following is not None:
                        if u == 5:
                            att_turned(following, 0)
                        if u == 9:
                            att_turned(following, 1)
                        if u == 14:
                            att_query(following)
                    if u % 4 == 3 and u > 4:
                        att_output(g, u // 4 - 1)
                    if u < 14:
                        att_scores(g, u + 2)
                    if following is not None and u in (1, 2):
                        att_norm(following, 2 * u - 2)
                        att_norm(following, 2 * u - 1)
                    if gated is not None:
                        if u == 0:
                            gate_rows(gated)
                        if u == 3:
                            gate_turned(gated, 1)
                        if u == 5:
                            gate_select(gated)
                        if u == 6:
                            gate_weights(gated)
                if following is not None:
                    att_scores(following, 0)
                att_normalise(g, TG - 1)
                if following is not None:
                    att_scores(following, 1)
                att_output(g, TG - 1)
                f()
                moments(0, TG, gst, gmean, gvar).then_inc(S["d_var"], 1)
                restart()

            att_query(0)
            for u in range(2):
                att_scores(0, u)
            block_stats(NG - 1)
            f()
            moments(NT - TG, TG).then_inc(S["c_var"], 1)
            dve.wait_ge(S["c_std"], 2 + 1)
            c(dve.reciprocal(rstd[:, NT - TG:], std[:, NT - TG:]))
            restart()
            att_group(0, 1, None)
            with dve.Fori(1, NG - 1) as g:
                att_group(g, dve.snap(g + 1), dve.snap(g - 1))
            att_group(NG - 1, None, NG - 2)
            gate_rows(NG - 1)
            for k in range(KB):
                gate_turned(NG - 1, k)
            gate_top(NG - 1)
            gate_select(NG - 1)
            gate_weights(NG - 1)
            gate_slots(NG - 1)

            dve.wait_ge(S["pos_taken"], NG + 1)
            c(TT(cnt, run, rowv[:, RO["tstart"]:RO["tstart"] + E], ALU.subtract))
            f()
            dve.tensor_copy(tabc, cnt).then_inc(S["cnt_ready"], 1)
            NK = NTOK // TW
            cv = cwork[:, 0:E * NK].rearrange("p (e k) -> p e k", e=E)
            c(TT(cv, over(cnt, NK), rowv[:, RO["tstart"] + E:RO["tstart"] + E + NK].unsqueeze(1).to_broadcast([P, E, NK]), ALU.is_gt))
            f()
            c(dve.tensor_reduce(tabf[:, 0:E], cv, AX, ALU.add))
            f()
            c(TS(tabf[:, 0:E], tabf[:, 0:E], 2.0, None, ALU.max))
            f()
            cv = cwork[:, 0:E * E].rearrange("p (e k) -> p e k", e=E)
            c(TT(cv, tabf[:, 0:E].unsqueeze(1).to_broadcast([P, E, E]),
                 rowv[:, RO["tri"]:RO["tri"] + E * E].rearrange("p (e k) -> p e k", e=E), ALU.mult))
            f()
            c(dve.tensor_reduce(tabf[:, E:2 * E], cv, AX, ALU.add))
            f()
            c(TT(tabf[:, 2 * E:2 * E + 1], tabf[:, E - 1:E], tabf[:, 2 * E - 1:2 * E], ALU.add))
            f()
            c(dve.memset(tstep, 0.0))
            f()
            c(TS(tstep[:, 1:E], tabf[:, 0:E - 1], -float(TW), float(ROWS), ALU.mult, ALU.add))
            c(TS(cwork[:, 0:1], tabf[:, 2 * E:2 * E + 1], -1.0, None, ALU.add))
            f()
            c(TS(tk, rowv[:, RO["tstart"] + E + NK:RO["tstart"] + E + NK + MT], cwork[:, 0:1], None, ALU.min))
            f()
            c(TT(tcmp, over(tk, E), tabf[:, E:2 * E].unsqueeze(1).to_broadcast([P, MT, E]), ALU.is_ge))
            f()
            c(TT(tcmp, tcmp, tstep.unsqueeze(1).to_broadcast([P, MT, E]), ALU.mult))
            f()
            c(dve.tensor_reduce(tilef, tcmp, AX, ALU.add))
            f()
            c(STT(tilef, tk, float(TW), tilef, ALU.mult, ALU.add))
            f()
            c(dve.tensor_copy(tiletab, tilef))
            f()
            dve.tensor_copy(tab, tabf).then_inc(S["tab_ready"], 1)
            dve.wait_ge(S["tab_ready"], 1 + 1)

            def take_rows(k):
                dve.wait_ge(S["t_ps"], k + 1 + 1)
                dve.tensor_copy(xT, ps[:, 0, 0:KB * TW].rearrange("p (k n) -> p k n", k=KB)).then_inc(S["xT_ready"], 1)

            def take_meta(k):
                dve.tensor_copy(meta, xt[:, :, D:RW]).then_inc(S["meta_ready"], 1)

            take_rows(0)
            take_meta(0)
            with dve.Fori(0, E // 2) as ep:
                for s in range(2):
                    e = dve.snap(2 * ep + s)
                    dve.wait_ge(exp_in[s], 4 * 16 * ep + 4 * 16)
                    dve.sem_inc(dve_pad, 1)
                    tiles = dve.value_load(tab[0:1, ds(e, 1)], min_val=2, max_val=NTOK // TW)
                    first = dve.value_load(tab[0:1, ds(E + e, 1)], min_val=0, max_val=MAXT)
                    with dve.Fori(0, tiles) as j:
                        k = dve.snap(first + j)
                        dve.wait_ge(S["u_ps"], HB * k + HB + 1)
                        take_rows(k + 1)
                        for r in range(SUB):
                            dve.wait_ge(S["y_gone"], SUB * k + 1)
                            dve.wait_ge(S["meta_ready"], k + 1 + 1)
                            dve.wait_ge(S["dn_ps"], SUB * k + r + 1 + 1)
                            dve.sem_inc(dve_pad, 1)
                            TT(ysc[:, r, :], ps[:, 6 + r, 0:D], bdn[s][:, :], ALU.add).then_inc(S["y_sum"], 1)
                            dve.tensor_copy(ytok[:, r:r + 1], meta[:, r, 0:1]).then_inc(S["y_ready"], 1)
                            dve.wait_ge(S["y_sum"], SUB * k + r + 1 + 1)
                            TS(ysc[:, r, :], ysc[:, r, :], meta[:, r, ds(e + 1, 1)], None, ALU.mult).then_inc(S["y_ready"], 1)
                        dve.wait_ge(S["y_ready"], 2 * SUB * (k + 1) + 1)
                        dve.sem_inc(dve_pad, 1)
                        take_meta(k + 1)

        @block.scalar
        def _(act):
            A = act.activation
            for name in act_names:
                act.sem_inc(S[name], 1)
            for r in range(2):
                act.wait_ge(S["ln_var"], r + 1 + 1)
                A(std[:, :], var[:, :], ACT.Sqrt).then_inc(S["ln_std"], 1)
            act.wait_ge(S["aneg_in"], 1 + 1)
            A(aneg[:, :], aneg[:, :], ACT.Exp).then_inc(S["aneg_exp"], 1)
            with act.Fori(0, NG) as g:
                act.wait_ge(S["dt_abs"], g + 1 + 1)
                A(small["e"][:, :, :], small["abs"][:, :, :], ACT.Exp, scale=-1.0).then_inc(S["dt_e"], 1)
                act.wait_ge(S["conv_done"], XB * g + 1)
                for k in range(XB):
                    if k == 2:
                        act.wait_ge(S["dt_w"], g + 1 + 1)
                        A(small["lw"][:, :, :], small["w"][:, :, :], ACT.Ln).then_inc(S["dt_lw"], 1)
                    pp = P if k < IB else NS
                    act.wait_ge(S["x_ps"], XB * g + k + 1 + 1)
                    A(xbc[0:pp, k, :], ps[0:pp, k % 4, :], ACT.Copy, scale=tap(k, TAPS - 1))
                    A(pre[0:pp, k, TAPS - 1:TAPS - 1 + GW], ps[0:pp, k % 4, :], ACT.Copy).then_inc(S["x_ev"], 1)

                def gate(j):
                    act.wait_ge(S["z_ps"], TG * g + j + 1 + 1)
                    A(zs[:, j, :], bank(2 + j % 2), ACT.Silu).then_inc(S["z_act"], 1)

                def channels(k):
                    pp = P if k < IB else NS
                    act.wait_ge(S["conv_done"], XB * g + k + 1 + 1)
                    A(xbc[0:pp, k, :], xbc[0:pp, k, :], ACT.Silu,
                      bias=colv[0:pp, CO["convb"] + k:CO["convb"] + k + 1]).then_inc(S["x_act"], 1)

                for j in range(TG):
                    gate(j)
                    if j > 0:
                        channels(j - 1)
                for k in range(TG - 1, XB):
                    channels(k)
                act.wait_ge(S["c_ps"], g + 1 + 1)
                A(cexp[:, :, :, :].rearrange("p a j h -> p (a j h)"), bank(7, 3 * TG * NH), ACT.Exp).then_inc(S["c_exp"], 1)

                def before(j):
                    s = j % 2
                    i = TG * g + j
                    if j >= 2:
                        act.wait_ge(S["xdt_ready"], i - 1 + 1)
                        act.wait_ge(S["xsD_ready"], i - 1 + 1)
                    act.wait_ge(S["xT_ps"], i + 1 + 1)
                    A(xs[s], bank(4), ACT.Copy).then_inc(S["xs_ready"], 1)
                    act.wait_ge(S["seg_ps"], i + 1 + 1)
                    A(wgt[s].rearrange("p (c h) n -> p c (h n)", c=2), ps[:, 2:4, :], ACT.Exp).then_inc(S["e_ready"], 1)

                def squares(j):
                    i = TG * g + j
                    act.wait_ge(S["yg_ready"], i + 1 + 1)
                    act.wait_ge(S["ss_ready"], i + 1)
                    A(sq[:, :], ygat[j % 2], ACT.Square, accum_out=ss[:, j:j + 1]).then_inc(S["ss_ready"], 1)

                def out_turned(j):
                    act.wait_ge(S["yT_ps"], TG * g + j + 1 + 1)
                    A(yT[:, :, :].rearrange("p k n -> p (k n)"), bank(1), ACT.Copy).then_inc(S["yT_ready"], 1)

                def out_kept(j):
                    act.wait_ge(S["op_ps"], TG * g + j + 1 + 1)
                    A(nrm[:, j, :], ps[:, 1, 0:D], ACT.Copy).then_inc(S["op_ready"], 1)

                before(0)
                for j in range(TG):
                    if j + 1 < TG:
                        before(j + 1)
                    if j > 0:
                        squares(j - 1)
                        out_turned(j - 1)
                        out_kept(j - 1)
                squares(TG - 1)
                out_turned(TG - 1)
                act.wait_ge(S["rms_var"], g + 1 + 1)
                A(sstd[:, :], sv[:, :], ACT.Sqrt).then_inc(S["rms_std"], 1)
                out_kept(TG - 1)
            def mlp_std(g):
                act.wait_ge(S["b_var"], g + 1 + 1)
                act.sem_inc(act_pad, 1)
                A(gstd, gvar, ACT.Sqrt).then_inc(S["b_std"], 1)

            def mlp_hidden(g):
                act.wait_ge(S["b_dn_ps"], TG * g + 1)
                for m in range(FB):
                    act.wait_ge(S["b_up_ps"], FB * g + m + 1 + 1)
                    A(gT[:, m, :], bank(2 + m % 4), ACT.Gelu, bias=col("fcb", m)).then_inc(S["b_gel"], 1)

            mlp_std(0)
            with act.Fori(0, NG - 1) as g:
                mlp_hidden(g)
                mlp_std(act.snap(g + 1))
            mlp_hidden(NG - 1)
            act.wait_ge(S["c_var"], 1 + 1)
            A(std[:, 0:NT - TG], var[:, 0:NT - TG], ACT.Sqrt).then_inc(S["c_std"], 1)

            def att_exp(g, u):
                s = u % 2
                act.wait_ge(S["c_sub"], 16 * g + u + 1 + 1)
                act.sem_inc(act_pad, 1)
                A(pr[s], sc[s], ACT.Exp).then_inc(S["p_ready"], 1)

            def gate_std(gg):
                act.wait_ge(S["d_var"], gg + 1 + 1)
                act.sem_inc(act_pad, 1)
                A(gstd, gvar, ACT.Ln).then_inc(S["d_ln"], 1)
                act.wait_ge(S["d_ln"], gg + 1 + 1)
                act.sem_inc(act_pad, 1)
                A(grstd, gstd, ACT.Exp, scale=-0.5).then_inc(S["d_std"], 1)

            def gate_exp(gg):
                act.wait_ge(S["d_shift"], gg + 1 + 1)
                act.sem_inc(act_pad, 1)
                A(tex[:, :, :], tsh[:, :, :], ACT.Exp).then_inc(S["d_exp"], 1)

            def att_group(g, following, gated):
                for u in range(16):
                    act.wait_ge(S["pT_ps"], 16 * g + u + 1 + 1)
                    A(pT[u % 2][0:KT, :, :].rearrange("p (c h) n -> p c (h n)", c=2), ps[0:KT, 6:8, :], ACT.Copy).then_inc(S["pT_ready"], 1)
                    if u % 4 == 1 and u > 4:
                        att_turn(g, u // 4 - 1)
                    if u == 0 and gated is not None:
                        gate_std(gated)
                    if u < 14:
                        att_exp(g, u + 2)
                    if u == 4 and gated is not None:
                        gate_exp(gated)
                att_turn(g, TG - 1)
                if following is not None:
                    for u in range(2):
                        att_exp(following, u)

            def att_turn(g, j):
                act.wait_ge(S["cxT_ps"], TG * g + j + 1 + 1)
                A(cxT.rearrange("p k n -> p (k n)"), ps[:, 0, 0:D], ACT.Copy).then_inc(S["cxT_ready"], 1)

            for u in range(2):
                att_exp(0, u)
            act.wait_ge(S["c_var"], 2 + 1)
            A(std[:, NT - TG:], var[:, NT - TG:], ACT.Sqrt).then_inc(S["c_std"], 1)
            att_group(0, 1, None)
            with act.Fori(1, NG - 1) as g:
                att_group(g, act.snap(g + 1), act.snap(g - 1))
            att_group(NG - 1, None, NG - 2)
            gate_std(NG - 1)
            gate_exp(NG - 1)
            pad_experts(act, E // 2)
            act.wait_ge(S["tab_ready"], 1 + 1)

            def hidden(e, s, ep):
                first = act.value_load(tab[0:1, ds(E + e, 1)], min_val=0, max_val=MAXT)
                tiles = act.value_load(tab[0:1, ds(e, 1)], min_val=2, max_val=NTOK // TW)
                act.wait_ge(exp_in[s], 4 * 16 * ep + 4 * 16)
                act.sem_inc(act_pad, 1)
                if s == 0:
                    A(warm[:, :], bup[s][:, 0:1], ACT.Gelu)
                with act.Fori(0, tiles) as j:
                    k = act.snap(first + j)
                    act.wait_ge(S["dn_ps"], SUB * k + 1)
                    for m in range(HB):
                        act.wait_ge(S["u_ps"], HB * k + m + 1 + 1)
                        A(eT[:, m, :], bank(2 + m % 4, TW), ACT.Gelu, bias=bup[s][:, m:m + 1]).then_inc(S["d_gel"], 1)

            with act.Fori(0, E // 2) as ep:
                for s in range(2):
                    hidden(act.snap(2 * ep + s), s, ep)

        @block.gpsimd
        def _(pool):
            TT = pool.tensor_tensor
            for name in pool_names:
                pool.sem_inc(S[name], 1)
            pool.wait_ge(prm_in, 8 * 16)
            for k in range(IB):
                TT(wout[:, k, :], wout[:, k, :], col("normw", k).to_broadcast([P, D]), ALU.mult).then_inc(S["wout_ready"], 1)
            with batch_groups(pool) as (b, _, g):
                def log_decays(j):
                    if j > 1:
                        pool.wait_ge(S["seg_ps"], TG * g + j - 1 + 1)
                    TT(aU[j % 2], upto.unsqueeze(1).to_broadcast([P, NH, P]), over(small["a"][:, j, :], P), ALU.mult).then_inc(S["aU_ready"], 1)

                def weighted(j):
                    s = j % 2
                    if j == 0:
                        pool.wait_ge(S["c_exp"], g + 1 + 1)
                    pool.wait_ge(S["xdt_ready"], TG * g + j + 1 + 1)
                    TT(heads(xw[s]), heads(xdt[s]), over(cexp[:, 1, j, :], HD), ALU.mult).then_inc(S["xw_ready"], 1)

                def skipped(j):
                    s = j % 2
                    pool.wait_ge(S["xs_ready"], TG * g + j + 1 + 1)
                    TT(xsD[s], xs[s], rowv[:, RO["dpar"]:RO["dpar"] + DI], ALU.mult).then_inc(S["xsD_ready"], 1)

                def decayed(j):
                    pool.wait_ge(S["state_ready"], TG * g + j + b + 1 + 1)
                    TT(heads(sdec[0:NS, :]), heads(state[0:NS, :]), over(cexp[0:NS, 2, j, :], HD), ALU.mult).then_inc(S["sdec_ready"], 1)

                pool.wait_ge(S["a_ready"], g + 1 + 1)
                log_decays(0)
                log_decays(1)
                weighted(0)
                skipped(0)
                for j in range(TG):
                    if j + 1 < TG:
                        weighted(j + 1)
                    if j + 2 < TG:
                        log_decays(j + 2)
                    decayed(j)
                    if j + 1 < TG:
                        skipped(j + 1)
            with pool.Fori(0, NT) as i:
                pool.wait_ge(S["b_res"], i + 1 + 1)
                pool.sem_inc(pool_pad, 1)
                xr = X[:, ds(i, 1), :].squeeze(1)
                TT(xr, xr, HR[:, ds(i, 1), :].squeeze(1), ALU.add).then_inc(S["b_x"], 1)
            pool.wait_ge(S["kv_ready"], 1 + 1)

            def att_shift(g, u):
                s = u % 2
                pool.wait_ge(S["c_max"], 16 * g + u + 1 + 1)
                TT(sc[s], sc[s], over(smx[s][:, :], S2), ALU.subtract).then_inc(S["c_sub"], 1)

            def scatter(j, r):
                pool.indirect_dma_start(slots, bass.IndirectOffsetOnAxis(ap=posk[:, 3 * j + r:3 * j + r + 1], axis=0),
                                        rowx[:, j, :], None).then_inc(rows_out, 16)

            def scattered(gg):
                pool.wait_ge(rows_out, 3 * TG * 16 * gg + 3 * TG * 16)
                pool.sem_inc(S["rows_gone"], 1)

            def att_group(g, following, gated):
                for u in range(2, 16):
                    att_shift(g, u)
                    if gated is not None and u >= 10:
                        if u == 10:
                            pool.wait_ge(S["pos_ready"], gated + 1 + 1)
                            pool.sem_inc(pool_pad, 1)
                        for n in (2 * (u - 10), 2 * (u - 10) + 1):
                            scatter(n // 3, n % 3)
                if following is not None:
                    for u in range(2):
                        att_shift(following, u)
                if gated is not None:
                    scattered(gated)

            for u in range(2):
                att_shift(0, u)
            att_group(0, 1, None)
            with pool.Fori(1, NG - 1) as g:
                att_group(g, pool.snap(g + 1), pool.snap(g - 1))
            att_group(NG - 1, None, NG - 2)
            pool.wait_ge(S["pos_ready"], NG + 1)
            for n in range(3 * TG):
                scatter(n // 3, n % 3)
            pool.wait_ge(acc_in, 16 * (NG + 1))
            pool.wait_ge(S["tab_ready"], 1 + 1)
            with pool.Fori(0, E) as e:
                tiles = pool.value_load(tab[0:1, ds(e, 1)], min_val=2, max_val=NTOK // TW)
                first = pool.value_load(tab[0:1, ds(E + e, 1)], min_val=0, max_val=MAXT)
                with pool.Fori(0, tiles) as j:
                    k = pool.snap(first + j)
                    for r in range(SUB):
                        pool.wait_ge(S["y_ready"], 2 * (SUB * k + r + 1) + 1)
                        pool.sem_inc(pool_pad, 1)
                        pool.indirect_dma_start(t["out"], bass.IndirectOffsetOnAxis(ap=ytok[:, r:r + 1], axis=0),
                                                ysc[:, r, :], None, compute_op=ALU.add).then_inc(acc_out, 16)
                        pool.wait_ge(acc_out, 16 * (SUB * k + r + 1))
                        pool.sem_inc(S["y_gone"], 1)

        @block.tensor
        def _(pe):
            mm = pe.matmul
            for name in pe_names:
                pe.sem_inc(S[name], 1)
            pe.wait_ge(prm_in, 8 * 16)

            def turn_group(ready, done, g, src=nrm):
                pe.wait_ge(S[ready], g + 1 + 1)
                for k in range(KB):
                    for j in range(TG):
                        ins = pe.transpose(ps[:, k, j * P:(j + 1) * P], src[:, j, k * P:(k + 1) * P], ident)
                    ins.then_inc(S[done], 1)

            pe.wait_ge(S["wout_ready"], IB + 1)
            with batch_groups(pe) as (b, _, g):
                pe.wait_ge(S["h_done"], TG * g + 1)
                turn_group("n_ready", "nT_ps", g)
                pe.wait_ge(S["nT_ready"], KB * g + KB + 1)
                for j in range(TG):
                    for k in range(KB):
                        ins = mm(ps[:, 7, j * NH:(j + 1) * NH], nT[:, k, j * P:(j + 1) * P], win[:, k, EP - NH:EP],
                                 start=(k == 0), stop=(k == KB - 1))
                ins.then_inc(S["dt_ps"], 1)
                for m in range(XB):
                    if m == 2:
                        pe.wait_ge(S["e_ready"], TG * g + 1)
                    c0 = DI + (m * P if m < IB else DI + (m - IB) * NS)
                    w = P if m < IB else NS
                    if m >= 4:
                        pe.wait_ge(S["x_ev"], XB * g + m - 3 + 1)
                    for k in range(KB):
                        ins = mm(ps[0:w, m % 4, :], win[:, k, c0:c0 + w], nT[:, k, :], start=(k == 0), stop=(k == KB - 1))
                    ins.then_inc(S["x_ps"], 1)
                for j in range(TG):
                    if j < 2:
                        pe.wait_ge(S["x_ev"], XB * g + 3 + j + 1)
                    else:
                        pe.wait_ge(S["z_act"], TG * g + j - 1 + 1)
                    for k in range(KB):
                        ins = mm(bank(2 + j % 2), nT[:, k, j * P:(j + 1) * P], win[:, k, 0:DI], start=(k == 0), stop=(k == KB - 1))
                    ins.then_inc(S["z_ps"], 1)
                pe.wait_ge(S["a_ready"], g + 1 + 1)
                av = small["a"][:, :, :].rearrange("p j h -> p (j h)")
                for r, lhs in enumerate((upto, after, ones)):
                    ins = mm(ps[:, 7, r * TG * NH:(r + 1) * TG * NH], lhs, av, start=True, stop=True)
                ins.then_inc(S["c_ps"], 1)

                def before(j):
                    i = TG * g + j
                    tok = slice(j * P, (j + 1) * P)
                    if j == 0:
                        pe.wait_ge(S["x_act"], XB * g + XB + 1)
                    pe.wait_ge(S["xs_ready"], i + 1)
                    for k in range(IB):
                        ins = pe.transpose(ps[:, 4, k * P:(k + 1) * P], xbc[:, k, tok], ident)
                    ins.then_inc(S["xT_ps"], 1)
                    pe.wait_ge(S["gm_ready"], i + 1)
                    mm(ps[:, 5, P:2 * P], xbc[0:NS, IB, tok], xbc[0:NS, IB + 1, tok], start=True, stop=True)
                    pe.transpose(ps[:, 5, 0:NS], xbc[0:NS, IB, tok], ident[0:NS, 0:NS]).then_inc(S["bg_ps"], 1)
                    pe.wait_ge(S["aU_ready"], i + 1 + 1)
                    pe.wait_ge(S["e_ready"], i + 1)
                    for r in range(2):
                        ins = mm(bank(2 + r), after, aU[j % 2][:, r * 4:(r + 1) * 4, :].rearrange("p h n -> p (h n)"), start=True, stop=True)
                    ins.then_inc(S["seg_ps"], 1)

                def main(j):
                    s = j % 2
                    i = TG * g + j
                    tok = slice(j * P, (j + 1) * P)
                    if j == 0:
                        pe.wait_ge(S["c_exp"], g + 1 + 1)
                        pe.wait_ge(S["z_act"], TG * g + TG + 1)
                    pe.wait_ge(S["y1_ready"], i + 1)
                    pe.wait_ge(S["state_ready"], i + b + 1 + 1)
                    mm(bank(7), xbc[0:NS, IB + 1, tok], state[0:NS, :], start=True, stop=True).then_inc(S["off_ps"], 1)
                    pe.wait_ge(S["xw_ready"], i + 1 + 1)
                    pe.wait_ge(S["gm_ready"], i + 1 + 1)
                    mm(ps[0:NS, 0, :], bst[s], xw[s], start=True, stop=True).then_inc(S["st_ps"], 1)
                    pe.wait_ge(S["yg_ready"], i + 1)
                    pe.wait_ge(S["w_ready"], i + 1 + 1)
                    for h in range(NH):
                        ins = mm(ps[:, 6, h * HD:(h + 1) * HD], wgt[s][:, h, :], xdt[s][:, h * HD:(h + 1) * HD], start=True, stop=True)
                    ins.then_inc(S["y_ps"], 1)

                def out_turn(j):
                    i = TG * g + j
                    pe.wait_ge(S["yg_ready"], i + 1 + 1)
                    pe.wait_ge(S["op_ready"], i + 1)
                    for k in range(IB):
                        ins = pe.transpose(ps[:, 1, k * P:(k + 1) * P], ygat[j % 2][:, k * P:(k + 1) * P], ident)
                    ins.then_inc(S["yT_ps"], 1)

                def out_project(j):
                    pe.wait_ge(S["yT_ready"], TG * g + j + 1 + 1)
                    for k in range(IB):
                        ins = mm(ps[:, 1, 0:D], yT[:, k, :], wout[:, k, :], start=(k == 0), stop=(k == IB - 1))
                    ins.then_inc(S["op_ps"], 1)

                before(0)
                for j in range(TG):
                    if j + 1 < TG:
                        before(j + 1)
                    if j > 0:
                        out_turn(j - 1)
                    main(j)
                    if j > 0:
                        out_project(j - 1)
                out_turn(TG - 1)
                out_project(TG - 1)
                pe.wait_ge(S["state_ready"], TG * g + TG + b + 1 + 1)

            pe.wait_ge(att_in, 8 * 16)
            pe.wait_ge(S["h_done"], NT + 1)
            for m in range(KB):
                for k in range(KB):
                    ins = mm(ps[:, m, 0:B * S2], wk[:, k, m * P:(m + 1) * P], ctxT[:, k, :], start=(k == 0), stop=(k == KB - 1))
                ins.then_inc(S["k_ps"], 1)
            for kt in range(2):
                for b in range(B):
                    for k in range(KB):
                        c0 = b * S2 + kt * KT
                        ins = mm(ps[0:KT, 2 + kt * B + b, 0:D], ctxT[:, k, c0:c0 + KT], wv[:, k, :], start=(k == 0), stop=(k == KB - 1))
                    ins.then_inc(S["v_ps"], 1)

            pe.wait_ge(mlp_in, 2 * 16)

            def mlp_up(g):
                pe.wait_ge(S["b_nT"], KB * g + KB + 1)
                for m in range(FB):
                    pe.wait_ge(S["b_gel"], FB * g + max(m - 3, 0) + 1)
                    for k in range(KB):
                        ins = mm(bank(2 + m % 4), wfc[:, k, m * P:(m + 1) * P], nT[:, k, :], start=(k == 0), stop=(k == KB - 1))
                    ins.then_inc(S["b_up_ps"], 1)

            def mlp_down(g, j):
                pe.wait_ge(S["b_res"], TG * g + max(j - 1, 0) + 1)
                for m in range(FB):
                    if j == 0:
                        pe.wait_ge(S["b_gel"], FB * g + m + 1 + 1)
                    ins = mm(ps[:, 6 + j % 2, 0:D], gT[:, m, j * P:(j + 1) * P], wproj[:, m, :], start=(m == 0), stop=(m == FB - 1))
                ins.then_inc(S["b_dn_ps"], 1)

            pe.wait_ge(S["k_flat"], KB + 1)
            turn_group("b_n", "b_nT_ps", 0)
            pe.wait_ge(S["v_flat"], 2 * B + 1)
            with pe.Fori(0, NG - 1) as g:
                mlp_up(g)
                for j in range(TG):
                    mlp_down(g, j)
                    if j == 1:
                        turn_group("b_n", "b_nT_ps", pe.snap(g + 1))
            mlp_up(NG - 1)

            def gate_turn(gg, k):
                pe.wait_ge(S["d_n"], gg + 1 + 1)
                if k == 0:
                    pe.wait_ge(S["c_out"], TG * gg + TG + 1)
                else:
                    pe.wait_ge(S["d_nT"], KB * gg + k + 1)
                for j in range(TG):
                    ins = pe.transpose(ps[:, 0, j * P:(j + 1) * P], rowx[:, j, k * P:(k + 1) * P], ident)
                ins.then_inc(S["d_nT_ps"], 1)

            def gate_logits(gg):
                pe.wait_ge(S["d_nT"], KB * gg + KB + 1)
                for j in range(TG):
                    for k in range(KB):
                        ins = mm(ps[:, 0, j * E:(j + 1) * E], nT[:, k, j * P:(j + 1) * P], wg[:, k, :], start=(k == 0), stop=(k == KB - 1))
                ins.then_inc(S["lg_ps"], 1)

            def gate_slots(gg):
                pe.wait_ge(S["sel_ready"], gg + 1 + 1)
                own = sel.rearrange("p j n -> p (j n)")
                prior = csel.rearrange("p j n -> p (j n)")
                mm(ps[:, 0, 0:E], upto, own[:, 0:E], start=True, stop=True)
                mm(ps[:, 0, E:TG * E], upto, own[:, E:], start=True, stop=False)
                mm(ps[:, 0, E:TG * E], ones, prior[:, 0:(TG - 1) * E], start=False, stop=True)
                ins = mm(ps[:, 0, TG * E:(TG + 1) * E], ones, prior[:, (TG - 1) * E:], start=True, stop=True)
                ins.then_inc(S["pos_ps"], 1)

            def att_turn(g, k, gated=None):
                pe.wait_ge(S["c_n"], g + 1 + 1)
                if gated is not None:
                    pe.wait_ge(S["d_lg" if k == 0 else "pos_taken"], gated + 1 + 1)
                elif k == 1:
                    pe.wait_ge(S["c_nT" if g == 0 else "c_out"], 1 + 1)
                for j in range(TG):
                    ins = pe.transpose(ps[:, 0, j * P:(j + 1) * P], nrm[:, j, k * P:(k + 1) * P], ident)
                ins.then_inc(S["c_nT_ps"], 1)

            def att_query(g):
                pe.wait_ge(S["c_nT"], KB * g + KB + 1)
                for m in range(KB):
                    for k in range(KB):
                        ins = mm(bank(2 + m), wq[:, k, m * P:(m + 1) * P], nT[:, k, :], start=(k == 0), stop=(k == KB - 1))
                    ins.then_inc(S["q_ps"], 1)

            def att_scores(g, u):
                s, j, k, q = u % 2, u // 4, u % 4 // 2, u % 2
                if u < 2:
                    pe.wait_ge(S["c_q"], KB * g + KB + 1)
                if not (isinstance(g, int) and u < 2):
                    pe.wait_ge(S["c_sc"], 16 * g + u - 1 + 1)
                for r in range(2):
                    c0 = (4 * q + 2 * r) * S2
                    ins = mm(ps[:, 2 + 2 * s + r, 0:2 * S2], qT[:, k, j * P:(j + 1) * P],
                             kbd[:, k, ds(g // GPB, 1), c0:c0 + 2 * S2].squeeze(1), start=True, stop=True)
                ins.then_inc(S["sc_ps"], 1)

            def att_weights(g, u):
                s = u % 2
                pe.wait_ge(S["p_ready"], 16 * g + u + 1 + 1)
                pe.wait_ge(S["pT_ready"], 16 * g + u + 1)
                for h in range(4):
                    for kt in range(2):
                        w = 2 * h + kt
                        ins = pe.transpose(ps[0:KT, 6 + w // 4, (w % 4) * P:(w % 4 + 1) * P],
                                           pr[s][:, h, kt * KT:(kt + 1) * KT], ident)
                ins.then_inc(S["pT_ps"], 1)

            def att_values(g, u):
                s, j, q = u % 2, u // 4, u % 4
                pe.wait_ge(S["pT_ready"], 16 * g + u + 1 + 1)
                if q == 0:
                    pe.wait_ge(S["cx_ready"], TG * g + j + 1)
                for h in range(4):
                    hh = 4 * q + h
                    for kt in range(2):
                        ins = mm(ps[:, 1, hh * (DK + 1):(hh + 1) * (DK + 1)], pT[s][0:KT, 2 * h + kt, :],
                                 vone[0:KT, kt, ds(g // GPB, 1), hh, :].squeeze(1), start=(kt == 0), stop=(kt == 1))
                ins.then_inc(S["val_ps"], 1) if q < 3 else ins.then_inc(S["ctx_ps"], 1)

            def att_context(g, j, following, gated):
                i = TG * g + j
                if gated is not None and j == 1:
                    pe.wait_ge(S["pos_taken"], gated + 1 + 1)
                if following is not None and j < KB:
                    pe.wait_ge(S["c_nT"], KB * following + j + 1 + 1)
                pe.wait_ge(S["cx_ready"], i + 1 + 1)
                pe.wait_ge(S["c_out"], i + 1)
                for k in range(KB):
                    ins = pe.transpose(ps[:, 0, k * P:(k + 1) * P], cx[:, k * P:(k + 1) * P], ident)
                ins.then_inc(S["cxT_ps"], 1)

            def att_output(g, j):
                i = TG * g + j
                pe.wait_ge(S["cxT_ready"], i + 1 + 1)
                for k in range(KB):
                    ins = mm(ps[:, 0, D:2 * D], cxT[:, k, :], wo[:, k, :], start=(k == 0), stop=(k == KB - 1))
                ins.then_inc(S["co_ps"], 1)

            def att_group(g, following, gated):
                for u in range(16):
                    if u < 14:
                        att_scores(g, u + 2)
                    elif u == 14 and following is not None:
                        pe.wait_ge(S["c_sc"], 16 * g + 14 + 1 + 1)
                        att_query(following)
                    if gated is not None and u == 3:
                        gate_turn(gated, 1)
                    att_weights(g, u)
                    if u > 0:
                        att_values(g, u - 1)
                    if gated is not None:
                        if u == 2:
                            gate_turn(gated, 0)
                        if u == 3:
                            gate_logits(gated)
                        if u == 7:
                            pe.wait_ge(S["c_out"], TG * g + 1 + 1)
                            gate_slots(gated)
                    if following is not None and u == 4:
                        att_turn(following, 0, gated)
                    if following is not None and u == 8:
                        att_turn(following, 1, gated)
                    if u % 4 == 1 and u > 4:
                        att_context(g, u // 4 - 1, following, gated)
                    if u % 4 == 2 and u > 4:
                        att_output(g, u // 4 - 1)
                if following is not None:
                    att_scores(following, 0)
                att_values(g, 15)
                if following is not None:
                    att_scores(following, 1)
                att_context(g, TG - 1, following, gated)
                att_output(g, TG - 1)

            for j in range(TG):
                mlp_down(NG - 1, j)
                if 1 <= j < 1 + KB:
                    att_turn(0, j - 1)
            att_query(0)
            pe.wait_ge(S["kv_ready"], 1 + 1)
            for u in range(2):
                att_scores(0, u)
            att_group(0, 1, None)
            with pe.Fori(1, NG - 1) as g:
                att_group(g, pe.snap(g + 1), pe.snap(g - 1))
            att_group(NG - 1, None, NG - 2)
            for k in range(KB):
                gate_turn(NG - 1, k)
            gate_logits(NG - 1)
            pe.wait_ge(S["d_lg"], NG + 1)
            gate_slots(NG - 1)

            def turn_tile(k):
                pe.wait_ge(xt_in, 16 * (k + 1))
                pe.wait_ge(S["xT_ready"], k + 1)
                for m in range(KB):
                    for r in range(SUB):
                        ins = pe.transpose(ps[:, 0, m * TW + r * P:m * TW + (r + 1) * P], xt[:, r, m * P:(m + 1) * P], ident)
                ins.then_inc(S["t_ps"], 1)

            pe.wait_ge(S["tab_ready"], 1 + 1)
            turn_tile(0)
            with pe.Fori(0, E // 2) as ep:
                for s in range(2):
                    e = pe.snap(2 * ep + s)
                    pe.wait_ge(exp_in[s], 4 * 16 * ep + 4 * 16)
                    pe.sem_inc(pe_pad, 1)
                    tiles = pe.value_load(tab[0:1, ds(e, 1)], min_val=2, max_val=NTOK // TW)
                    first = pe.value_load(tab[0:1, ds(E + e, 1)], min_val=0, max_val=MAXT)
                    with pe.Fori(0, tiles) as j:
                        k = pe.snap(first + j)
                        pe.wait_ge(S["xT_ready"], k + 1 + 1)
                        for m in range(HB):
                            pe.wait_ge(S["d_gel"], HB * k + max(m - 3, 0) + 1)
                            for c in range(KB):
                                ins = mm(bank(2 + m % 4, TW), wup[s][:, c, m * P:(m + 1) * P], xT[:, c, :], start=(c == 0), stop=(c == KB - 1))
                            ins.then_inc(S["u_ps"], 1)
                        pe.wait_ge(S["y_ready"], 2 * SUB * k + 1)
                        for r in range(SUB):
                            for m in range(HB):
                                if r == 0:
                                    pe.wait_ge(S["d_gel"], HB * k + m + 1 + 1)
                                if r == 0 and m == HB // 2:
                                    turn_tile(k + 1)
                                ins = mm(ps[:, 6 + r, 0:D], eT[:, m, r * P:(r + 1) * P], wdn[s][:, m, :], start=(m == 0), stop=(m == HB - 1))
                            ins.then_inc(S["dn_ps"], 1)



def kernel(**inputs):
    import numpy as np
    import concourse.bacc as bacc
    from concourse import mybir
    from concourse.bass_utils import run_bass_kernel_spmd as run

    g = {k: np.asarray(v) for k, v in inputs.items()}
    a = {k[len("L0_attn_"):]: v for k, v in g.items() if k.startswith("L0_attn_")}
    xa = {k[len("L0_xattn_"):]: v for k, v in g.items() if k.startswith("L0_xattn_")}
    ff = {k[len("L0_ffn_"):]: v for k, v in g.items() if k.startswith("L0_ffn_")}
    P = 128
    idx = np.arange(P)

    def cols(v):
        return v.reshape(-1, P).T

    def halves(v):
        out = np.zeros((P, v.shape[1]), v.dtype)
        out[:v.shape[0]] = v
        return out

    cw, cb = a["conv_w"], a["conv_b"][:, None]
    blocks_w = [cw[k * P:(k + 1) * P] for k in range(4)] + [halves(cw[512:576]), halves(cw[576:640])]
    blocks_b = [cb[k * P:(k + 1) * P] for k in range(4)] + [halves(cb[512:576]), halves(cb[576:640])]
    arrays = {
        "x": g["x"],
        "consts": np.stack([np.eye(P), idx[:, None] <= idx[None, :], idx[:, None] > idx[None, :],
                            np.ones((P, P))]).astype(np.float32),
        "headmask": (idx[:, None] // 16 == np.arange(8)[None, :]).astype(np.float32),
        "iota12": np.broadcast_to(np.arange(12, dtype=np.float32), (P, 12)),
        "cols": np.concatenate([cols(a["ln1_w"]), cols(a["ln1_b"]), cols(a["ln2_w"]), cols(a["ln2_b"]),
                                cols(a["fc_b"]), cols(xa["bq"]), cols(xa["bk"]), cols(a["norm_w"])]
                               + blocks_w + blocks_b, axis=1),
        "rows": np.concatenate([a["dt_bias"], a["A_log"], np.repeat(a["D_param"], 64), a["proj_b"],
                                xa["bo"], xa["bv"],
                                (np.arange(12)[:, None] > np.arange(12)[None, :]).astype(np.float32).ravel(),
                                (np.arange(12) * (2048 + 2 * TW) - 1).astype(np.float32),
                                (np.arange(2048 // TW) * TW).astype(np.float32),
                                np.arange((3 * 2048 + 2048) // TW + 2 * 12 + 1, dtype=np.float32)]),
        "tokid": np.arange(17)[None, :].astype(np.float32) * P + idx[:, None].astype(np.float32),
        "in_proj": a["in_proj_w"].T, "out_proj": a["out_proj_w"].T,
        "fc": a["fc_w"].T, "proj": a["proj_w"].T,
        "Wq": xa["Wq"].T, "Wk": xa["Wk"].T, "Wv": xa["Wv"].T, "Wo": xa["Wo"].T,
        "ctxT": g["ctx_1024"].transpose(2, 0, 1),
        "qmask": g["mask_1xSxS2_ik1"], "kmask": g["mask_BxS2_ik1"],
        "Wg": ff["Wg"], "Wup": ff["Wup"], "Wdown": ff["Wdown"], "bdown": ff["bdown"],
        "bup": ff["bup"].reshape(12, 8, P).transpose(0, 2, 1),
    }
    arrays = {k: np.ascontiguousarray(v) for k, v in arrays.items()}
    nc = bacc.Bacc("TRN2", target_bir_lowering=False, num_devices=1)
    t = {k: nc.dram_tensor("in_" + k, v.shape, mybir.dt.from_np(v.dtype), kind="ExternalInput").ap()
         for k, v in arrays.items()}
    t["out"] = nc.dram_tensor("out_x", (2048 + P, 256), mybir.dt.float32, kind="ExternalOutput").ap()
    build(nc, t)
    r = run(nc, [{"in_" + k: v for k, v in arrays.items()}], core_ids=[0])
    return r.results[0]["out_x"][:2048].reshape(2, 1024, 256)
```
